# Optimizing a Trainium2 kernel written in Bass

```python
import numpy as np
import jax
import jax.numpy as jnp

def _softmax(x, axis=-1):
    return jax.nn.softmax(x, axis=axis)

def _gelu(x):
    return jax.nn.gelu(x, approximate=True)

def _silu(x):
    return jax.nn.silu(x)

def _sigmoid(x):
    return jax.nn.sigmoid(x)

def _layernorm(x, axis=-1, eps=1e-05):
    m = jnp.mean(x, axis=axis, keepdims=True)
    v = jnp.var(x, axis=axis, keepdims=True)
    return (x - m) / jnp.sqrt(v + eps)

def _scatter_add(tgt, idx, src, axis=0):
    return tgt.at[idx].add(src)

def _segment_sum(src, seg, n):
    return jax.ops.segment_sum(src, seg, n)
kernel_name = 'mk_gps_d1_gnn_r8_09d5c0'

def setup_inputs(seed: int=0):
    np.random.seed(seed)
    _w = jnp.asarray

    def _rec_inputs():
        import jax
        import jax.numpy as jnp
        _gk = jax.random.key(seed)
        x = -0.0003713 + 1 * jax.random.normal(jax.random.fold_in(_gk, 1), (12500, 256), jnp.float32)
        src = jax.random.randint(jax.random.fold_in(_gk, 2), (200000,), 0, 12500, jnp.int32)
        dst = jnp.minimum((12500 * jax.random.uniform(jax.random.fold_in(_gk, 3), (200000,)) ** 2.0).astype(jnp.int32), 99999)
        _o = jnp.argsort(dst, stable=True)
        src = src[_o]
        dst = dst[_o]
        return (x, src, dst)
    x, src, dst = _rec_inputs()

    def _L0_gnn_setup():
        import jax, jax.numpy as jnp
        import numpy as np
        N, IN_CH, HEADS, OUT_CH, E = (6250, 256, 4, 64, 100000)
        key = jax.random.key(seed)
        k1, k2, k3, k4, k5 = jax.random.split(key, 5)
        x = jax.random.normal(k1, (N, IN_CH), dtype=jnp.float32)
        edge_index = jax.random.randint(k2, (2, E), 0, N, dtype=jnp.int64)
        bw = float(np.sqrt(6.0 / (IN_CH + HEADS * OUT_CH)))
        ba = float(np.sqrt(6.0 / (HEADS + OUT_CH)))
        weight = jax.random.uniform(k3, (IN_CH, HEADS * OUT_CH), jnp.float32, -bw, bw)
        attn_l = jax.random.uniform(k4, (HEADS, OUT_CH), jnp.float32, -ba, ba)
        attn_r = jax.random.uniform(k5, (HEADS, OUT_CH), jnp.float32, -ba, ba)
        return {'x': x, 'edge_index': edge_index, 'weight': weight, 'attn_l': attn_l, 'attn_r': attn_r}
    _L0_gnn_all = _L0_gnn_setup()
    _L0_gnn_in = {k: v for k, v in _L0_gnn_all.items() if k in ('weight', 'attn_l', 'attn_r')}
    del _L0_gnn_all

    def _L0_mix_setup():
        import jax, jax.numpy as jnp
        import numpy as np
        NUM_HEADS = 8
        key = jax.random.key(seed)
        ks = jax.random.split(key, 5)
        B, N, C = (8, 2048, 256)
        x = jax.random.normal(ks[0], (B, N, C), dtype=jnp.float32)
        Wq = jax.random.normal(ks[1], (C, C), dtype=jnp.float32) * 0.02
        Wkv = jax.random.normal(ks[2], (2 * C, C), dtype=jnp.float32) * 0.02
        Wproj = jax.random.normal(ks[3], (C, C), dtype=jnp.float32) * 0.02
        bproj = jnp.zeros((C,), dtype=jnp.float32)
        return {'x': x, 'Wq': Wq, 'Wkv': Wkv, 'Wproj': Wproj, 'bproj': bproj}
    _L0_mix_all = _L0_mix_setup()
    _L0_mix_in = {k: v for k, v in _L0_mix_all.items() if k in ('Wq', 'Wkv', 'Wproj', 'bproj')}
    del _L0_mix_all

    def _L0_ffn_setup():
        import math
        import jax, jax.numpy as jnp
        import numpy as np
        CAPACITY_FACTOR = 1.25
        key = jax.random.key(seed)
        ks = jax.random.split(key, 5)
        B, L, D, F, E = (8, 1024, 256, 1024, 8)
        h = jax.random.normal(ks[0], (B, L, D), dtype=jnp.float32)
        gate_w = jax.random.normal(ks[1], (D, E), dtype=jnp.float32) * 0.02
        gate_b = jnp.zeros((E,), dtype=jnp.float32)
        w1 = jax.random.normal(ks[2], (E, D, F), dtype=jnp.float32) * (1.0 / math.sqrt(D))
        b1 = jnp.zeros((E, F), dtype=jnp.float32)
        w2 = jax.random.normal(ks[3], (E, F, D), dtype=jnp.float32) * (1.0 / math.sqrt(F))
        b2 = jnp.zeros((E, D), dtype=jnp.float32)
        return {'h': h, 'gate_w': gate_w, 'gate_b': gate_b, 'w1': w1, 'b1': b1, 'w2': w2, 'b2': b2}
    _L0_ffn_all = _L0_ffn_setup()
    _L0_ffn_in = {k: v for k, v in _L0_ffn_all.items() if k in ('gate_w', 'gate_b', 'w1', 'b1', 'w2', 'b2')}
    del _L0_ffn_all
    return {'x': x, 'src': src, 'dst': dst, 'L0_gnn_weight': _L0_gnn_in['weight'], 'L0_gnn_attn_l': _L0_gnn_in['attn_l'], 'L0_gnn_attn_r': _L0_gnn_in['attn_r'], 'L0_mix_Wq': _L0_mix_in['Wq'], 'L0_mix_Wkv': _L0_mix_in['Wkv'], 'L0_mix_Wproj': _L0_mix_in['Wproj'], 'L0_mix_bproj': _L0_mix_in['bproj'], 'L0_ffn_gate_w': _L0_ffn_in['gate_w'], 'L0_ffn_gate_b': _L0_ffn_in['gate_b'], 'L0_ffn_w1': _L0_ffn_in['w1'], 'L0_ffn_b1': _L0_ffn_in['b1'], 'L0_ffn_w2': _L0_ffn_in['w2'], 'L0_ffn_b2': _L0_ffn_in['b2']}

def reference(x, src, dst, L0_gnn_weight, L0_gnn_attn_l, L0_gnn_attn_r, L0_mix_Wq, L0_mix_Wkv, L0_mix_Wproj, L0_mix_bproj, L0_ffn_gate_w, L0_ffn_gate_b, L0_ffn_w1, L0_ffn_b1, L0_ffn_w2, L0_ffn_b2):
    import jax
    import jax.numpy as jnp

    def _L0_gnn_ref(x, edge_index, weight, attn_l, attn_r):
        import jax, jax.numpy as jnp
        import numpy as np
        N, IN_CH, HEADS, OUT_CH, E = (6250, 256, 4, 64, 100000)
        heads, out_ch = attn_l.shape
        n = x.shape[0]
        xt = jnp.matmul(x, weight).reshape(-1, heads, out_ch)
        row, col = (edge_index[0], edge_index[1])
        alpha_l = jnp.einsum('ehd,hd->eh', xt[row], attn_l)
        alpha_r = jnp.einsum('ehd,hd->eh', xt[col], attn_r)
        alpha = jax.nn.softmax(jax.nn.leaky_relu(alpha_l + alpha_r, 0.01), axis=1)
        tmp = jnp.einsum('nh,nhd->nd', alpha[:n], xt[col[:n]])
        out = jnp.broadcast_to(tmp[:, None, :], (n, heads, out_ch))
        return out.reshape(n, heads * out_ch)

    def _L0_mix_ref(x, Wq, Wkv, Wproj, bproj):
        import jax, jax.numpy as jnp
        import numpy as np
        NUM_HEADS = 8
        B, N, C = x.shape
        h = NUM_HEADS
        d = C // h
        q = jnp.einsum('bnc,oc->bno', x, Wq).reshape(B, N, h, d).transpose(0, 2, 1, 3)
        kv = jnp.einsum('bnc,oc->bno', x, Wkv).reshape(B, N, 2, h, d)
        k = kv[:, :, 0].transpose(0, 2, 1, 3)
        v = kv[:, :, 1].transpose(0, 2, 1, 3)
        q = jax.nn.elu(q) + 1.0
        k = jax.nn.elu(k) + 1.0
        k_sum = k.sum(axis=2)
        D_inv = 1.0 / jnp.maximum(jnp.einsum('bhnd,bhd->bhn', q, k_sum), 1e-06)
        context = jnp.einsum('bhnd,bhne->bhde', k, v)
        attn = jnp.einsum('bhnd,bhde->bhne', q, context) * D_inv[..., None]
        out = attn.transpose(0, 2, 1, 3).reshape(B, N, C)
        out = jnp.einsum('bnc,oc->bno', out, Wproj) + bproj
        return out

    def _L0_ffn_ref(h, gate_w, gate_b, w1, b1, w2, b2):
        import math
        import jax, jax.numpy as jnp
        import numpy as np
        CAPACITY_FACTOR = 1.25
        B, L, D = h.shape
        E = gate_w.shape[1]
        T = B * L
        C = max(1, math.ceil(CAPACITY_FACTOR * T / E))
        x = h.reshape(T, D)
        logits = x @ gate_w + gate_b
        probs = jax.nn.softmax(logits, axis=-1)
        idx = jnp.argmax(probs, axis=-1)
        prb = jnp.take_along_axis(probs, idx[:, None], axis=1)[:, 0]
        one_hot = jax.nn.one_hot(idx, E, dtype=jnp.float32)
        pos = (jnp.cumsum(one_hot, axis=0) * one_hot).sum(-1).astype(jnp.int32) - 1
        kept = pos < C
        pos_safe = jnp.where(kept, pos, C)
        buf = jnp.zeros((E, C, D), dtype=h.dtype).at[idx, pos_safe].set(x, mode='drop')
        hmid = jax.nn.relu(jnp.einsum('ecd,edf->ecf', buf, w1) + b1[:, None, :])
        ybuf = jnp.einsum('ecf,efd->ecd', hmid, w2) + b2[:, None, :]
        pos_g = jnp.minimum(pos, C - 1)
        y_tok = ybuf[idx, pos_g] * (prb * kept)[:, None]
        y = y_tok.reshape(B, L, D)
        y = jnp.nan_to_num(y, nan=0.0, posinf=10000.0, neginf=-10000.0)
        return y
    edge_index = jnp.stack([src, dst])
    xn = _layernorm(x, axis=-1)
    x = x + _L0_gnn_ref(xn, edge_index, L0_gnn_weight, L0_gnn_attn_l, L0_gnn_attn_r) + _L0_mix_ref(xn[None], L0_mix_Wq, L0_mix_Wkv, L0_mix_Wproj, L0_mix_bproj)[0]
    x = x + _L0_ffn_ref(_layernorm(x, axis=-1)[None], L0_ffn_gate_w, L0_ffn_gate_b, L0_ffn_w1, L0_ffn_b1, L0_ffn_w2, L0_ffn_b2)[0]
    return x

_drawn_inputs = setup_inputs


def setup_inputs(seed=0):
    import zlib

    import numpy as np

    out = dict(_drawn_inputs(seed))
    spreads = {'L0_mix_bproj': (0.0, 0.1),
     'L0_ffn_gate_b': (0.0, 0.1),
     'L0_ffn_b1': (0.0, 0.734),
     'L0_ffn_b2': (0.0, 0.52)}
    factors = {'L0_mix_Wq': 8.0, 'L0_mix_Wkv': 8.0, 'L0_mix_Wproj': 8.0}
    for name, (base, spread) in spreads.items():
        noise = np.random.default_rng([zlib.crc32(name.encode()), seed]).standard_normal(out[name].shape)
        drawn = base * np.exp(spread * noise) if base else spread * noise
        out[name] = jnp.asarray(drawn.astype(out[name].dtype))
    for name, factor in factors.items():
        out[name] = (out[name] * factor).astype(out[name].dtype)
    return out
```

```python
from contextlib import ExitStack

import concourse.bass as bass
from concourse import mybir

ALU = mybir.AluOpType
ACT = mybir.ActivationFunctionType
F32 = mybir.dt.float32
F32R = mybir.dt.float32r
I32 = mybir.dt.int32
AX = mybir.AxisListType

P = 128
EPS = 1e-5
FAR = 60000.0
BIG = 1000000.0


def passed(eng, sem):
    eng.sem_inc(sem)


def over_tiles(eng, step, n):
    step(0, 0, 0, False)
    step(1, 1, 0, False)
    with eng.Fori(1, n // 2) as i:
        step(2 * i, 0, i, False)
        step(2 * i + 1, 1, i, False)
    step(n - 1, 0, n // 2, True)


def gps_layer(nc, x, src, dst, gnn_w, attn_l, attn_r, wq, wkv, wproj, bproj,
              gate_w, gate_b, w1, b1, w2, b2, out):
    N, D = x.shape
    H, DH = attn_l.shape
    E, _, F = w1.shape
    QH = 8
    QD = D // QH
    KC = D // P
    T, J = 125, 4
    TS = T * J
    NS = N // TS
    assert NS * TS == N and NS % 2 == 1
    CAP = -(-5 * N // (4 * E))
    T3 = 124
    TS3 = T3 * J
    ST = -(-CAP // TS3)
    ROWS = ST * TS3
    NF = F // P
    XW = D + 2 * H
    TW = D + H
    RW = D + 4
    GW = D + 2

    table = nc.dram_tensor("graph_table", [N, TW], F32, kind="Internal").ap()
    table_l = nc.dram_tensor("alpha_l_table", [N, H], F32, kind="Internal").ap()
    rows = nc.dram_tensor("expert_rows", [E * ROWS, RW], F32, kind="Internal").ap()

    base = ExitStack()

    def sb_in(stack, name, shape, dt=F32):
        return stack.enter_context(nc.sbuf_tensor(name, shape, dt))

    def ps_in(stack, name, shape):
        return stack.enter_context(nc.psum_tensor(name, shape, F32))

    def sem_in(stack, name):
        return stack.enter_context(nc.semaphore(name))

    def tok(t, s, w):
        return t[bass.ds(s * TS, TS), :].rearrange("(p j) w -> p j w", j=J)

    def wide(a, n):
        dims = list(a.shape)
        names = "pjh"[:len(dims)]
        spread = a.rearrange(f"{' '.join(names[:-1])} ({names[-1]} z) -> {' '.join(names)} z", z=1)
        return spread.broadcast_to(dims + [n])

    def halves(eng, first_half, second_half):
        def pair(i):
            second_half(2 * i, 0, i)
            first_half(2 * i + 1, 1, i)
            second_half(2 * i + 1, 1, i)
            first_half(2 * i + 2, 0, i + 1)

        first_half(0, 0, 0)
        pair(0)
        with eng.Fori(1, NS // 2) as i:
            pair(i)
        second_half(NS - 1, 0, NS // 2)

    with base:
        def sb(name, shape, dt=F32):
            return sb_in(base, name, shape, dt)

        ident = sb("ident", [P, P])
        mhalf = sb("mhalf", [P, J])
        x_sb = sb("x_sb", [T, 2, J, D])
        wv_t = sb("wv_t", [P, KC, D])
        wp_t = sb("wp_t", [P, KC, D])
        g_sb = sb("g_sb", [P, KC, GW])

        late = ExitStack()
        q_all = sb_in(late, "q_all", [P, KC, N])

        with ExitStack() as ph, nc.Block() as block:
            def sb1(name, shape, dt=F32):
                return sb_in(ph, name, shape, dt)

            wqkvp = q_all[:, 0, N - 4 * KC * D:N].rearrange("p (n c i) -> p n c i", n=4, c=KC)
            attn_bc = q_all[:, 1, N - 2 * D:N].rearrange("p (n i) -> p n i", n=2)
            wprod = q_all[:, 1, N - 4 * D:N - 2 * D].rearrange("p (c i) -> p c i", c=KC)
            wx_f = sb1("wx_f", [P, KC, XW])
            wx_hi = sb1("wx_hi", [P, KC, XW], F32R)
            wx_lo = sb1("wx_lo", [P, KC, XW], F32R)
            wq_hi = sb1("wq_hi", [P, KC, D], F32R)
            wq_lo = sb1("wq_lo", [P, KC, D], F32R)
            wk_hi = sb1("wk_hi", [P, KC, D], F32R)
            wk_lo = sb1("wk_lo", [P, KC, D], F32R)
            empty = sb1("empty", [P, J, RW])
            st6 = sb1("st6", [T, J, 6])
            mv = sb1("mv", [T, J, 2])
            rstd = sb1("rstd", [T, J])
            xn = sb1("xn", [T, J, D])
            xn_hi = sb1("xn_hi", [T, 2, J, GW], F32R)
            xn_lo = sb1("xn_lo", [T, 2, J, GW], F32R)
            xt_hi = sb1("xt_hi", [P, KC, TS], F32R)
            xt_lo = sb1("xt_lo", [P, KC, TS], F32R)
            eq = sb1("eq", [P, KC, TS])
            ek = sb1("ek", [T, 2, 2, D])
            kf = sb1("kf", [T, 2, 2, D])
            k_hi = sb1("k_hi", [T, J, D], F32R)
            k_lo = sb1("k_lo", [T, J, D], F32R)
            tab_sb = sb1("tab_sb", [T, 2, J, XW])

            psT = [ps_in(ph, f"psT{c}", [P, 512]) for c in range(KC)]
            psG = [ps_in(ph, f"psG{c}", [P, 512]) for c in range(KC)]
            psR = [ps_in(ph, f"psR{c}", [P, 512]) for c in range(4)]

            s_w_in = sem_in(ph, "s_w_in")
            s_w_t = sem_in(ph, "s_w_t")
            s_wt_out = sem_in(ph, "s_wt_out")
            s_ident0 = sem_in(ph, "s_ident0")
            s_ident1 = sem_in(ph, "s_ident1")
            s_const1 = sem_in(ph, "s_const1")
            s_wa0 = sem_in(ph, "s_wa0")
            s_wa1 = sem_in(ph, "s_wa1")
            s_wsplit = sem_in(ph, "s_wsplit")
            s_wsplit_lo = sem_in(ph, "s_wsplit_lo")
            s_empty_set = sem_in(ph, "s_empty_set")
            s_empty_out = sem_in(ph, "s_empty_out")
            s_var_ready = sem_in(ph, "s_var_ready")
            s_mhalf_set = sem_in(ph, "s_mhalf_set")
            s_pool_passed = sem_in(ph, "s_pool_passed")
            s_dve_passed = sem_in(ph, "s_dve_passed")
            s_x_in0 = sem_in(ph, "s_x_in0")
            s_x_in1 = sem_in(ph, "s_x_in1")
            s_stats = sem_in(ph, "s_stats")
            s_aggr = sem_in(ph, "s_aggr")
            s_rstd_ready = sem_in(ph, "s_rstd_ready")
            s_xn_ready = sem_in(ph, "s_xn_ready")
            s_xnhi_ready = sem_in(ph, "s_xnhi_ready")
            s_xnlo_ready = sem_in(ph, "s_xnlo_ready")
            s_t_done = sem_in(ph, "s_t_done")
            s_hit_done = sem_in(ph, "s_hit_done")
            s_lot_done = sem_in(ph, "s_lot_done")
            s_q_mm = sem_in(ph, "s_q_mm")
            s_k_mm = sem_in(ph, "s_k_mm")
            s_xt_mm = sem_in(ph, "s_xt_mm")
            s_g_done = sem_in(ph, "s_g_done")
            s_eq_exp = sem_in(ph, "s_eq_exp")
            s_ek_exp = sem_in(ph, "s_ek_exp")
            s_eq_min = sem_in(ph, "s_eq_min")
            s_ek_min = sem_in(ph, "s_ek_min")
            s_q_done = sem_in(ph, "s_q_done")
            s_k_done = sem_in(ph, "s_k_done")
            s_khi_done = sem_in(ph, "s_khi_done")
            s_klo_done = sem_in(ph, "s_klo_done")
            s_tab_ready = sem_in(ph, "s_tab_ready")
            s_tab_out0 = sem_in(ph, "s_tab_out0")
            s_tab_out1 = sem_in(ph, "s_tab_out1")
            s_g_out = sem_in(ph, "s_g_out")
            x_in = [s_x_in0, s_x_in1]
            tab_out = [s_tab_out0, s_tab_out1]

            @block.sync
            def _(sp):
                def load_x(s, par):
                    sp.dma_start(x_sb[:, par, :, :], tok(x, s, D)).then_inc(x_in[par], 16)

                load_x(0, 0)
                for n, w in enumerate((wq, wkv[0:D, :], wkv[D:2 * D, :], wproj)):
                    sp.dma_start(wqkvp[:, n, :, :], w.rearrange("(c p) i -> p c i", p=P)).then_inc(s_w_in, 16)
                sp.dma_start(wx_f[:, :, 0:D], gnn_w.rearrange("(c p) o -> p c o", p=P)).then_inc(s_w_in, 16)
                for n, a in enumerate((attn_r, attn_l)):
                    sp.dma_start(attn_bc[:, n, :], a.rearrange("(a h) d -> a (h d)", a=1).partition_broadcast(P))\
                      .then_inc(s_w_in, 16)
                load_x(1, 1)

                def step(s, par, h, last, load):
                    if load:
                        sp.wait_ge(s_xn_ready, s + 1)
                        load_x(s + 2, par)
                    sp.wait_ge(s_tab_ready, J * (s + 1))
                    sp.dma_start(tok(table, s, TW), tab_sb[:, par, :, 0:TW]).then_inc(tab_out[par], 16)
                    sp.dma_start(tok(table_l, s, H), tab_sb[:, par, :, TW:XW]).then_inc(tab_out[par], 16)

                step(0, 0, 0, False, True)
                step(1, 1, 0, False, True)
                with sp.Fori(1, (NS - 3) // 2) as i:
                    step(2 * i, 0, i, False, True)
                    step(2 * i + 1, 1, i, False, True)
                step(NS - 3, 0, (NS - 3) // 2, False, True)
                step(NS - 2, 1, 0, False, False)
                step(NS - 1, 0, 0, True, False)
                sp.wait_ge(tab_out[0], 32 * (NS // 2 + 1))
                sp.wait_ge(tab_out[1], 32 * (NS // 2))
                sp.wait_ge(s_empty_out, 16 * (E * ROWS // (P * J)))

            @block.gpsimd
            def _(pool):
                nc.gpsimd.memset(ident[:, :], 0.0).then_inc(s_ident0, 1)
                pool.wait_ge(s_ident0, 1)
                nc.gpsimd.affine_select(out=ident[:, :], in_=ident[:, :], compare_op=ALU.not_equal, fill=1.0,
                                        base=0, pattern=[[-1, P]], channel_multiplier=1).then_inc(s_ident1, 1)
                nc.gpsimd.memset(empty[:, :, :], 0.0).then_inc(s_empty_set, 1)
                pool.wait_ge(s_empty_set, 1)
                nc.gpsimd.memset(empty[:, :, D + 1:D + 2], FAR).then_inc(s_empty_set, 1)
                pool.wait_ge(s_empty_set, 2)
                groups = rows.rearrange("(g p j) w -> g p (j w)", p=P, j=J)
                with pool.Fori(0, E * ROWS // (P * J)) as g:
                    pool.dma_start(groups[bass.ds(g, 1), :, :].rearrange("a p w -> (a p) w"),
                                   empty[:, :, :].rearrange("p j w -> p (j w)")).then_inc(s_empty_out, 16)

                def rstd_of(s):
                    pool.wait_ge(s_aggr, J * (s + 1))
                    pool.wait_ge(s_xn_ready, s)
                    passed(pool, s_pool_passed)
                    nc.gpsimd.tensor_scalar(rstd[:, :], mv[:, :, 1], EPS, None, ALU.add).then_inc(s_var_ready, 1)
                    pool.wait_ge(s_var_ready, s + 1)
                    nc.gpsimd.tensor_tensor(rstd[:, :], rstd[:, :], mhalf[0:T, :], ALU.pow).then_inc(s_rstd_ready, 1)

                nc.gpsimd.memset(mhalf[:, :], -0.5).then_inc(s_mhalf_set, 1)
                pool.wait_ge(s_mhalf_set, 1)
                rstd_of(0)

                def step(s, par, h, last):
                    for c in range(KC):
                        pool.wait_ge(s_eq_exp, KC * s + c + 1)
                        passed(pool, s_pool_passed)
                        nc.gpsimd.tensor_scalar(eq[:, c, :], eq[:, c, :], 1.0, None, ALU.min).then_inc(s_eq_min, 1)
                        if c == 0 and not last:
                            rstd_of(s + 1)
                    for n in range(2):
                        pool.wait_ge(s_ek_exp, 2 * s + n + 1)
                        passed(pool, s_pool_passed)
                        nc.gpsimd.tensor_scalar(ek[:, n, :, :], ek[:, n, :, :], 1.0, None, ALU.min).then_inc(s_ek_min, 1)

                over_tiles(pool, step, NS)

            @block.scalar
            def _(act):
                for n, o in enumerate((wq_hi, wk_hi, wv_t, wp_t)):
                    act.wait_ge(s_w_t, n + 1)
                    act.activation(o[:, :, :], psR[n][:, :].rearrange("p (c o) -> p c o", c=KC), ACT.Copy)\
                       .then_inc(s_wsplit, 1)
                act.wait_ge(s_wa1, 2)
                act.activation(wx_hi[:, :, :], wx_f[:, :, :], ACT.Copy).then_inc(s_wsplit, 1)

                def xn_high(s, par):
                    act.wait_ge(s_xn_ready, s + 1)
                    act.activation(xn_hi[:, par, :, 0:D], xn[:, :, :], ACT.Copy).then_inc(s_xnhi_ready, 1)

                act.wait_ge(s_const1, 1)
                xn_high(0, 0)

                def step(s, par, h, last):
                    act.wait_ge(s_t_done, s + 1)
                    for c in range(KC):
                        act.activation(xt_hi[:, c, :], psT[c][:, 0:TS], ACT.Copy).then_inc(s_hit_done, 1)
                    for c in range(KC):
                        act.wait_ge(s_q_mm, KC * s + c + 1)
                        act.wait_ge(s_q_done, KC * s)
                        act.activation(eq[:, c, :], psR[c][:, 0:TS], ACT.Exp).then_inc(s_eq_exp, 1)
                    for n in range(2):
                        act.wait_ge(s_k_mm, 2 * s + n + 1)
                        act.wait_ge(s_k_done, 2 * s)
                        act.activation(ek[:, n, :, :], psR[2 + n][0:T, :].rearrange("p (j o) -> p j o", j=2),
                                       ACT.Exp).then_inc(s_ek_exp, 1)
                    if not last:
                        act.wait_ge(s_g_done, s)
                        xn_high(s + 1, 1 - par)
                    for n in range(2):
                        act.wait_ge(s_k_done, 2 * s + n + 1)
                        act.wait_ge(s_g_done, s)
                        act.activation(k_hi[:, 2 * n:2 * n + 2, :], kf[:, n, :, :], ACT.Copy).then_inc(s_khi_done, 1)
                    for j in range(J):
                        act.wait_ge(s_xt_mm, J * s + j + 1)
                        if j == 0:
                            act.wait_ge(tab_out[par], 32 * h)
                        act.activation(tab_sb[:, par, j, :], psR[j][0:T, 0:XW], ACT.Copy).then_inc(s_tab_ready, 1)

                over_tiles(act, step, NS)

            @block.vector
            def _(dve):
                for par in range(2):
                    nc.vector.memset(xn_lo[:, par, :, D:GW].bitcast(F32), 0.0)
                    nc.vector.memset(xn_hi[:, par, :, D + 1:GW].bitcast(F32), 0.0)
                    ins = nc.vector.memset(xn_hi[:, par, :, D:D + 1].bitcast(F32), 1.0)
                ins.then_inc(s_const1, 1)

                def stats(s, par, h):
                    dve.wait_ge(x_in[par], 16 * (h + 1))
                    for j in range(J):
                        nc.vector.bn_stats(st6[:, j, :], x_sb[:, par, j, :]).then_inc(s_stats, 1)
                    dve.wait_ge(s_rstd_ready, s)
                    dve.wait_ge(s_stats, J * (s + 1))
                    passed(dve, s_dve_passed)
                    for j in range(J):
                        nc.vector.bn_aggr(mv[:, j, :], st6[:, j, :]).then_inc(s_aggr, 1)

                def norm(s, par):
                    dve.wait_ge(s_rstd_ready, s + 1)
                    dve.wait_ge(s_t_done, s)
                    dve.wait_ge(s_xnhi_ready, s)
                    for j in range(J):
                        ins = nc.vector.tensor_scalar(xn[:, j, :], x_sb[:, par, j, :], mv[:, j, 0:1],
                                                      rstd[:, j:j + 1], ALU.subtract, ALU.mult)
                    ins.then_inc(s_xn_ready, 1)

                def xn_low(s, par):
                    dve.wait_ge(s_xnhi_ready, s + 1)
                    nc.vector.tensor_tensor(xn_lo[:, par, :, 0:D], xn[:, :, :],
                                            xn_hi[:, par, :, 0:D].bitcast(F32), ALU.subtract).then_inc(s_xnlo_ready, 1)

                dve.wait_ge(s_w_in, 16 * 7)
                for n in range(2):
                    dve.wait_ge(s_wa1, n)
                    nc.vector.tensor_tensor(wprod[:, :, :], wx_f[:, :, 0:D],
                                            attn_bc[:, n:n + 1, :].broadcast_to([P, KC, D]), ALU.mult).then_inc(s_wa0, 1)
                    dve.wait_ge(s_wa0, n + 1)
                    nc.vector.tensor_reduce(wx_f[:, :, D + n * H:D + (n + 1) * H],
                                            wprod[:, :, :].rearrange("p c (h d) -> p c h d", h=H),
                                            axis=AX.X, op=ALU.add).then_inc(s_wa1, 1)
                for n, (hi, lo) in enumerate(((wq_hi, wq_lo), (wk_hi, wk_lo))):
                    dve.wait_ge(s_wsplit, n + 1)
                    nc.vector.tensor_tensor(lo[:, :, :], psR[n][:, :].rearrange("p (c o) -> p c o", c=KC),
                                            hi[:, :, :].bitcast(F32), ALU.subtract).then_inc(s_wsplit_lo, 1)
                dve.wait_ge(s_wsplit, 5)
                nc.vector.tensor_tensor(wx_lo[:, :, :], wx_f[:, :, :], wx_hi[:, :, :].bitcast(F32),
                                        ALU.subtract).then_inc(s_wsplit_lo, 1)
                stats(0, 0, 0)
                norm(0, 0)
                xn_low(0, 0)

                def step(s, par, h, last):
                    for c in range(KC):
                        dve.wait_ge(s_hit_done, KC * s + c + 1)
                        nc.vector.tensor_tensor(xt_lo[:, c, :], psT[c][:, 0:TS], xt_hi[:, c, :].bitcast(F32),
                                                ALU.subtract).then_inc(s_lot_done, 1)
                    if not last:
                        stats(s + 1, 1 - par, h + par)
                    for c in range(KC):
                        dve.wait_ge(s_eq_min, KC * s + c + 1)
                        nc.vector.scalar_tensor_tensor(q_all[:, c, bass.ds(s * TS, TS)], psR[c][:, 0:TS], 1.0,
                                                       eq[:, c, :], ALU.add, ALU.max).then_inc(s_q_done, 1)
                    if not last:
                        norm(s + 1, 1 - par)
                    for n in range(2):
                        dve.wait_ge(s_ek_min, 2 * s + n + 1)
                        dve.wait_ge(s_khi_done, 2 * s)
                        dve.wait_ge(s_klo_done, 2 * s)
                        nc.vector.scalar_tensor_tensor(kf[:, n, :, :],
                                                       psR[2 + n][0:T, :].rearrange("p (j o) -> p j o", j=2), 1.0,
                                                       ek[:, n, :, :], ALU.add, ALU.max).then_inc(s_k_done, 1)
                    if not last:
                        dve.wait_ge(s_g_done, s)
                        xn_low(s + 1, 1 - par)
                    for n in range(2):
                        dve.wait_ge(s_khi_done, 2 * s + n + 1)
                        nc.vector.tensor_tensor(k_lo[:, 2 * n:2 * n + 2, :], kf[:, n, :, :],
                                                k_hi[:, 2 * n:2 * n + 2, :].bitcast(F32),
                                                ALU.subtract).then_inc(s_klo_done, 1)

                over_tiles(dve, step, NS)
                dve.wait_ge(s_g_done, NS)
                for c in range(KC):
                    nc.vector.tensor_copy(g_sb[:, c, :], psG[c][:, 0:GW]).then_inc(s_g_out, 1)

            @block.tensor
            def _(pe):
                pe.wait_ge(s_ident1, 1)
                pe.wait_ge(s_w_in, 16 * 7)
                for n in range(4):
                    for oc in range(KC):
                        for ic in range(KC):
                            ins = nc.tensor.transpose(psR[n][:, ic * D + oc * P:ic * D + oc * P + P],
                                                      wqkvp[:, n, oc, ic * P:ic * P + P], ident[:, :])
                    ins.then_inc(s_w_t, 1)

                def transposes(s):
                    pe.wait_ge(s_xn_ready, s + 1)
                    pe.wait_ge(s_hit_done, KC * s)
                    pe.wait_ge(s_lot_done, KC * s)
                    for c in range(KC):
                        for j in range(J):
                            ins = nc.tensor.transpose(psT[c][:, j * T:(j + 1) * T], xn[:, j, c * P:(c + 1) * P],
                                                      ident[0:T, 0:T])
                    ins.then_inc(s_t_done, 1)

                transposes(0)
                pe.wait_ge(s_wsplit, 5)
                pe.wait_ge(s_wsplit_lo, 3)

                def step(s, par, h, last):
                    first = isinstance(s, int) and s == 0
                    pe.wait_ge(s_hit_done, KC * (s + 1))
                    pe.wait_ge(s_lot_done, KC * (s + 1))
                    pe.wait_ge(s_tab_ready, J * s)
                    for c in range(KC):
                        n = 0
                        for wgt, xt in ((wq_hi, xt_hi), (wq_lo, xt_hi), (wq_hi, xt_lo)):
                            for kc in range(KC):
                                ins = nc.tensor.matmul(psR[c][:, 0:TS], wgt[:, kc, c * P:(c + 1) * P], xt[:, kc, :],
                                                       start=n == 0, stop=n == 3 * KC - 1)
                                n += 1
                        ins.then_inc(s_q_mm, 1)
                    for j in range(J):
                        n = 0
                        for xt, wgt in ((xt_hi, wk_hi), (xt_hi, wk_lo), (xt_lo, wk_hi)):
                            for kc in range(KC):
                                ins = nc.tensor.matmul(psR[2 + j // 2][0:T, (j % 2) * D:(j % 2 + 1) * D],
                                                       xt[:, kc, j * T:(j + 1) * T], wgt[:, kc, :],
                                                       start=n == 0, stop=n == 3 * KC - 1)
                                n += 1
                        if j % 2:
                            ins.then_inc(s_k_mm, 1)
                    for j in range(J):
                        if j < KC:
                            pe.wait_ge(s_q_done, KC * s + j + 1)
                        else:
                            pe.wait_ge(s_k_done, 2 * s + j - KC + 1)
                        n = 0
                        for xt, wgt in ((xt_hi, wx_hi), (xt_hi, wx_lo), (xt_lo, wx_hi)):
                            for kc in range(KC):
                                ins = nc.tensor.matmul(psR[j][0:T, 0:XW], xt[:, kc, j * T:(j + 1) * T], wgt[:, kc, :],
                                                       start=n == 0, stop=n == 3 * KC - 1)
                                n += 1
                        ins.then_inc(s_xt_mm, 1)
                    if not last:
                        transposes(s + 1)
                    pe.wait_ge(s_khi_done, 2 * (s + 1))
                    pe.wait_ge(s_klo_done, 2 * (s + 1))
                    pe.wait_ge(s_xnhi_ready, s + 1)
                    pe.wait_ge(s_xnlo_ready, s + 1)
                    for c in range(KC):
                        for j in range(J):
                            for n, (kk, xx) in enumerate(((k_hi, xn_hi), (k_hi, xn_lo), (k_lo, xn_hi))):
                                ins = nc.tensor.matmul(psG[c][:, 0:GW], kk[:, j, c * P:(c + 1) * P], xx[:, par, j, :],
                                                       start=first and j == 0 and n == 0,
                                                       stop=last and j == J - 1 and n == 2)
                    ins.then_inc(s_g_done, 1)

                over_tiles(pe, step, NS)

        with ExitStack() as ph, nc.Block() as block:
            def sb2(name, shape, dt=F32):
                return sb_in(ph, name, shape, dt)

            heads = sb2("heads", [P, P])
            gt_sb = sb2("gt_sb", [P, KC, D])
            ctx_t = sb2("ctx_t", [P, KC, P])
            ksum = sb2("ksum", [P, KC, P])
            mix_w = sb2("mix_w", [P, KC, D])
            first = sb2("first", [P, T])
            bias_p = sb2("bias_p", [P, D])
            bias_g = sb2("bias_g", [P, E])
            gw_sb = sb2("gw_sb", [P, KC, E])
            before = sb2("before", [P, T])
            ones = sb2("ones", [P, T])
            desc = sb2("desc", [T, J, E])
            limit = sb2("limit", [T, J, E])
            token = sb2("token", [T, J])
            seen = sb2("seen", [T, E])
            isrc = sb2("isrc", [T, 2, J], I32)
            idst = sb2("idst", [T, 2, J], I32)
            gx = sb2("gx", [T, 2, J, TW])
            gl = sb2("gl", [T, 2, J, H])
            qp = sb2("qp", [P, KC, TS])
            att = sb2("att", [T, J, H])
            att2 = sb2("att2", [T, J, H])
            atm = sb2("atm", [T, J])
            ati = sb2("ati", [T, J])
            pr = sb2("pr", [T, J, H, DH])
            pr2 = sb2("pr2", [T, J, 2, DH])
            pr4 = sb2("pr4", [T, J, DH])
            xg = sb2("xg", [T, J, D])
            xd = sb2("xd", [T, 2, J, RW])
            st6 = sb2("st6b", [T, J, 6])
            mv = sb2("mvb", [T, J, 2])
            rstd = sb2("rstdb", [T, J])
            nmr = sb2("nmr", [T, J])
            xn2 = sb2("xn2", [T, J, D])
            x2t = sb2("x2t", [P, KC, TS])
            lmax = sb2("lmax", [T, J])
            eqm = sb2("eqm", [T, J, E])
            lex = sb2("lex", [T, J, E])
            lsum = sb2("lsum", [T, J])
            wmax = sb2("wmax", [T, J])
            oh = sb2("oh", [T, J, E])
            cum = sb2("cum", [T, J + 1, E])
            pos = sb2("pos", [T, J, E])
            over = sb2("over", [T, J, E])
            slotf = sb2("slotf", [T, J])
            slots = sb2("slots", [T, 2, J], I32)

            psD = [ps_in(ph, f"psD{c}", [P, 512]) for c in range(KC)]
            psM = [ps_in(ph, f"psM{c}", [P, 512]) for c in range(2)]
            psX = [ps_in(ph, f"psX{c}", [P, 512]) for c in range(KC)]
            psL = ps_in(ph, "psL", [P, 512])
            psC = ps_in(ph, "psC", [P, 512])

            s_c_in = sem_in(ph, "s_c_in")
            s_c_zero = sem_in(ph, "s_c_zero")
            s_c_set = sem_in(ph, "s_c_set")
            s_c_gate = sem_in(ph, "s_c_gate")
            s_gt_mm = sem_in(ph, "s_gt_mm")
            s_gt_sb_done = sem_in(ph, "s_gt_sb_done")
            s_ctx_mm = sem_in(ph, "s_ctx_mm")
            s_ctx_done = sem_in(ph, "s_ctx_done")
            s_ks_done = sem_in(ph, "s_ks_done")
            s_mixw_mm = sem_in(ph, "s_mixw_mm")
            s_mixw_done = sem_in(ph, "s_mixw_done")
            s_x_in0 = sem_in(ph, "s_x_in0")
            s_x_in1 = sem_in(ph, "s_x_in1")
            s_idx_in0 = sem_in(ph, "s_idx_in0")
            s_idx_in1 = sem_in(ph, "s_idx_in1")
            s_gat0 = sem_in(ph, "s_gat0")
            s_gat1 = sem_in(ph, "s_gat1")
            s_x_out0 = sem_in(ph, "s_x_out0")
            s_x_out1 = sem_in(ph, "s_x_out1")
            s_scat0 = sem_in(ph, "s_scat0")
            s_scat1 = sem_in(ph, "s_scat1")
            s_d_mm = sem_in(ph, "s_d_mm")
            s_den_done = sem_in(ph, "s_den_done")
            s_qp_done = sem_in(ph, "s_qp_done")
            s_mix_mm = sem_in(ph, "s_mix_mm")
            s_a_sum = sem_in(ph, "s_a_sum")
            s_a_lin = sem_in(ph, "s_a_lin")
            s_a_max = sem_in(ph, "s_a_max")
            s_a_sub = sem_in(ph, "s_a_sub")
            s_a_exp = sem_in(ph, "s_a_exp")
            s_a_tot = sem_in(ph, "s_a_tot")
            s_a_inv = sem_in(ph, "s_a_inv")
            s_a_div = sem_in(ph, "s_a_div")
            s_pr_done = sem_in(ph, "s_pr_done")
            s_pr2_done = sem_in(ph, "s_pr2_done")
            s_pr4_done = sem_in(ph, "s_pr4_done")
            s_xg_done = sem_in(ph, "s_xg_done")
            s_x2_ready = sem_in(ph, "s_x2_ready")
            s_stats2 = sem_in(ph, "s_stats2")
            s_aggr2 = sem_in(ph, "s_aggr2")
            s_var2 = sem_in(ph, "s_var2")
            s_rstd2 = sem_in(ph, "s_rstd2")
            s_nmr_done = sem_in(ph, "s_nmr_done")
            s_xn2_ready = sem_in(ph, "s_xn2_ready")
            s_t2_done = sem_in(ph, "s_t2_done")
            s_x2t_ready = sem_in(ph, "s_x2t_ready")
            s_lg_mm = sem_in(ph, "s_lg_mm")
            s_l_max = sem_in(ph, "s_l_max")
            s_l_eq = sem_in(ph, "s_l_eq")
            s_l_sub = sem_in(ph, "s_l_sub")
            s_l_exp = sem_in(ph, "s_l_exp")
            s_l_sum = sem_in(ph, "s_l_sum")
            s_prb_done = sem_in(ph, "s_prb_done")
            s_w_done = sem_in(ph, "s_w_done")
            s_w_max = sem_in(ph, "s_w_max")
            s_oh_done = sem_in(ph, "s_oh_done")
            s_cum_done = sem_in(ph, "s_cum_done")
            s_pos_mm = sem_in(ph, "s_pos_mm")
            s_seen_done = sem_in(ph, "s_seen_done")
            s_pos_done = sem_in(ph, "s_pos_done")
            s_over_done = sem_in(ph, "s_over_done")
            s_pos2_done = sem_in(ph, "s_pos2_done")
            s_pick_done = sem_in(ph, "s_pick_done")
            s_slot_sum = sem_in(ph, "s_slot_sum")
            s_slots_ready = sem_in(ph, "s_slots_ready")
            s_tok_set = sem_in(ph, "s_tok_set")
            s_token_next = sem_in(ph, "s_token_next")
            s_pool_passed = sem_in(ph, "s_pool_passed")
            s_dve_passed = sem_in(ph, "s_dve_passed")
            x_in, idx_in = [s_x_in0, s_x_in1], [s_idx_in0, s_idx_in1]
            gat, x_out, scat = [s_gat0, s_gat1], [s_x_out0, s_x_out1], [s_scat0, s_scat1]

            @block.sync
            def _(sp):
                sp.wait_ge(s_c_zero, 1)
                sp.dma_start(bias_p[0:1, :], bproj.rearrange("(a n) -> a n", a=1)).then_inc(s_c_in, 16)
                sp.dma_start(bias_g[0:1, :], gate_b.rearrange("(a n) -> a n", a=1)).then_inc(s_c_in, 16)
                sp.dma_start(gw_sb[:, :, :], gate_w.rearrange("(c p) e -> p c e", p=P)).then_inc(s_c_in, 16)

                def idx(t, s):
                    return t[bass.ds(s * TS, TS)].rearrange("(p j) -> p j", j=J)

                def load(s, par):
                    sp.dma_start(isrc[:, par, :], idx(src, s)).then_inc(idx_in[par], 16)
                    sp.dma_start(idst[:, par, :], idx(dst, s)).then_inc(idx_in[par], 16)
                    sp.dma_start(x_sb[:, par, :, :], tok(x, s, D)).then_inc(x_in[par], 16)

                load(0, 0)
                load(1, 1)

                def step(s, par, h, more):
                    sp.wait_ge(s_x2_ready, 2 * (s + 1))
                    sp.dma_start(tok(out, s, D), xd[:, par, :, 0:D]).then_inc(x_out[par], 16)
                    if more:
                        sp.wait_ge(s_xg_done, s + 1)
                        sp.wait_ge(gat[par], 32 * J * (h + 1))
                        load(s + 2, par)

                step(0, 0, 0, True)
                step(1, 1, 0, True)
                with sp.Fori(1, (NS - 3) // 2) as i:
                    step(2 * i, 0, i, True)
                    step(2 * i + 1, 1, i, True)
                step(NS - 3, 0, (NS - 3) // 2, True)
                step(NS - 2, 1, 0, False)
                step(NS - 1, 0, 0, False)
                for par in range(2):
                    n = NS // 2 + (1 - par)
                    sp.wait_ge(x_out[par], 16 * n)
                    sp.wait_ge(scat[par], 16 * J * n)

            @block.gpsimd
            def _(pool):
                nc.gpsimd.memset(first[:, :], 0.0)
                nc.gpsimd.memset(bias_p[:, :], 0.0)
                nc.gpsimd.memset(bias_g[:, :], 0.0)
                nc.gpsimd.memset(before[:, :], 1.0)
                nc.gpsimd.memset(ones[:, :], 1.0).then_inc(s_c_zero, 1)
                pool.wait_ge(s_c_zero, 1)
                nc.gpsimd.memset(first[0:1, :], 1.0)
                nc.gpsimd.affine_select(out=before[:, :], in_=before[:, :], compare_op=ALU.is_gt, fill=0.0,
                                        base=0, pattern=[[1, T]], channel_multiplier=-1)
                nc.gpsimd.iota(desc[:, :, :], [[0, J], [-1, E]], base=E, channel_multiplier=0,
                               allow_small_or_imprecise_dtypes=True)
                nc.gpsimd.iota(limit[:, :, :], [[0, J], [ROWS, E]], base=CAP, channel_multiplier=0,
                               allow_small_or_imprecise_dtypes=True)
                nc.gpsimd.iota(token[:, :], [[1, J]], base=0, channel_multiplier=J,
                               allow_small_or_imprecise_dtypes=True)
                nc.gpsimd.memset(xd[:, :, :, :], 0.0)
                nc.gpsimd.memset(cum[:, 0, :], 0.0)
                nc.gpsimd.memset(seen[:, :], 0.0).then_inc(s_c_set, 1)
                pool.wait_ge(s_c_set, 1)
                nc.gpsimd.iota(seen[0:1, :], [[ROWS, E]], base=0, channel_multiplier=0,
                               allow_small_or_imprecise_dtypes=True).then_inc(s_c_set, 1)

                def gather(s, par, h):
                    pool.wait_ge(idx_in[par], 32 * (h + 1))
                    pool.wait_ge(s_pr_done, s - 1 if not isinstance(s, int) else max(s - 1, 0))
                    passed(pool, s_pool_passed)
                    for j in range(J):
                        pool.indirect_dma_start(out=gx[:, par, j, :], out_offset=None, in_=table,
                                                in_offset=bass.IndirectOffsetOnAxis(ap=idst[:, par, j:j + 1], axis=0))\
                            .then_inc(gat[par], 16)
                        pool.indirect_dma_start(out=gl[:, par, j, :], out_offset=None, in_=table_l,
                                                in_offset=bass.IndirectOffsetOnAxis(ap=isrc[:, par, j:j + 1], axis=0))\
                            .then_inc(gat[par], 16)

                def scatter(s, par):
                    pool.wait_ge(s_slots_ready, s + 1)
                    passed(pool, s_pool_passed)
                    for j in range(J):
                        pool.indirect_dma_start(out=rows, in_=xd[:, par, j, :], in_offset=None,
                                                out_offset=bass.IndirectOffsetOnAxis(ap=slots[:, par, j:j + 1], axis=0),
                                                bounds_check=E * ROWS - 1, oob_is_err=False).then_inc(scat[par], 16)

                def rstd_of(s):
                    pool.wait_ge(s_aggr2, J * (s + 1))
                    pool.wait_ge(s_xn2_ready, s)
                    passed(pool, s_pool_passed)
                    nc.gpsimd.tensor_scalar(rstd[:, :], mv[:, :, 1], EPS, None, ALU.add).then_inc(s_var2, 1)
                    pool.wait_ge(s_var2, s + 1)
                    nc.gpsimd.tensor_tensor(rstd[:, :], rstd[:, :], mhalf[0:T, :], ALU.pow).then_inc(s_rstd2, 1)

                gather(0, 0, 0)
                gather(1, 1, 0)
                rstd_of(0)

                def pair(i):
                    gather(2 * i + 2, 0, i + 1)
                    rstd_of(2 * i + 1)
                    scatter(2 * i, 0)
                    gather(2 * i + 3, 1, i + 1)
                    rstd_of(2 * i + 2)
                    scatter(2 * i + 1, 1)

                pair(0)
                with pool.Fori(1, (NS - 3) // 2) as i:
                    pair(i)
                gather(NS - 1, 0, NS // 2)
                rstd_of(NS - 2)
                scatter(NS - 3, 0)
                rstd_of(NS - 1)
                scatter(NS - 2, 1)
                scatter(NS - 1, 0)

            @block.scalar
            def _(act):
                for c in range(KC):
                    act.wait_ge(s_gt_mm, KC)
                    act.activation(gt_sb[:, c, :], psD[c][:, 0:D], ACT.Copy).then_inc(s_gt_sb_done, 1)
                for c in range(KC):
                    act.wait_ge(s_mixw_mm, KC)
                    act.activation(mix_w[:, c, :], psX[c][:, 0:D], ACT.Copy).then_inc(s_mixw_done, 1)

                def first_half(s, par, h):
                    act.wait_ge(s_a_sub, s + 1)
                    act.activation(att2[:, :, :], att2[:, :, :], ACT.Exp).then_inc(s_a_exp, 1)
                    act.wait_ge(s_nmr_done, s + 1)
                    act.wait_ge(s_t2_done, s)
                    for j in range(J):
                        ins = act.activation(xn2[:, j, :], xd[:, par, j, 0:D], ACT.Identity, bias=nmr[:, j:j + 1],
                                             scale=rstd[:, j:j + 1])
                    ins.then_inc(s_xn2_ready, 1)

                def second_half(s, par, h):
                    act.wait_ge(s_t2_done, s + 1)
                    for c in range(KC):
                        act.activation(x2t[:, c, :], psX[c][:, 0:TS], ACT.Copy).then_inc(s_x2t_ready, 1)
                    act.wait_ge(s_l_sub, s + 1)
                    act.activation(lex[:, :, :], lex[:, :, :], ACT.Exp).then_inc(s_l_exp, 1)

                halves(act, first_half, second_half)

            @block.vector
            def _(dve):
                nc.vector.memset(heads[:, :], 0.0).then_inc(s_tok_set, 1)
                dve.wait_ge(s_tok_set, 1)
                for b in range(P // QD):
                    ins = nc.vector.memset(heads[b * QD:(b + 1) * QD, b * QD:(b + 1) * QD], 1.0)
                ins.then_inc(s_tok_set, 1)
                dve.wait_ge(s_tok_set, 2)
                for c in range(KC):
                    nc.vector.tensor_scalar(ksum[:, c, :], heads[:, :], g_sb[:, c, D:D + 1], None, ALU.mult)\
                      .then_inc(s_ks_done, 1)
                for c in range(KC):
                    dve.wait_ge(s_ctx_mm, KC)
                    nc.vector.tensor_tensor(ctx_t[:, c, :], psM[c][:, 0:P], heads[:, :], ALU.mult).then_inc(s_ctx_done, 1)
                dve.wait_ge(s_c_set, 2)

                def first_half(s, par, h):
                    for c in range(KC):
                        dve.wait_ge(s_d_mm, KC * s + c + 1)
                        dve.wait_ge(s_mix_mm, 2 * s)
                        nc.vector.reciprocal(qp[:, c, :], psD[c][:, 0:TS]).then_inc(s_den_done, 1)
                    for c in range(KC):
                        dve.wait_ge(s_den_done, KC * s + c + 1)
                        nc.vector.scalar_tensor_tensor(qp[:, c, :], qp[:, c, :], 1e6, q_all[:, c, bass.ds(s * TS, TS)],
                                                       ALU.min, ALU.mult).then_inc(s_qp_done, 1)
                    dve.wait_ge(gat[par], 32 * J * (h + 1))
                    nc.vector.tensor_tensor(att[:, :, :], gl[:, par, :, :], gx[:, par, :, D:TW], ALU.add)\
                      .then_inc(s_a_sum, 1)
                    dve.wait_ge(s_a_sum, s + 1)
                    nc.vector.scalar_tensor_tensor(att2[:, :, :], att[:, :, :], 0.01, att[:, :, :], ALU.mult, ALU.max)\
                      .then_inc(s_a_lin, 1)
                    dve.wait_ge(s_a_lin, s + 1)
                    nc.vector.tensor_reduce(atm[:, :], att2[:, :, :], axis=AX.X, op=ALU.max).then_inc(s_a_max, 1)
                    dve.wait_ge(s_a_max, s + 1)
                    nc.vector.tensor_tensor(att2[:, :, :], att2[:, :, :], wide(atm[:, :], H), ALU.subtract)\
                      .then_inc(s_a_sub, 1)
                    dve.wait_ge(s_a_exp, s + 1)
                    nc.vector.tensor_reduce(atm[:, :], att2[:, :, :], axis=AX.X, op=ALU.add).then_inc(s_a_tot, 1)
                    dve.wait_ge(s_a_tot, s + 1)
                    nc.vector.reciprocal(ati[:, :], atm[:, :]).then_inc(s_a_inv, 1)
                    dve.wait_ge(s_a_inv, s + 1)
                    nc.vector.tensor_tensor(att2[:, :, :], att2[:, :, :], wide(ati[:, :], H), ALU.mult)\
                      .then_inc(s_a_div, 1)
                    dve.wait_ge(s_a_div, s + 1)
                    nc.vector.tensor_tensor(pr[:, :, :, :],
                                            gx[:, par, :, 0:D].rearrange("p j (h d) -> p j h d", h=H),
                                            wide(att2[:, :, :], DH), ALU.mult).then_inc(s_pr_done, 1)
                    dve.wait_ge(s_pr_done, s + 1)
                    nc.vector.tensor_tensor(pr2[:, :, :, :], pr[:, :, 0:2, :], pr[:, :, 2:4, :], ALU.add)\
                      .then_inc(s_pr2_done, 1)
                    dve.wait_ge(s_pr2_done, s + 1)
                    nc.vector.tensor_tensor(pr4[:, :, :], pr2[:, :, 0, :], pr2[:, :, 1, :], ALU.add)\
                      .then_inc(s_pr4_done, 1)
                    dve.wait_ge(s_pr4_done, s + 1)
                    dve.wait_ge(x_in[par], 16 * (h + 1))
                    nc.vector.tensor_tensor(xg[:, :, :].rearrange("p j (h d) -> p j h d", h=H),
                                            x_sb[:, par, :, :].rearrange("p j (h d) -> p j h d", h=H),
                                            pr4[:, :, :].rearrange("p j (a d) -> p j a d", a=1)
                                            .broadcast_to([T, J, H, DH]), ALU.add).then_inc(s_xg_done, 1)
                    dve.wait_ge(s_xg_done, s + 1)
                    dve.wait_ge(x_out[par], 16 * h)
                    dve.wait_ge(scat[par], 16 * J * h)
                    for n in range(2):
                        dve.wait_ge(s_mix_mm, 2 * s + n + 1)
                        nc.vector.tensor_tensor(xd[:, par, 2 * n:2 * n + 2, 0:D],
                                                psM[n][0:T, :].rearrange("p (j o) -> p j o", j=2),
                                                xg[:, 2 * n:2 * n + 2, :], ALU.add).then_inc(s_x2_ready, 1)
                    nc.vector.tensor_scalar(xd[:, par, :, D + 1], token[:, :], 0.0, None, ALU.add)
                    for j in range(J):
                        dve.wait_ge(s_x2_ready, 2 * s + j // 2 + 1)
                        nc.vector.bn_stats(st6[:, j, :], xd[:, par, j, 0:D]).then_inc(s_stats2, 1)
                    nc.vector.tensor_scalar(token[:, :], token[:, :], float(TS), None, ALU.add).then_inc(s_token_next, 1)
                    dve.wait_ge(s_stats2, J * (s + 1))
                    passed(dve, s_dve_passed)
                    for j in range(J):
                        nc.vector.bn_aggr(mv[:, j, :], st6[:, j, :]).then_inc(s_aggr2, 1)
                    dve.wait_ge(s_rstd2, s + 1)
                    nc.vector.scalar_tensor_tensor(nmr[:, :], mv[:, :, 0], -1.0, rstd[:, :], ALU.mult, ALU.mult)\
                      .then_inc(s_nmr_done, 1)

                def second_half(s, par, h):
                    lg = psL[0:T, 0:J * E].rearrange("p (j e) -> p j e", e=E)
                    dve.wait_ge(s_lg_mm, s + 1)
                    nc.vector.tensor_reduce(lmax[:, :], lg, axis=AX.X, op=ALU.max).then_inc(s_l_max, 1)
                    dve.wait_ge(s_l_max, s + 1)
                    nc.vector.tensor_tensor(lex[:, :, :], lg, wide(lmax[:, :], E), ALU.subtract).then_inc(s_l_sub, 1)
                    nc.vector.tensor_tensor(eqm[:, :, :], lg, wide(lmax[:, :], E), ALU.is_equal).then_inc(s_l_eq, 1)
                    dve.wait_ge(s_l_eq, s + 1)
                    nc.vector.tensor_tensor(eqm[:, :, :], eqm[:, :, :], desc[:, :, :], ALU.mult).then_inc(s_w_done, 1)
                    dve.wait_ge(s_w_done, s + 1)
                    nc.vector.tensor_reduce(wmax[:, :], eqm[:, :, :], axis=AX.X, op=ALU.max).then_inc(s_w_max, 1)
                    dve.wait_ge(s_w_max, s + 1)
                    dve.wait_ge(s_pos_mm, s)
                    nc.vector.tensor_tensor(oh[:, :, :], eqm[:, :, :], wide(wmax[:, :], E), ALU.is_equal)\
                      .then_inc(s_oh_done, 1)
                    for j in range(J):
                        dve.wait_ge(s_oh_done, s + 1)
                        dve.wait_ge(s_cum_done, J * s + j)
                        nc.vector.tensor_tensor(cum[:, j + 1, :], cum[:, j, :], oh[:, j, :], ALU.add)\
                          .then_inc(s_cum_done, 1)
                    dve.wait_ge(s_l_exp, s + 1)
                    nc.vector.tensor_reduce(lsum[:, :], lex[:, :, :], axis=AX.X, op=ALU.add).then_inc(s_l_sum, 1)
                    dve.wait_ge(s_l_sum, s + 1)
                    nc.vector.reciprocal(xd[:, par, :, D], lsum[:, :]).then_inc(s_prb_done, 1)
                    dve.wait_ge(s_pos_mm, s + 1)
                    nc.vector.tensor_tensor(seen[:, :], seen[:, :], cum[:, J, :], ALU.add).then_inc(s_seen_done, 1)
                    nc.vector.tensor_tensor(pos[:, :, :], cum[:, 0:J, :],
                                            psC[0:T, 0:E].rearrange("p (a e) -> p a e", a=1).broadcast_to([T, J, E]),
                                            ALU.add).then_inc(s_pos_done, 1)
                    dve.wait_ge(s_pos_done, s + 1)
                    nc.vector.tensor_tensor(over[:, :, :], pos[:, :, :], limit[:, :, :], ALU.is_ge).then_inc(s_over_done, 1)
                    dve.wait_ge(s_over_done, s + 1)
                    nc.vector.scalar_tensor_tensor(pos[:, :, :], over[:, :, :], BIG, pos[:, :, :], ALU.mult, ALU.add)\
                      .then_inc(s_pos2_done, 1)
                    dve.wait_ge(s_pos2_done, s + 1)
                    nc.vector.tensor_tensor(over[:, :, :], pos[:, :, :], oh[:, :, :], ALU.mult).then_inc(s_pick_done, 1)
                    dve.wait_ge(s_pick_done, s + 1)
                    nc.vector.tensor_reduce(slotf[:, :], over[:, :, :], axis=AX.X, op=ALU.add).then_inc(s_slot_sum, 1)
                    dve.wait_ge(s_slot_sum, s + 1)
                    dve.wait_ge(s_prb_done, s + 1)
                    dve.wait_ge(scat[par], 16 * J * h)
                    nc.vector.tensor_copy(slots[:, par, :], slotf[:, :]).then_inc(s_slots_ready, 1)

                halves(dve, first_half, second_half)

            @block.tensor
            def _(pe):
                for c in range(KC):
                    for fc in range(KC):
                        ins = nc.tensor.transpose(psD[c][:, fc * P:(fc + 1) * P], g_sb[:, fc, c * P:(c + 1) * P],
                                                  ident[:, :])
                    ins.then_inc(s_gt_mm, 1)
                pe.wait_ge(s_gt_sb_done, KC)
                for ec in range(KC):
                    for cc in range(KC):
                        ins = nc.tensor.matmul(psM[ec][:, 0:P], wv_t[:, cc, ec * P:(ec + 1) * P],
                                               gt_sb[:, cc, ec * P:(ec + 1) * P], start=cc == 0, stop=cc == KC - 1)
                    ins.then_inc(s_ctx_mm, 1)
                pe.wait_ge(s_ctx_done, KC)
                for fc in range(KC):
                    nc.tensor.matmul(psX[fc][:, 0:D], ctx_t[:, fc, :], wp_t[:, fc, :], start=True, stop=True)\
                      .then_inc(s_mixw_mm, 1)
                pe.wait_ge(s_mixw_done, KC)
                pe.wait_ge(s_ks_done, KC)
                pe.wait_ge(s_c_in, 48)
                pe.wait_ge(s_c_set, 2)

                def denominators(s):
                    pe.wait_ge(s_qp_done, KC * s)
                    for c in range(KC):
                        nc.tensor.matmul(psD[c][:, 0:TS], ksum[:, c, :], q_all[:, c, bass.ds(s * TS, TS)],
                                         start=True, stop=True).then_inc(s_d_mm, 1)

                def first_half(s, par, h):
                    pe.wait_ge(s_qp_done, KC * (s + 1))
                    pe.wait_ge(s_x2_ready, 2 * s)
                    for j in range(J):
                        o = psM[j // 2][0:T, (j % 2) * D:(j % 2 + 1) * D]
                        nc.tensor.matmul(o, first[:, :], bias_p[:, :], start=True, stop=False)
                        for kc in range(KC):
                            ins = nc.tensor.matmul(o, qp[:, kc, j * T:(j + 1) * T], mix_w[:, kc, :],
                                                   start=False, stop=kc == KC - 1)
                        if j % 2:
                            ins.then_inc(s_mix_mm, 1)

                def second_half(s, more=True):
                    pe.wait_ge(s_xn2_ready, s + 1)
                    pe.wait_ge(s_x2t_ready, KC * s)
                    for c in range(KC):
                        for j in range(J):
                            ins = nc.tensor.transpose(psX[c][:, j * T:(j + 1) * T], xn2[:, j, c * P:(c + 1) * P],
                                                      ident[0:T, 0:T])
                    ins.then_inc(s_t2_done, 1)
                    if more:
                        denominators(s + 1)
                    pe.wait_ge(s_x2t_ready, KC * (s + 1))
                    pe.wait_ge(s_l_sub, s)
                    pe.wait_ge(s_l_eq, s)
                    for j in range(J):
                        o = psL[0:T, j * E:(j + 1) * E]
                        nc.tensor.matmul(o, first[:, :], bias_g[:, :], start=True, stop=False)
                        for kc in range(KC):
                            ins = nc.tensor.matmul(o, x2t[:, kc, j * T:(j + 1) * T], gw_sb[:, kc, :],
                                                   start=False, stop=kc == KC - 1)
                    ins.then_inc(s_lg_mm, 1)
                    pe.wait_ge(s_cum_done, J * (s + 1))
                    pe.wait_ge(s_seen_done, s)
                    pe.wait_ge(s_pos_done, s)
                    nc.tensor.matmul(psC[0:T, 0:E], before[0:T, :], cum[:, J, :], start=True, stop=False)
                    nc.tensor.matmul(psC[0:T, 0:E], ones[0:T, :], seen[:, :], start=False, stop=True)\
                      .then_inc(s_pos_mm, 1)

                denominators(0)
                first_half(0, 0, 0)
                second_half(0)
                first_half(1, 0, 0)
                with pe.Fori(1, NS - 1) as s:
                    second_half(s)
                    first_half(s + 1, 0, 0)
                second_half(NS - 1, more=False)

        late.close()
        with ExitStack() as ph, nc.Block() as block:
            def sb3(name, shape, dt=F32):
                return sb_in(ph, name, shape, dt)

            NG = E * ST
            wraw = sb3("wraw", [P, KC * F + NF * D])
            w1_raw = wraw[:, 0:KC * F].rearrange("p (c f) -> p c f", c=KC)
            w2_raw = wraw[:, KC * F:].rearrange("p (c d) -> p c d", c=NF)
            w1_hi = sb3("w1_hi", [P, KC, F], F32R)
            w1_lo = sb3("w1_lo", [P, KC, F], F32R)
            w2_hi = sb3("w2_hi", [P, NF, D], F32R)
            w2_lo = sb3("w2_lo", [P, NF, D], F32R)
            b1_rows = sb3("b1_rows", [E * NF, P])
            b1_sb = sb3("b1_sb", [P, E * NF])
            b2_bc = sb3("b2_bc", [T3, E, D])
            xr = sb3("xr", [T3, 2, J, RW])
            st6 = sb3("st6c", [T3, J, 6])
            mv = sb3("mvc", [T3, J, 2])
            std = sb3("std", [T3, J])
            rstd = sb3("rstdc", [T3, J])
            nmr = sb3("nmrc", [T3, J])
            eps_c = sb3("eps_c", [P, 1])
            xn3 = sb3("xn3", [T3, J, D])
            xt_hi = sb3("xt3_hi", [P, 2, KC, TS3], F32R)
            xt_lo = sb3("xt3_lo", [P, 2, KC, TS3], F32R)
            hf = sb3("hf", [P, 4, TS3])
            h_hi = sb3("h_hi", [P, 4, TS3], F32R)
            h_lo = sb3("h_lo", [P, 4, TS3], F32R)
            yb = sb3("yb", [T3, J, D])
            ys = sb3("ys", [T3, J, D])
            yc = sb3("yc", [T3, J, D])
            fin = sb3("fin", [T3, J, D], I32)
            o_sb = sb3("o_sb", [T3, 2, J, D])
            tok_i = sb3("tok_i", [T3, 2, J], I32)

            psX = [ps_in(ph, f"psX3{c}", [P, 512]) for c in range(KC)]
            psH = [ps_in(ph, f"psH{c}", [P, 512]) for c in range(2)]
            psY = [ps_in(ph, f"psY{c}", [P, 512]) for c in range(J)]

            s_b_in = sem_in(ph, "s_b_in")
            s_w_in = sem_in(ph, "s_w_in")
            s_w1hi = sem_in(ph, "s_w1hi")
            s_w1lo = sem_in(ph, "s_w1lo")
            s_w2hi = sem_in(ph, "s_w2hi")
            s_w2lo = sem_in(ph, "s_w2lo")
            s_xr_in0 = sem_in(ph, "s_xr_in0")
            s_xr_in1 = sem_in(ph, "s_xr_in1")
            s_stats = sem_in(ph, "s_stats")
            s_aggr = sem_in(ph, "s_aggr")
            s_std_ready = sem_in(ph, "s_std_ready")
            s_rstd_ready = sem_in(ph, "s_rstd_ready")
            s_nmr_ready = sem_in(ph, "s_nmr_ready")
            s_xn_ready = sem_in(ph, "s_xn_ready")
            s_t_done = sem_in(ph, "s_t_done")
            s_hit = sem_in(ph, "s_hit")
            s_lot = sem_in(ph, "s_lot")
            s_h_mm = sem_in(ph, "s_h_mm")
            s_hf_ready = sem_in(ph, "s_hf_ready")
            s_hhi_ready = sem_in(ph, "s_hhi_ready")
            s_hlo_ready = sem_in(ph, "s_hlo_ready")
            s_w2_mm = sem_in(ph, "s_w2_mm")
            s_yb_done = sem_in(ph, "s_yb_done")
            s_ys_done = sem_in(ph, "s_ys_done")
            s_yc_done = sem_in(ph, "s_yc_done")
            s_fin_done = sem_in(ph, "s_fin_done")
            s_nan_done = sem_in(ph, "s_nan_done")
            s_yz_done = sem_in(ph, "s_yz_done")
            s_yp_done = sem_in(ph, "s_yp_done")
            s_o_ready = sem_in(ph, "s_o_ready")
            s_tok_ready = sem_in(ph, "s_tok_ready")
            s_sc0 = sem_in(ph, "s_sc0")
            s_sc1 = sem_in(ph, "s_sc1")
            s_eps_set = sem_in(ph, "s_eps_set")
            s_b1_t = sem_in(ph, "s_b1_t")
            s_b1_set = sem_in(ph, "s_b1_set")
            s_pool_passed = sem_in(ph, "s_pool_passed")
            s_dve_passed = sem_in(ph, "s_dve_passed")
            s_act_passed = sem_in(ph, "s_act_passed")
            xr_in, sc = [s_xr_in0, s_xr_in1], [s_sc0, s_sc1]

            def over_experts(eng, body):
                body(0, False)
                with eng.Fori(1, E - 1) as e:
                    body(e, False)
                body(E - 1, True)

            @block.sync
            def _(sp):
                def load_w(e):
                    w1e = w1[bass.ds(e, 1), :, :].rearrange("a (c p) f -> p (a c) f", p=P)
                    w2e = w2[bass.ds(e, 1), :, :].rearrange("a (c p) d -> p (a c) d", p=P)
                    sp.dma_start(w1_raw, w1e).then_inc(s_w_in, 16)
                    sp.dma_start(w2_raw, w2e).then_inc(s_w_in, 16)

                def load_x(g, par):
                    sp.dma_start(xr[:, par, :, :],
                                 rows[bass.ds(g * TS3, TS3), :].rearrange("(p j) w -> p j w", j=J)).then_inc(xr_in[par], 16)

                load_x(0, 0)
                load_w(0)
                sp.dma_start(b1_rows[:, :], b1.rearrange("e (c p) -> (e c) p", p=P)).then_inc(s_b_in, 16)
                sp.dma_start(b2_bc[:, :, :], b2.rearrange("(a e) d -> a (e d)", a=1).partition_broadcast(T3)
                             ).then_inc(s_b_in, 16)
                load_x(1, 1)

                def body(e, last):
                    if not last:
                        for sem in (s_w1hi, s_w1lo, s_w2hi, s_w2lo):
                            sp.wait_ge(sem, NF * (e + 1))
                        load_w(e + 1)
                    for st in range(ST):
                        if not (last and st >= ST - 2):
                            g = ST * e + st
                            sp.wait_ge(s_o_ready, g + 1)
                            sp.wait_ge(s_tok_ready, g + 1)
                            load_x(g + 2, st % 2)

                over_experts(sp, body)
                sp.wait_ge(sc[0], 16 * J * (NG // 2))
                sp.wait_ge(sc[1], 16 * J * (NG // 2))

            @block.gpsimd
            def _(pool):
                def body(e, last):
                    for st in range(ST):
                        g, par = ST * e + st, st % 2
                        pool.wait_ge(s_ys_done, J * (g + 1))
                        pool.wait_ge(s_yp_done, g)
                        passed(pool, s_pool_passed)
                        nc.gpsimd.tensor_scalar(fin[:, :, :], ys[:, :, :], 0.0, 0.0, ALU.mult, ALU.is_equal)\
                          .then_inc(s_fin_done, 1)
                        pool.wait_ge(s_o_ready, g + 1)
                        pool.wait_ge(s_tok_ready, g + 1)
                        passed(pool, s_pool_passed)
                        for j in range(J):
                            pool.indirect_dma_start(out=out, in_=o_sb[:, par, j, :], in_offset=None,
                                                    out_offset=bass.IndirectOffsetOnAxis(ap=tok_i[:, par, j:j + 1], axis=0),
                                                    bounds_check=N - 1, oob_is_err=False).then_inc(sc[par], 16)

                over_experts(pool, body)

            @block.scalar
            def _(act):
                def split_w1(f, n):
                    act.wait_ge(s_w_in, 32 * n)
                    act.activation(w1_hi[:, :, f * P:(f + 1) * P], w1_raw[:, :, f * P:(f + 1) * P], ACT.Copy)\
                       .then_inc(s_w1hi, 1)

                def split_w2(f, n):
                    act.wait_ge(s_w_in, 32 * n)
                    act.activation(w2_hi[:, f, :], w2_raw[:, f, :], ACT.Copy).then_inc(s_w2hi, 1)

                def normal(g, par, use):
                    act.wait_ge(s_aggr, J * (g + 1))
                    act.wait_ge(s_rstd_ready, g)
                    act.activation(std[:, :], mv[:, :, 1], ACT.Sqrt, bias=eps_c[0:T3, :]).then_inc(s_std_ready, 1)
                    act.wait_ge(s_nmr_ready, g + 1)
                    act.wait_ge(s_t_done, g)
                    for j in range(J):
                        ins = act.activation(xn3[:, j, :], xr[:, par, j, 0:D], ACT.Identity, bias=nmr[:, j:j + 1],
                                             scale=rstd[:, j:j + 1])
                    ins.then_inc(s_xn_ready, 1)

                def high_t(g, par):
                    act.wait_ge(s_t_done, g + 1)
                    for c in range(KC):
                        act.activation(xt_hi[:, par, c, :], psX[c][:, 0:TS3], ACT.Copy).then_inc(s_hit, 1)

                act.wait_ge(s_eps_set, 1)
                normal(0, 0, 0)
                high_t(0, 0)
                for f in range(NF):
                    split_w1(f, 1)
                    split_w2(f, 1)
                act.wait_ge(s_b1_t, 1)
                act.activation(b1_sb[:, :], psY[0][:, 0:E * NF], ACT.Copy).then_inc(s_b1_set, 1)
                act.wait_ge(s_b1_set, 1)

                def body(e, last):
                    for st in range(ST):
                        g, par = ST * e + st, st % 2
                        refill = st == ST - 1 and not last
                        for f in range(NF):
                            act.wait_ge(s_h_mm, NF * g + f + 1)
                            act.wait_ge(s_hlo_ready, NF * g + f - 3 if f >= 4 else NF * g)
                            passed(act, s_act_passed)
                            act.activation(hf[:, f % 4, :], psH[f % 2][:, 0:TS3], ACT.Relu,
                                           bias=b1_sb[:, bass.ds(e * NF + f, 1)]).then_inc(s_hf_ready, 1)
                            if f == 2 and not (last and st == ST - 1):
                                normal(g + 1, 1 - par, 0)
                            if f == 6 and not (last and st == ST - 1):
                                high_t(g + 1, 1 - par)
                            if refill:
                                split_w1(f, e + 2)
                        if refill:
                            for f in range(NF):
                                act.wait_ge(s_w2_mm, NF * g + f + 1)
                                split_w2(f, e + 2)

                over_experts(act, body)

            @block.vector
            def _(dve):
                nc.vector.memset(eps_c[:, :], EPS).then_inc(s_eps_set, 1)

                def split_w1(f, n):
                    dve.wait_ge(s_w1hi, NF * (n - 1) + f + 1)
                    nc.vector.tensor_tensor(w1_lo[:, :, f * P:(f + 1) * P], w1_raw[:, :, f * P:(f + 1) * P],
                                            w1_hi[:, :, f * P:(f + 1) * P].bitcast(F32), ALU.subtract).then_inc(s_w1lo, 1)

                def split_w2(f, n):
                    dve.wait_ge(s_w2hi, NF * (n - 1) + f + 1)
                    nc.vector.tensor_tensor(w2_lo[:, f, :], w2_raw[:, f, :], w2_hi[:, f, :].bitcast(F32),
                                            ALU.subtract).then_inc(s_w2lo, 1)

                def stats(g, par, n):
                    dve.wait_ge(xr_in[par], 16 * n)
                    for j in range(J):
                        nc.vector.bn_stats(st6[:, j, :], xr[:, par, j, 0:D]).then_inc(s_stats, 1)
                    dve.wait_ge(s_xn_ready, g)
                    dve.wait_ge(s_stats, J * (g + 1))
                    passed(dve, s_dve_passed)
                    for j in range(J):
                        nc.vector.bn_aggr(mv[:, j, :], st6[:, j, :]).then_inc(s_aggr, 1)

                def scales(g):
                    dve.wait_ge(s_std_ready, g + 1)
                    nc.vector.reciprocal(rstd[:, :], std[:, :]).then_inc(s_rstd_ready, 1)
                    dve.wait_ge(s_rstd_ready, g + 1)
                    nc.vector.scalar_tensor_tensor(nmr[:, :], mv[:, :, 0], -1.0, rstd[:, :], ALU.mult, ALU.mult)\
                      .then_inc(s_nmr_ready, 1)

                def low_t(g, par):
                    for c in range(KC):
                        dve.wait_ge(s_hit, KC * g + c + 1)
                        nc.vector.tensor_tensor(xt_lo[:, par, c, :], psX[c][:, 0:TS3], xt_hi[:, par, c, :].bitcast(F32),
                                                ALU.subtract).then_inc(s_lot, 1)

                stats(0, 0, 1)
                scales(0)
                low_t(0, 0)
                for f in range(NF):
                    split_w1(f, 1)
                    split_w2(f, 1)
                dve.wait_ge(s_b_in, 32)
                dve.wait_ge(s_b1_set, 1)

                def body(e, last):
                    for st in range(ST):
                        g, par = ST * e + st, st % 2
                        end = last and st == ST - 1
                        refill = st == ST - 1 and not last
                        for f in range(NF):
                            dve.wait_ge(s_hf_ready, NF * g + f + 1)
                            dve.wait_ge(s_w2_mm, NF * g + f - 3 if f >= 4 else NF * g)
                            nc.vector.tensor_copy(h_hi[:, f % 4, :], hf[:, f % 4, :]).then_inc(s_hhi_ready, 1)
                            dve.wait_ge(s_hhi_ready, NF * g + f + 1)
                            nc.vector.tensor_tensor(h_lo[:, f % 4, :], hf[:, f % 4, :], h_hi[:, f % 4, :].bitcast(F32),
                                                    ALU.subtract).then_inc(s_hlo_ready, 1)
                            if f == 0 and not end:
                                stats(g + 1, 1 - par, e * (ST // 2) + (st + 1) // 2 + 1)
                            if f == 2 and not end:
                                scales(g + 1)
                            if f == 6 and not end:
                                low_t(g + 1, 1 - par)
                            if refill:
                                split_w1(f, e + 2)
                        for j in range(J):
                            dve.wait_ge(s_w2_mm, NF * (g + 1))
                            nc.vector.tensor_tensor(yb[:, j, :], psY[j][0:T3, 0:D],
                                                    b2_bc[:, bass.ds(e, 1), :].rearrange("p a d -> p (a d)"),
                                                    ALU.add).then_inc(s_yb_done, 1)
                        for j in range(J):
                            dve.wait_ge(s_yb_done, J * g + j + 1)
                            nc.vector.tensor_scalar(ys[:, j, :], yb[:, j, :], xr[:, par, j, D:D + 1], None, ALU.mult)\
                              .then_inc(s_ys_done, 1)
                        dve.wait_ge(s_ys_done, J * (g + 1))
                        nc.vector.tensor_scalar(yc[:, :, :], ys[:, :, :], -1e4, 1e4, ALU.max, ALU.min).then_inc(s_yc_done, 1)
                        nc.vector.tensor_tensor(yb[:, :, :], ys[:, :, :], ys[:, :, :], ALU.is_equal).then_inc(s_nan_done, 1)
                        dve.wait_ge(s_nan_done, g + 1)
                        dve.wait_ge(s_yc_done, g + 1)
                        nc.vector.tensor_tensor(yc[:, :, :], yc[:, :, :], yb[:, :, :], ALU.mult).then_inc(s_yz_done, 1)
                        dve.wait_ge(s_yz_done, g + 1)
                        dve.wait_ge(s_fin_done, g + 1)
                        passed(dve, s_dve_passed)
                        nc.vector.copy_predicated(yc[:, :, :], fin[:, :, :], ys[:, :, :]).then_inc(s_yp_done, 1)
                        dve.wait_ge(s_yp_done, g + 1)
                        dve.wait_ge(sc[par], 16 * J * (e * (ST // 2) + st // 2))
                        nc.vector.tensor_copy(tok_i[:, par, :], xr[:, par, :, D + 1]).then_inc(s_tok_ready, 1)
                        nc.vector.tensor_tensor(o_sb[:, par, :, :], yc[:, :, :], xr[:, par, :, 0:D], ALU.add)\
                          .then_inc(s_o_ready, 1)
                        if refill:
                            for f in range(NF):
                                split_w2(f, e + 2)

                over_experts(dve, body)

            @block.tensor
            def _(pe):
                def transposes(g):
                    pe.wait_ge(s_xn_ready, g + 1)
                    pe.wait_ge(s_hit, KC * g)
                    pe.wait_ge(s_lot, KC * g)
                    for c in range(KC):
                        for j in range(J):
                            ins = nc.tensor.transpose(psX[c][:, j * T3:(j + 1) * T3], xn3[:, j, c * P:(c + 1) * P],
                                                      ident[0:T3, 0:T3])
                    ins.then_inc(s_t_done, 1)

                pe.wait_ge(s_b_in, 32)
                nc.tensor.transpose(psY[0][:, 0:E * NF], b1_rows[:, :], ident[0:E * NF, 0:E * NF]).then_inc(s_b1_t, 1)
                transposes(0)
                pe.wait_ge(s_b1_set, 1)

                def body(e, last):
                    for st in range(ST):
                        g, par = ST * e + st, st % 2
                        for slot in range(NF + 2):
                            if slot < NF:
                                f = slot
                                if f == 0:
                                    pe.wait_ge(s_hit, KC * (g + 1))
                                    pe.wait_ge(s_lot, KC * (g + 1))
                                if st == 0:
                                    pe.wait_ge(s_w1hi, NF * e + f + 1)
                                    pe.wait_ge(s_w1lo, NF * e + f + 1)
                                pe.wait_ge(s_hf_ready, NF * g + f - 1 if f >= 2 else NF * g)
                                n = 0
                                for w, xt in ((w1_hi, xt_hi), (w1_lo, xt_hi), (w1_hi, xt_lo)):
                                    for kc in range(KC):
                                        ins = nc.tensor.matmul(psH[f % 2][:, 0:TS3], w[:, kc, f * P:(f + 1) * P],
                                                               xt[:, par, kc, :], start=n == 0, stop=n == 3 * KC - 1)
                                        n += 1
                                ins.then_inc(s_h_mm, 1)
                            if slot == 5 and not (last and st == ST - 1):
                                transposes(g + 1)
                            if slot >= 2:
                                f = slot - 2
                                if f == 0:
                                    pe.wait_ge(s_yb_done, J * g)
                                if st == 0:
                                    pe.wait_ge(s_w2hi, NF * e + f + 1)
                                    pe.wait_ge(s_w2lo, NF * e + f + 1)
                                pe.wait_ge(s_hhi_ready, NF * g + f + 1)
                                pe.wait_ge(s_hlo_ready, NF * g + f + 1)
                                for j in range(J):
                                    for n, (hh, w) in enumerate(((h_hi, w2_hi), (h_hi, w2_lo), (h_lo, w2_hi))):
                                        ins = nc.tensor.matmul(psY[j][0:T3, 0:D], hh[:, f % 4, j * T3:(j + 1) * T3],
                                                               w[:, f, :], start=f == 0 and n == 0,
                                                               stop=f == NF - 1 and n == 2)
                                ins.then_inc(s_w2_mm, 1)

                over_experts(pe, body)

_INS = ["x", "src", "dst", "L0_gnn_weight", "L0_gnn_attn_l", "L0_gnn_attn_r", "L0_mix_Wq", "L0_mix_Wkv",
        "L0_mix_Wproj", "L0_mix_bproj", "L0_ffn_gate_w", "L0_ffn_gate_b", "L0_ffn_w1", "L0_ffn_b1",
        "L0_ffn_w2", "L0_ffn_b2"]


def kernel(**inputs):
    import numpy as _np
    import concourse.bacc as _bacc
    from concourse import mybir as _mybir
    from concourse.bass_utils import run_bass_kernel_spmd as _run

    nc = _bacc.Bacc("TRN2", target_bir_lowering=False, num_devices=1)
    arrays, args = {}, []
    for name in _INS:
        a = _np.ascontiguousarray(inputs[name])
        arrays[f"in_{name}"] = a
        args.append(nc.dram_tensor(f"in_{name}", a.shape, _mybir.dt.from_np(a.dtype), kind="ExternalInput").ap())
    out = nc.dram_tensor("out_0", arrays["in_x"].shape, _mybir.dt.float32, kind="ExternalOutput").ap()
    gps_layer(nc, *args, out)
    r = _run(nc, [arrays], core_ids=[0])
    return r.results[0]["out_0"]
```

```python
from contextlib import ExitStack

import concourse.bass as bass
from concourse import mybir

ALU = mybir.AluOpType
ACT = mybir.ActivationFunctionType
F32 = mybir.dt.float32
F32R = mybir.dt.float32r
I32 = mybir.dt.int32
AX = mybir.AxisListType

P = 128
EPS = 1e-5
FAR = 60000.0
BIG = 1000000.0


def passed(eng, sem):
    eng.sem_inc(sem)


def over_tiles(eng, step, n):
    step(0, 0, 0, False)
    step(1, 1, 0, False)
    with eng.Fori(1, n // 2) as i:
        step(2 * i, 0, i, False)
        step(2 * i + 1, 1, i, False)
    step(n - 1, 0, n // 2, True)


def gps_layer(nc, x, src, dst, gnn_w, attn_l, attn_r, wq, wkv, wproj, bproj,
              gate_w, gate_b, w1, b1, w2, b2, out):
    N, D = x.shape
    H, DH = attn_l.shape
    E, _, F = w1.shape
    QH = 8
    QD = D // QH
    KC = D // P
    T, J = 125, 4
    TS = T * J
    NS = N // TS
    assert NS * TS == N and NS % 2 == 1
    CAP = -(-5 * N // (4 * E))
    T3 = 124
    TS3 = T3 * J
    ST = -(-CAP // TS3)
    ROWS = ST * TS3
    NF = F // P
    XW = D + 2 * H
    TW = D + H
    RW = D + 4
    GW = D + 2

    table = nc.dram_tensor("graph_table", [N, TW], F32, kind="Internal").ap()
    table_l = nc.dram_tensor("alpha_l_table", [N, H], F32, kind="Internal").ap()
    rows = nc.dram_tensor("expert_rows", [E * ROWS, RW], F32, kind="Internal").ap()

    base = ExitStack()

    def sb_in(stack, name, shape, dt=F32):
        return stack.enter_context(nc.sbuf_tensor(name, shape, dt))

    def ps_in(stack, name, shape):
        return stack.enter_context(nc.psum_tensor(name, shape, F32))

    def sem_in(stack, name):
        return stack.enter_context(nc.semaphore(name))

    def tok(t, s, w):
        return t[bass.ds(s * TS, TS), :].rearrange("(p j) w -> p j w", j=J)

    def wide(a, n):
        dims = list(a.shape)
        names = "pjh"[:len(dims)]
        spread = a.rearrange(f"{' '.join(names[:-1])} ({names[-1]} z) -> {' '.join(names)} z", z=1)
        return spread.broadcast_to(dims + [n])

    with base:
        def sb(name, shape, dt=F32):
            return sb_in(base, name, shape, dt)

        ident = sb("ident", [P, P])
        mhalf = sb("mhalf", [P, J])
        x_sb = sb("x_sb", [T, 2, J, D])
        wv_t = sb("wv_t", [P, KC, D])
        wp_t = sb("wp_t", [P, KC, D])
        g_sb = sb("g_sb", [P, KC, GW])

        late = ExitStack()
        q_all = sb_in(late, "q_all", [P, KC, N])

        with ExitStack() as ph, nc.Block() as block:
            def sb1(name, shape, dt=F32):
                return sb_in(ph, name, shape, dt)

            wqkvp = q_all[:, 0, N - 4 * KC * D:N].rearrange("p (n c i) -> p n c i", n=4, c=KC)
            attn_bc = q_all[:, 1, N - 2 * D:N].rearrange("p (n i) -> p n i", n=2)
            wprod = q_all[:, 1, N - 4 * D:N - 2 * D].rearrange("p (c i) -> p c i", c=KC)
            wx_f = sb1("wx_f", [P, KC, XW])
            wx_hi = sb1("wx_hi", [P, KC, XW], F32R)
            wx_lo = sb1("wx_lo", [P, KC, XW], F32R)
            wq_hi = sb1("wq_hi", [P, KC, D], F32R)
            wq_lo = sb1("wq_lo", [P, KC, D], F32R)
            wk_hi = sb1("wk_hi", [P, KC, D], F32R)
            wk_lo = sb1("wk_lo", [P, KC, D], F32R)
            empty = sb1("empty", [P, J, RW])
            st6 = sb1("st6", [T, J, 6])
            mv = sb1("mv", [T, J, 2])
            rstd = sb1("rstd", [T, J])
            xn = sb1("xn", [T, J, D])
            xn_hi = sb1("xn_hi", [T, 2, J, GW], F32R)
            xn_lo = sb1("xn_lo", [T, 2, J, GW], F32R)
            xt_hi = sb1("xt_hi", [P, KC, TS], F32R)
            xt_lo = sb1("xt_lo", [P, KC, TS], F32R)
            eq = sb1("eq", [P, KC, TS])
            ek = sb1("ek", [T, 2, 2, D])
            kf = sb1("kf", [T, 2, 2, D])
            k_hi = sb1("k_hi", [T, J, D], F32R)
            k_lo = sb1("k_lo", [T, J, D], F32R)
            tab_sb = sb1("tab_sb", [T, 2, J, XW])

            psT = [ps_in(ph, f"psT{c}", [P, 512]) for c in range(KC)]
            psG = [ps_in(ph, f"psG{c}", [P, 512]) for c in range(KC)]
            psR = [ps_in(ph, f"psR{c}", [P, 512]) for c in range(4)]

            s_w_in = sem_in(ph, "s_w_in")
            s_w_t = sem_in(ph, "s_w_t")
            s_wt_out = sem_in(ph, "s_wt_out")
            s_ident0 = sem_in(ph, "s_ident0")
            s_ident1 = sem_in(ph, "s_ident1")
            s_const1 = sem_in(ph, "s_const1")
            s_wa0 = sem_in(ph, "s_wa0")
            s_wa1 = sem_in(ph, "s_wa1")
            s_wsplit = sem_in(ph, "s_wsplit")
            s_wsplit_lo = sem_in(ph, "s_wsplit_lo")
            s_empty_set = sem_in(ph, "s_empty_set")
            s_empty_out = sem_in(ph, "s_empty_out")
            s_var_ready = sem_in(ph, "s_var_ready")
            s_mhalf_set = sem_in(ph, "s_mhalf_set")
            s_pool_passed = sem_in(ph, "s_pool_passed")
            s_dve_passed = sem_in(ph, "s_dve_passed")
            s_x_in0 = sem_in(ph, "s_x_in0")
            s_x_in1 = sem_in(ph, "s_x_in1")
            s_stats = sem_in(ph, "s_stats")
            s_aggr = sem_in(ph, "s_aggr")
            s_rstd_ready = sem_in(ph, "s_rstd_ready")
            s_xn_ready = sem_in(ph, "s_xn_ready")
            s_xnhi_ready = sem_in(ph, "s_xnhi_ready")
            s_xnlo_ready = sem_in(ph, "s_xnlo_ready")
            s_t_done = sem_in(ph, "s_t_done")
            s_hit_done = sem_in(ph, "s_hit_done")
            s_lot_done = sem_in(ph, "s_lot_done")
            s_q_mm = sem_in(ph, "s_q_mm")
            s_k_mm = sem_in(ph, "s_k_mm")
            s_xt_mm = sem_in(ph, "s_xt_mm")
            s_g_done = sem_in(ph, "s_g_done")
            s_eq_exp = sem_in(ph, "s_eq_exp")
            s_ek_exp = sem_in(ph, "s_ek_exp")
            s_eq_min = sem_in(ph, "s_eq_min")
            s_ek_min = sem_in(ph, "s_ek_min")
            s_q_done = sem_in(ph, "s_q_done")
            s_k_done = sem_in(ph, "s_k_done")
            s_khi_done = sem_in(ph, "s_khi_done")
            s_klo_done = sem_in(ph, "s_klo_done")
            s_tab_ready = sem_in(ph, "s_tab_ready")
            s_tab_out0 = sem_in(ph, "s_tab_out0")
            s_tab_out1 = sem_in(ph, "s_tab_out1")
            s_g_out = sem_in(ph, "s_g_out")
            x_in = [s_x_in0, s_x_in1]
            tab_out = [s_tab_out0, s_tab_out1]

            @block.sync
            def _(sp):
                def load_x(s, par):
                    sp.dma_start(x_sb[:, par, :, :], tok(x, s, D)).then_inc(x_in[par], 16)

                load_x(0, 0)
                for n, w in enumerate((wq, wkv[0:D, :], wkv[D:2 * D, :], wproj)):
                    sp.dma_start(wqkvp[:, n, :, :], w.rearrange("(c p) i -> p c i", p=P)).then_inc(s_w_in, 16)
                sp.dma_start(wx_f[:, :, 0:D], gnn_w.rearrange("(c p) o -> p c o", p=P)).then_inc(s_w_in, 16)
                for n, a in enumerate((attn_r, attn_l)):
                    sp.dma_start(attn_bc[:, n, :], a.rearrange("(a h) d -> a (h d)", a=1).partition_broadcast(P))\
                      .then_inc(s_w_in, 16)
                load_x(1, 1)

                def step(s, par, h, last, load):
                    if load:
                        sp.wait_ge(s_xn_ready, s + 1)
                        load_x(s + 2, par)
                    sp.wait_ge(s_tab_ready, J * (s + 1))
                    sp.dma_start(tok(table, s, TW), tab_sb[:, par, :, 0:TW]).then_inc(tab_out[par], 16)
                    sp.dma_start(tok(table_l, s, H), tab_sb[:, par, :, TW:XW]).then_inc(tab_out[par], 16)

                step(0, 0, 0, False, True)
                step(1, 1, 0, False, True)
                with sp.Fori(1, (NS - 3) // 2) as i:
                    step(2 * i, 0, i, False, True)
                    step(2 * i + 1, 1, i, False, True)
                step(NS - 3, 0, (NS - 3) // 2, False, True)
                step(NS - 2, 1, 0, False, False)
                step(NS - 1, 0, 0, True, False)
                sp.wait_ge(tab_out[0], 32 * (NS // 2 + 1))
                sp.wait_ge(tab_out[1], 32 * (NS // 2))
                sp.wait_ge(s_empty_out, 16 * (E * ROWS // (P * J)))

            @block.gpsimd
            def _(pool):
                nc.gpsimd.memset(ident[:, :], 0.0).then_inc(s_ident0, 1)
                pool.wait_ge(s_ident0, 1)
                nc.gpsimd.affine_select(out=ident[:, :], in_=ident[:, :], compare_op=ALU.not_equal, fill=1.0,
                                        base=0, pattern=[[-1, P]], channel_multiplier=1).then_inc(s_ident1, 1)
                nc.gpsimd.memset(empty[:, :, :], 0.0).then_inc(s_empty_set, 1)
                pool.wait_ge(s_empty_set, 1)
                nc.gpsimd.memset(empty[:, :, D + 1:D + 2], FAR).then_inc(s_empty_set, 1)
                pool.wait_ge(s_empty_set, 2)
                groups = rows.rearrange("(g p j) w -> g p (j w)", p=P, j=J)
                with pool.Fori(0, E * ROWS // (P * J)) as g:
                    pool.dma_start(groups[bass.ds(g, 1), :, :].rearrange("a p w -> (a p) w"),
                                   empty[:, :, :].rearrange("p j w -> p (j w)")).then_inc(s_empty_out, 16)

                def rstd_of(s):
                    pool.wait_ge(s_aggr, J * (s + 1))
                    pool.wait_ge(s_xn_ready, s)
                    passed(pool, s_pool_passed)
                    nc.gpsimd.tensor_scalar(rstd[:, :], mv[:, :, 1], EPS, None, ALU.add).then_inc(s_var_ready, 1)
                    pool.wait_ge(s_var_ready, s + 1)
                    nc.gpsimd.tensor_tensor(rstd[:, :], rstd[:, :], mhalf[0:T, :], ALU.pow).then_inc(s_rstd_ready, 1)

                nc.gpsimd.memset(mhalf[:, :], -0.5).then_inc(s_mhalf_set, 1)
                pool.wait_ge(s_mhalf_set, 1)
                rstd_of(0)

                def step(s, par, h, last):
                    for c in range(KC):
                        pool.wait_ge(s_eq_exp, KC * s + c + 1)
                        passed(pool, s_pool_passed)
                        nc.gpsimd.tensor_scalar(eq[:, c, :], eq[:, c, :], 1.0, None, ALU.min).then_inc(s_eq_min, 1)
                        if c == 0 and not last:
                            rstd_of(s + 1)
                    for n in range(2):
                        pool.wait_ge(s_ek_exp, 2 * s + n + 1)
                        passed(pool, s_pool_passed)
                        nc.gpsimd.tensor_scalar(ek[:, n, :, :], ek[:, n, :, :], 1.0, None, ALU.min).then_inc(s_ek_min, 1)

                over_tiles(pool, step, NS)

            @block.scalar
            def _(act):
                for n, o in enumerate((wq_hi, wk_hi, wv_t, wp_t)):
                    act.wait_ge(s_w_t, n + 1)
                    act.activation(o[:, :, :], psR[n][:, :].rearrange("p (c o) -> p c o", c=KC), ACT.Copy)\
                       .then_inc(s_wsplit, 1)
                act.wait_ge(s_wa1, 2)
                act.activation(wx_hi[:, :, :], wx_f[:, :, :], ACT.Copy).then_inc(s_wsplit, 1)

                def xn_high(s, par):
                    act.wait_ge(s_xn_ready, s + 1)
                    act.activation(xn_hi[:, par, :, 0:D], xn[:, :, :], ACT.Copy).then_inc(s_xnhi_ready, 1)

                act.wait_ge(s_const1, 1)
                xn_high(0, 0)

                def step(s, par, h, last):
                    act.wait_ge(s_t_done, s + 1)
                    for c in range(KC):
                        act.activation(xt_hi[:, c, :], psT[c][:, 0:TS], ACT.Copy).then_inc(s_hit_done, 1)
                    for c in range(KC):
                        act.wait_ge(s_q_mm, KC * s + c + 1)
                        act.wait_ge(s_q_done, KC * s)
                        act.activation(eq[:, c, :], psR[c][:, 0:TS], ACT.Exp).then_inc(s_eq_exp, 1)
                    for n in range(2):
                        act.wait_ge(s_k_mm, 2 * s + n + 1)
                        act.wait_ge(s_k_done, 2 * s)
                        act.activation(ek[:, n, :, :], psR[2 + n][0:T, :].rearrange("p (j o) -> p j o", j=2),
                                       ACT.Exp).then_inc(s_ek_exp, 1)
                    if not last:
                        act.wait_ge(s_g_done, s)
                        xn_high(s + 1, 1 - par)
                    for n in range(2):
                        act.wait_ge(s_k_done, 2 * s + n + 1)
                        act.wait_ge(s_g_done, s)
                        act.activation(k_hi[:, 2 * n:2 * n + 2, :], kf[:, n, :, :], ACT.Copy).then_inc(s_khi_done, 1)
                    for j in range(J):
                        act.wait_ge(s_xt_mm, J * s + j + 1)
                        if j == 0:
                            act.wait_ge(tab_out[par], 32 * h)
                        act.activation(tab_sb[:, par, j, :], psR[j][0:T, 0:XW], ACT.Copy).then_inc(s_tab_ready, 1)

                over_tiles(act, step, NS)

            @block.vector
            def _(dve):
                for par in range(2):
                    nc.vector.memset(xn_lo[:, par, :, D:GW].bitcast(F32), 0.0)
                    nc.vector.memset(xn_hi[:, par, :, D + 1:GW].bitcast(F32), 0.0)
                    ins = nc.vector.memset(xn_hi[:, par, :, D:D + 1].bitcast(F32), 1.0)
                ins.then_inc(s_const1, 1)

                def stats(s, par, h):
                    dve.wait_ge(x_in[par], 16 * (h + 1))
                    for j in range(J):
                        nc.vector.bn_stats(st6[:, j, :], x_sb[:, par, j, :]).then_inc(s_stats, 1)
                    dve.wait_ge(s_rstd_ready, s)
                    dve.wait_ge(s_stats, J * (s + 1))
                    passed(dve, s_dve_passed)
                    for j in range(J):
                        nc.vector.bn_aggr(mv[:, j, :], st6[:, j, :]).then_inc(s_aggr, 1)

                def norm(s, par):
                    dve.wait_ge(s_rstd_ready, s + 1)
                    dve.wait_ge(s_t_done, s)
                    dve.wait_ge(s_xnhi_ready, s)
                    for j in range(J):
                        ins = nc.vector.tensor_scalar(xn[:, j, :], x_sb[:, par, j, :], mv[:, j, 0:1],
                                                      rstd[:, j:j + 1], ALU.subtract, ALU.mult)
                    ins.then_inc(s_xn_ready, 1)

                def xn_low(s, par):
                    dve.wait_ge(s_xnhi_ready, s + 1)
                    nc.vector.tensor_tensor(xn_lo[:, par, :, 0:D], xn[:, :, :],
                                            xn_hi[:, par, :, 0:D].bitcast(F32), ALU.subtract).then_inc(s_xnlo_ready, 1)

                dve.wait_ge(s_w_in, 16 * 7)
                for n in range(2):
                    dve.wait_ge(s_wa1, n)
                    nc.vector.tensor_tensor(wprod[:, :, :], wx_f[:, :, 0:D],
                                            attn_bc[:, n:n + 1, :].broadcast_to([P, KC, D]), ALU.mult).then_inc(s_wa0, 1)
                    dve.wait_ge(s_wa0, n + 1)
                    nc.vector.tensor_reduce(wx_f[:, :, D + n * H:D + (n + 1) * H],
                                            wprod[:, :, :].rearrange("p c (h d) -> p c h d", h=H),
                                            axis=AX.X, op=ALU.add).then_inc(s_wa1, 1)
                for n, (hi, lo) in enumerate(((wq_hi, wq_lo), (wk_hi, wk_lo))):
                    dve.wait_ge(s_wsplit, n + 1)
                    nc.vector.tensor_tensor(lo[:, :, :], psR[n][:, :].rearrange("p (c o) -> p c o", c=KC),
                                            hi[:, :, :].bitcast(F32), ALU.subtract).then_inc(s_wsplit_lo, 1)
                dve.wait_ge(s_wsplit, 5)
                nc.vector.tensor_tensor(wx_lo[:, :, :], wx_f[:, :, :], wx_hi[:, :, :].bitcast(F32),
                                        ALU.subtract).then_inc(s_wsplit_lo, 1)
                stats(0, 0, 0)
                norm(0, 0)
                xn_low(0, 0)

                def step(s, par, h, last):
                    for c in range(KC):
                        dve.wait_ge(s_hit_done, KC * s + c + 1)
                        nc.vector.tensor_tensor(xt_lo[:, c, :], psT[c][:, 0:TS], xt_hi[:, c, :].bitcast(F32),
                                                ALU.subtract).then_inc(s_lot_done, 1)
                    if not last:
                        stats(s + 1, 1 - par, h + par)
                    for c in range(KC):
                        dve.wait_ge(s_eq_min, KC * s + c + 1)
                        nc.vector.scalar_tensor_tensor(q_all[:, c, bass.ds(s * TS, TS)], psR[c][:, 0:TS], 1.0,
                                                       eq[:, c, :], ALU.add, ALU.max).then_inc(s_q_done, 1)
                    if not last:
                        norm(s + 1, 1 - par)
                    for n in range(2):
                        dve.wait_ge(s_ek_min, 2 * s + n + 1)
                        dve.wait_ge(s_khi_done, 2 * s)
                        dve.wait_ge(s_klo_done, 2 * s)
                        nc.vector.scalar_tensor_tensor(kf[:, n, :, :],
                                                       psR[2 + n][0:T, :].rearrange("p (j o) -> p j o", j=2), 1.0,
                                                       ek[:, n, :, :], ALU.add, ALU.max).then_inc(s_k_done, 1)
                    if not last:
                        dve.wait_ge(s_g_done, s)
                        xn_low(s + 1, 1 - par)
                    for n in range(2):
                        dve.wait_ge(s_khi_done, 2 * s + n + 1)
                        nc.vector.tensor_tensor(k_lo[:, 2 * n:2 * n + 2, :], kf[:, n, :, :],
                                                k_hi[:, 2 * n:2 * n + 2, :].bitcast(F32),
                                                ALU.subtract).then_inc(s_klo_done, 1)

                over_tiles(dve, step, NS)
                dve.wait_ge(s_g_done, NS)
                for c in range(KC):
                    nc.vector.tensor_copy(g_sb[:, c, :], psG[c][:, 0:GW]).then_inc(s_g_out, 1)

            @block.tensor
            def _(pe):
                pe.wait_ge(s_ident1, 1)
                pe.wait_ge(s_w_in, 16 * 7)
                for n in range(4):
                    for oc in range(KC):
                        for ic in range(KC):
                            ins = nc.tensor.transpose(psR[n][:, ic * D + oc * P:ic * D + oc * P + P],
                                                      wqkvp[:, n, oc, ic * P:ic * P + P], ident[:, :])
                    ins.then_inc(s_w_t, 1)

                def transposes(s):
                    pe.wait_ge(s_xn_ready, s + 1)
                    pe.wait_ge(s_hit_done, KC * s)
                    pe.wait_ge(s_lot_done, KC * s)
                    for c in range(KC):
                        for j in range(J):
                            ins = nc.tensor.transpose(psT[c][:, j * T:(j + 1) * T], xn[:, j, c * P:(c + 1) * P],
                                                      ident[0:T, 0:T])
                    ins.then_inc(s_t_done, 1)

                transposes(0)
                pe.wait_ge(s_wsplit, 5)
                pe.wait_ge(s_wsplit_lo, 3)

                def step(s, par, h, last):
                    first = isinstance(s, int) and s == 0
                    pe.wait_ge(s_hit_done, KC * (s + 1))
                    pe.wait_ge(s_lot_done, KC * (s + 1))
                    pe.wait_ge(s_tab_ready, J * s)
                    for c in range(KC):
                        n = 0
                        for wgt, xt in ((wq_hi, xt_hi), (wq_lo, xt_hi), (wq_hi, xt_lo)):
                            for kc in range(KC):
                                ins = nc.tensor.matmul(psR[c][:, 0:TS], wgt[:, kc, c * P:(c + 1) * P], xt[:, kc, :],
                                                       start=n == 0, stop=n == 3 * KC - 1)
                                n += 1
                        ins.then_inc(s_q_mm, 1)
                    for j in range(J):
                        n = 0
                        for xt, wgt in ((xt_hi, wk_hi), (xt_hi, wk_lo), (xt_lo, wk_hi)):
                            for kc in range(KC):
                                ins = nc.tensor.matmul(psR[2 + j // 2][0:T, (j % 2) * D:(j % 2 + 1) * D],
                                                       xt[:, kc, j * T:(j + 1) * T], wgt[:, kc, :],
                                                       start=n == 0, stop=n == 3 * KC - 1)
                                n += 1
                        if j % 2:
                            ins.then_inc(s_k_mm, 1)
                    for j in range(J):
                        if j < KC:
                            pe.wait_ge(s_q_done, KC * s + j + 1)
                        else:
                            pe.wait_ge(s_k_done, 2 * s + j - KC + 1)
                        n = 0
                        for xt, wgt in ((xt_hi, wx_hi), (xt_hi, wx_lo), (xt_lo, wx_hi)):
                            for kc in range(KC):
                                ins = nc.tensor.matmul(psR[j][0:T, 0:XW], xt[:, kc, j * T:(j + 1) * T], wgt[:, kc, :],
                                                       start=n == 0, stop=n == 3 * KC - 1)
                                n += 1
                        ins.then_inc(s_xt_mm, 1)
                    if not last:
                        transposes(s + 1)
                    pe.wait_ge(s_khi_done, 2 * (s + 1))
                    pe.wait_ge(s_klo_done, 2 * (s + 1))
                    pe.wait_ge(s_xnhi_ready, s + 1)
                    pe.wait_ge(s_xnlo_ready, s + 1)
                    for c in range(KC):
                        for j in range(J):
                            for n, (kk, xx) in enumerate(((k_hi, xn_hi), (k_hi, xn_lo), (k_lo, xn_hi))):
                                ins = nc.tensor.matmul(psG[c][:, 0:GW], kk[:, j, c * P:(c + 1) * P], xx[:, par, j, :],
                                                       start=first and j == 0 and n == 0,
                                                       stop=last and j == J - 1 and n == 2)
                    ins.then_inc(s_g_done, 1)

                over_tiles(pe, step, NS)

        with ExitStack() as ph, nc.Block() as block:
            def sb2(name, shape, dt=F32):
                return sb_in(ph, name, shape, dt)

            heads = sb2("heads", [P, P])
            gt_sb = sb2("gt_sb", [P, KC, D])
            ctx_t = sb2("ctx_t", [P, KC, P])
            ksum = sb2("ksum", [P, KC, QH])
            spread = sb2("spread", [J * QH, J, KC, P])
            q_cur = sb2("q_cur", [P, KC, TS])
            den = sb2("den", [T, J * QH])
            den_t = sb2("den_t", [J * QH, T])
            mix_w = sb2("mix_w", [P, KC, D])
            first = sb2("first", [P, T])
            bias_p = sb2("bias_p", [P, D])
            bias_g = sb2("bias_g", [P, E])
            gw_sb = sb2("gw_sb", [P, KC, E])
            before = sb2("before", [P, T])
            ones = sb2("ones", [P, T])
            desc = sb2("desc", [T, J, E])
            limit = sb2("limit", [T, J, E])
            token = sb2("token", [T, J])
            seen = sb2("seen", [T, E])
            isrc = sb2("isrc", [T, 2, J], I32)
            idst = sb2("idst", [T, 2, J], I32)
            gx = sb2("gx", [T, 2, J, TW])
            gl = sb2("gl", [T, 2, J, H])
            qp = sb2("qp", [P, KC, TS])
            att = sb2("att", [T, J, H])
            att2 = sb2("att2", [T, J, H])
            atm = sb2("atm", [T, J])
            ati = sb2("ati", [T, J])
            pr = sb2("pr", [T, J, H, DH])
            pr2 = sb2("pr2", [T, J, 2, DH])
            pr4 = sb2("pr4", [T, J, DH])
            xg = sb2("xg", [T, J, D])
            xd = sb2("xd", [T, 2, J, RW])
            st6 = sb2("st6b", [T, J, 6])
            mv = sb2("mvb", [T, J, 2])
            rstd = sb2("rstdb", [T, J])
            nmr = sb2("nmr", [T, J])
            xn2 = sb2("xn2", [T, J, D])
            x2t = sb2("x2t", [P, KC, TS])
            lmax = sb2("lmax", [T, J])
            eqm = sb2("eqm", [T, J, E])
            lex = sb2("lex", [T, J, E])
            lsum = sb2("lsum", [T, J])
            wmax = sb2("wmax", [T, J])
            oh = sb2("oh", [T, J, E])
            cum = sb2("cum", [T, J + 1, E])
            pos = sb2("pos", [T, J, E])
            over = sb2("over", [T, J, E])
            slotf = sb2("slotf", [T, J])
            slots = sb2("slots", [T, 2, J], I32)

            psB = [ps_in(ph, f"psB{c}", [P, 512]) for c in range(KC)]
            psM = [ps_in(ph, f"psM{c}", [P, 512]) for c in range(2)]
            psX = [ps_in(ph, f"psX{c}", [P, 512]) for c in range(KC)]
            psL = ps_in(ph, "psL", [P, 512])
            psC = ps_in(ph, "psC", [P, 512])

            s_x_in0 = sem_in(ph, "s_x_in0")
            s_x_in1 = sem_in(ph, "s_x_in1")
            s_idx_in0 = sem_in(ph, "s_idx_in0")
            s_idx_in1 = sem_in(ph, "s_idx_in1")
            s_gat0 = sem_in(ph, "s_gat0")
            s_gat1 = sem_in(ph, "s_gat1")
            s_x_out0 = sem_in(ph, "s_x_out0")
            s_x_out1 = sem_in(ph, "s_x_out1")
            s_scat0 = sem_in(ph, "s_scat0")
            s_scat1 = sem_in(ph, "s_scat1")
            s_c_zero = sem_in(ph, "s_c_zero")
            s_c_in = sem_in(ph, "s_c_in")
            s_x2_ready = sem_in(ph, "s_x2_ready")
            s_xg_done = sem_in(ph, "s_xg_done")
            s_c_set = sem_in(ph, "s_c_set")
            s_pr_done = sem_in(ph, "s_pr_done")
            s_pool_passed = sem_in(ph, "s_pool_passed")
            s_slots_ready = sem_in(ph, "s_slots_ready")
            s_aggr2 = sem_in(ph, "s_aggr2")
            s_xn2_ready = sem_in(ph, "s_xn2_ready")
            s_var2 = sem_in(ph, "s_var2")
            s_rstd2 = sem_in(ph, "s_rstd2")
            s_gt_mm = sem_in(ph, "s_gt_mm")
            s_gt_sb_done = sem_in(ph, "s_gt_sb_done")
            s_mixw_mm = sem_in(ph, "s_mixw_mm")
            s_mixw_done = sem_in(ph, "s_mixw_done")
            s_qp_done = sem_in(ph, "s_qp_done")
            s_d_mm = sem_in(ph, "s_d_mm")
            s_q_ready = sem_in(ph, "s_q_ready")
            s_a_sub = sem_in(ph, "s_a_sub")
            s_a_exp = sem_in(ph, "s_a_exp")
            s_t2_done = sem_in(ph, "s_t2_done")
            s_x2t_ready = sem_in(ph, "s_x2t_ready")
            s_l_sub = sem_in(ph, "s_l_sub")
            s_l_exp = sem_in(ph, "s_l_exp")
            s_nmr_done = sem_in(ph, "s_nmr_done")
            s_heads_set = sem_in(ph, "s_heads_set")
            s_ctx_mm = sem_in(ph, "s_ctx_mm")
            s_ctx_done = sem_in(ph, "s_ctx_done")
            s_dt_mm = sem_in(ph, "s_dt_mm")
            s_den_max = sem_in(ph, "s_den_max")
            s_den_done = sem_in(ph, "s_den_done")
            s_a_sum = sem_in(ph, "s_a_sum")
            s_a_lin = sem_in(ph, "s_a_lin")
            s_a_max = sem_in(ph, "s_a_max")
            s_b_mm = sem_in(ph, "s_b_mm")
            s_den_t = sem_in(ph, "s_den_t")
            s_a_tot = sem_in(ph, "s_a_tot")
            s_a_inv = sem_in(ph, "s_a_inv")
            s_a_div = sem_in(ph, "s_a_div")
            s_mix_mm = sem_in(ph, "s_mix_mm")
            s_pr2_done = sem_in(ph, "s_pr2_done")
            s_pr4_done = sem_in(ph, "s_pr4_done")
            s_stats2 = sem_in(ph, "s_stats2")
            s_token_next = sem_in(ph, "s_token_next")
            s_dve_passed = sem_in(ph, "s_dve_passed")
            s_lg_mm = sem_in(ph, "s_lg_mm")
            s_l_max = sem_in(ph, "s_l_max")
            s_l_eq = sem_in(ph, "s_l_eq")
            s_w_done = sem_in(ph, "s_w_done")
            s_w_max = sem_in(ph, "s_w_max")
            s_oh_done = sem_in(ph, "s_oh_done")
            s_cum_done = sem_in(ph, "s_cum_done")
            s_l_sum = sem_in(ph, "s_l_sum")
            s_prb_done = sem_in(ph, "s_prb_done")
            s_pos_mm = sem_in(ph, "s_pos_mm")
            s_seen_done = sem_in(ph, "s_seen_done")
            s_pos_done = sem_in(ph, "s_pos_done")
            s_over_done = sem_in(ph, "s_over_done")
            s_pos2_done = sem_in(ph, "s_pos2_done")
            s_pick_done = sem_in(ph, "s_pick_done")
            s_slot_sum = sem_in(ph, "s_slot_sum")
            x_in, idx_in = [s_x_in0, s_x_in1], [s_idx_in0, s_idx_in1]
            gat, x_out, scat = [s_gat0, s_gat1], [s_x_out0, s_x_out1], [s_scat0, s_scat1]

            @block.sync
            def _(sp):
                sp.wait_ge(s_c_zero, 1)
                sp.dma_start(bias_p[0:1, :], bproj.rearrange("(a n) -> a n", a=1)).then_inc(s_c_in, 16)
                sp.dma_start(bias_g[0:1, :], gate_b.rearrange("(a n) -> a n", a=1)).then_inc(s_c_in, 16)
                sp.dma_start(gw_sb[:, :, :], gate_w.rearrange("(c p) e -> p c e", p=P)).then_inc(s_c_in, 16)

                def idx(t, s):
                    return t[bass.ds(s * TS, TS)].rearrange("(p j) -> p j", j=J)

                def load(s, par):
                    sp.dma_start(isrc[:, par, :], idx(src, s)).then_inc(idx_in[par], 16)
                    sp.dma_start(idst[:, par, :], idx(dst, s)).then_inc(idx_in[par], 16)
                    sp.dma_start(x_sb[:, par, :, :], tok(x, s, D)).then_inc(x_in[par], 16)

                load(0, 0)
                load(1, 1)

                def step(s, par, h, more):
                    sp.wait_ge(s_x2_ready, 2 * (s + 1))
                    sp.dma_start(tok(out, s, D), xd[:, par, :, 0:D]).then_inc(x_out[par], 16)
                    if more:
                        sp.wait_ge(s_xg_done, s + 1)
                        sp.wait_ge(gat[par], 32 * J * (h + 1))
                        load(s + 2, par)

                step(0, 0, 0, True)
                step(1, 1, 0, True)
                with sp.Fori(1, (NS - 3) // 2) as i:
                    step(2 * i, 0, i, True)
                    step(2 * i + 1, 1, i, True)
                step(NS - 3, 0, (NS - 3) // 2, True)
                step(NS - 2, 1, 0, False)
                step(NS - 1, 0, 0, False)
                for par in range(2):
                    n = NS // 2 + (1 - par)
                    sp.wait_ge(x_out[par], 16 * n)
                    sp.wait_ge(scat[par], 16 * J * n)

            @block.gpsimd
            def _(pool):
                nc.gpsimd.memset(first[:, :], 0.0)
                nc.gpsimd.memset(bias_p[:, :], 0.0)
                nc.gpsimd.memset(bias_g[:, :], 0.0)
                nc.gpsimd.memset(before[:, :], 1.0)
                nc.gpsimd.memset(spread[:, :, :, :], 0.0)
                nc.gpsimd.memset(ones[:, :], 1.0).then_inc(s_c_zero, 1)
                pool.wait_ge(s_c_zero, 1)
                nc.gpsimd.memset(first[0:1, :], 1.0)
                nc.gpsimd.affine_select(out=before[:, :], in_=before[:, :], compare_op=ALU.is_gt, fill=0.0,
                                        base=0, pattern=[[1, T]], channel_multiplier=-1)
                for c in range(KC):
                    nc.gpsimd.affine_select(out=spread[:, :, c, :].rearrange("p j (h d) -> p j h d", d=QD),
                                            in_=spread[:, :, c, :].rearrange("p j (h d) -> p j h d", d=QD),
                                            compare_op=ALU.not_equal, fill=1.0, base=-c * (QH // KC),
                                            pattern=[[-QH, J], [-1, QH // KC], [0, QD]], channel_multiplier=1)
                nc.gpsimd.iota(desc[:, :, :], [[0, J], [-1, E]], base=E, channel_multiplier=0,
                               allow_small_or_imprecise_dtypes=True)
                nc.gpsimd.iota(limit[:, :, :], [[0, J], [ROWS, E]], base=CAP, channel_multiplier=0,
                               allow_small_or_imprecise_dtypes=True)
                nc.gpsimd.iota(token[:, :], [[1, J]], base=0, channel_multiplier=J,
                               allow_small_or_imprecise_dtypes=True)
                nc.gpsimd.memset(xd[:, :, :, :], 0.0)
                nc.gpsimd.memset(cum[:, 0, :], 0.0)
                nc.gpsimd.memset(seen[:, :], 0.0).then_inc(s_c_set, 1)
                pool.wait_ge(s_c_set, 1)
                nc.gpsimd.iota(seen[0:1, :], [[ROWS, E]], base=0, channel_multiplier=0,
                               allow_small_or_imprecise_dtypes=True).then_inc(s_c_set, 1)

                def gather(s, par, h, used):
                    pool.wait_ge(idx_in[par], 32 * (h + 1))
                    if used:
                        pool.wait_ge(s_pr_done, s - 1)
                    passed(pool, s_pool_passed)
                    for j in range(J):
                        pool.indirect_dma_start(out=gx[:, par, j, :], out_offset=None, in_=table,
                                                in_offset=bass.IndirectOffsetOnAxis(ap=idst[:, par, j:j + 1], axis=0))\
                            .then_inc(gat[par], 16)
                        pool.indirect_dma_start(out=gl[:, par, j, :], out_offset=None, in_=table_l,
                                                in_offset=bass.IndirectOffsetOnAxis(ap=isrc[:, par, j:j + 1], axis=0))\
                            .then_inc(gat[par], 16)

                def scatter(s, par):
                    pool.wait_ge(s_slots_ready, s + 1)
                    passed(pool, s_pool_passed)
                    for j in range(J):
                        pool.indirect_dma_start(out=rows, in_=xd[:, par, j, :], in_offset=None,
                                                out_offset=bass.IndirectOffsetOnAxis(ap=slots[:, par, j:j + 1], axis=0),
                                                bounds_check=E * ROWS - 1, oob_is_err=False).then_inc(scat[par], 16)

                def rstd_of(s):
                    pool.wait_ge(s_aggr2, J * (s + 1))
                    pool.wait_ge(s_xn2_ready, s)
                    passed(pool, s_pool_passed)
                    nc.gpsimd.tensor_scalar(rstd[:, :], mv[:, :, 1], EPS, None, ALU.add).then_inc(s_var2, 1)
                    pool.wait_ge(s_var2, s + 1)
                    nc.gpsimd.tensor_tensor(rstd[:, :], rstd[:, :], mhalf[0:T, :], ALU.pow).then_inc(s_rstd2, 1)

                gather(0, 0, 0, False)
                gather(1, 1, 0, False)
                rstd_of(0)

                def pair(i):
                    gather(2 * i + 2, 0, i + 1, True)
                    rstd_of(2 * i + 1)
                    scatter(2 * i, 0)
                    gather(2 * i + 3, 1, i + 1, True)
                    rstd_of(2 * i + 2)
                    scatter(2 * i + 1, 1)

                pair(0)
                with pool.Fori(1, (NS - 3) // 2) as i:
                    pair(i)
                gather(NS - 1, 0, NS // 2, True)
                rstd_of(NS - 2)
                scatter(NS - 3, 0)
                rstd_of(NS - 1)
                scatter(NS - 2, 1)
                scatter(NS - 1, 0)

            def all_steps(a_half, b_half):
                def pair(i):
                    a_half(2 * i + 1, 1, i, False)
                    b_half(2 * i, 0, i)
                    a_half(2 * i + 2, 0, i + 1, False)
                    b_half(2 * i + 1, 1, i)
                return pair

            @block.scalar
            def _(act):
                for c in range(KC):
                    act.wait_ge(s_gt_mm, KC)
                    act.activation(gt_sb[:, c, :], psB[c][:, 0:D], ACT.Copy).then_inc(s_gt_sb_done, 1)
                for c in range(KC):
                    act.wait_ge(s_mixw_mm, KC)
                    act.activation(mix_w[:, c, :], psX[c][:, 0:D], ACT.Copy).then_inc(s_mixw_done, 1)

                def q_of(s):
                    act.wait_ge(s_qp_done, KC * s)
                    act.wait_ge(s_d_mm, s)
                    act.activation(q_cur[:, :, :], q_all[:, :, bass.ds(s * TS, TS)], ACT.Copy).then_inc(s_q_ready, 1)

                def a_half(s, par, h, last):
                    act.wait_ge(s_a_sub, s + 1)
                    act.activation(att2[:, :, :], att2[:, :, :], ACT.Exp).then_inc(s_a_exp, 1)
                    if not last:
                        q_of(s + 1)

                def b_half(s, par, h):
                    act.wait_ge(s_t2_done, s + 1)
                    for c in range(KC):
                        act.activation(x2t[:, c, :], psX[c][:, 0:TS], ACT.Copy).then_inc(s_x2t_ready, 1)
                    act.wait_ge(s_l_sub, s + 1)
                    act.activation(lex[:, :, :], lex[:, :, :], ACT.Exp).then_inc(s_l_exp, 1)

                def normal(s, par):
                    act.wait_ge(s_nmr_done, s + 1)
                    act.wait_ge(s_t2_done, s)
                    for j in range(J):
                        ins = act.activation(xn2[:, j, :], xd[:, par, j, 0:D], ACT.Identity, bias=nmr[:, j:j + 1],
                                             scale=rstd[:, j:j + 1])
                    ins.then_inc(s_xn2_ready, 1)

                def pair(i):
                    a_half(2 * i + 1, 1, i, False)
                    b_half(2 * i, 0, i)
                    normal(2 * i + 1, 1)
                    a_half(2 * i + 2, 0, i + 1, False)
                    b_half(2 * i + 1, 1, i)
                    normal(2 * i + 2, 0)

                q_of(0)
                a_half(0, 0, 0, False)
                normal(0, 0)
                pair(0)
                with act.Fori(1, NS // 2 - 1) as i:
                    pair(i)
                a_half(NS - 2, 1, NS // 2 - 1, False)
                b_half(NS - 3, 0, NS // 2 - 1)
                normal(NS - 2, 1)
                a_half(NS - 1, 0, NS // 2, True)
                b_half(NS - 2, 1, NS // 2 - 1)
                normal(NS - 1, 0)
                b_half(NS - 1, 0, NS // 2)

            @block.vector
            def _(dve):
                nc.vector.memset(heads[:, :], 0.0)
                nc.vector.memset(ksum[:, :, :], 0.0).then_inc(s_heads_set, 1)
                dve.wait_ge(s_heads_set, 1)
                for b in range(P // QD):
                    mine = slice(b * QD, (b + 1) * QD)
                    nc.vector.memset(heads[mine, mine], 1.0)
                    for c in range(KC):
                        h = c * (QH // KC) + b
                        ins = nc.vector.tensor_copy(ksum[mine, c, h:h + 1], g_sb[mine, c, D:D + 1])
                ins.then_inc(s_heads_set, 1)
                dve.wait_ge(s_heads_set, 2)
                for c in range(KC):
                    dve.wait_ge(s_ctx_mm, KC)
                    nc.vector.tensor_tensor(ctx_t[:, c, :], psM[c][:, 0:P], heads[:, :], ALU.mult).then_inc(s_ctx_done, 1)
                dve.wait_ge(s_c_set, 2)

                def a_half(s, par, h, last):
                    dve.wait_ge(s_d_mm, s + 1)
                    dve.wait_ge(s_dt_mm, s)
                    nc.vector.tensor_scalar(den[:, :], psB[0][0:T, 0:J * QH], 1e-6, None, ALU.max).then_inc(s_den_max, 1)
                    dve.wait_ge(s_den_max, s + 1)
                    nc.vector.reciprocal(den[:, :], den[:, :]).then_inc(s_den_done, 1)
                    dve.wait_ge(gat[par], 32 * J * (h + 1))
                    nc.vector.tensor_tensor(att[:, :, :], gl[:, par, :, :], gx[:, par, :, D:TW], ALU.add)\
                      .then_inc(s_a_sum, 1)
                    dve.wait_ge(s_a_sum, s + 1)
                    nc.vector.scalar_tensor_tensor(att2[:, :, :], att[:, :, :], 0.01, att[:, :, :], ALU.mult, ALU.max)\
                      .then_inc(s_a_lin, 1)
                    dve.wait_ge(s_a_lin, s + 1)
                    nc.vector.tensor_reduce(atm[:, :], att2[:, :, :], axis=AX.X, op=ALU.max).then_inc(s_a_max, 1)
                    dve.wait_ge(s_dt_mm, s + 1)
                    dve.wait_ge(s_b_mm, KC * s)
                    nc.vector.tensor_copy(den_t[:, :], psB[1][0:J * QH, 0:T]).then_inc(s_den_t, 1)
                    dve.wait_ge(s_a_max, s + 1)
                    nc.vector.tensor_tensor(att2[:, :, :], att2[:, :, :], wide(atm[:, :], H), ALU.subtract)\
                      .then_inc(s_a_sub, 1)
                    dve.wait_ge(s_a_exp, s + 1)
                    nc.vector.tensor_reduce(atm[:, :], att2[:, :, :], axis=AX.X, op=ALU.add).then_inc(s_a_tot, 1)
                    dve.wait_ge(s_a_tot, s + 1)
                    nc.vector.reciprocal(ati[:, :], atm[:, :]).then_inc(s_a_inv, 1)
                    dve.wait_ge(s_a_inv, s + 1)
                    nc.vector.tensor_tensor(att2[:, :, :], att2[:, :, :], wide(ati[:, :], H), ALU.mult)\
                      .then_inc(s_a_div, 1)
                    dve.wait_ge(s_a_div, s + 1)
                    nc.vector.tensor_tensor(pr[:, :, :, :],
                                            gx[:, par, :, 0:D].rearrange("p j (h d) -> p j h d", h=H),
                                            wide(att2[:, :, :], DH), ALU.mult).then_inc(s_pr_done, 1)
                    dve.wait_ge(s_mix_mm, 2 * s)
                    for c in range(KC):
                        dve.wait_ge(s_b_mm, KC * s + c + 1)
                        nc.vector.tensor_tensor(qp[:, c, :], psB[c][:, 0:TS], q_cur[:, c, :], ALU.mult).then_inc(s_qp_done, 1)
                    dve.wait_ge(s_pr_done, s + 1)
                    nc.vector.tensor_tensor(pr2[:, :, :, :], pr[:, :, 0:2, :], pr[:, :, 2:4, :], ALU.add)\
                      .then_inc(s_pr2_done, 1)
                    dve.wait_ge(s_pr2_done, s + 1)
                    nc.vector.tensor_tensor(pr4[:, :, :], pr2[:, :, 0, :], pr2[:, :, 1, :], ALU.add)\
                      .then_inc(s_pr4_done, 1)
                    dve.wait_ge(s_pr4_done, s + 1)
                    dve.wait_ge(x_in[par], 16 * (h + 1))
                    nc.vector.tensor_tensor(xg[:, :, :].rearrange("p j (h d) -> p j h d", h=H),
                                            x_sb[:, par, :, :].rearrange("p j (h d) -> p j h d", h=H),
                                            pr4[:, :, :].rearrange("p j (a d) -> p j a d", a=1)
                                            .broadcast_to([T, J, H, DH]), ALU.add).then_inc(s_xg_done, 1)
                    dve.wait_ge(s_xg_done, s + 1)
                    dve.wait_ge(x_out[par], 16 * h)
                    dve.wait_ge(scat[par], 16 * J * h)
                    for n in range(2):
                        dve.wait_ge(s_mix_mm, 2 * s + n + 1)
                        nc.vector.tensor_tensor(xd[:, par, 2 * n:2 * n + 2, 0:D],
                                                psM[n][0:T, :].rearrange("p (j o) -> p j o", j=2),
                                                xg[:, 2 * n:2 * n + 2, :], ALU.add).then_inc(s_x2_ready, 1)
                    nc.vector.tensor_scalar(xd[:, par, :, D + 1], token[:, :], 0.0, None, ALU.add)
                    for j in range(J):
                        dve.wait_ge(s_x2_ready, 2 * s + j // 2 + 1)
                        nc.vector.bn_stats(st6[:, j, :], xd[:, par, j, 0:D]).then_inc(s_stats2, 1)
                    nc.vector.tensor_scalar(token[:, :], token[:, :], float(TS), None, ALU.add).then_inc(s_token_next, 1)
                    dve.wait_ge(s_stats2, J * (s + 1))
                    passed(dve, s_dve_passed)
                    for j in range(J):
                        nc.vector.bn_aggr(mv[:, j, :], st6[:, j, :]).then_inc(s_aggr2, 1)

                def scale_of(s):
                    dve.wait_ge(s_rstd2, s + 1)
                    nc.vector.scalar_tensor_tensor(nmr[:, :], mv[:, :, 0], -1.0, rstd[:, :], ALU.mult, ALU.mult)\
                      .then_inc(s_nmr_done, 1)

                def b_half(s, par, h, more=True):
                    lg = psL[0:T, 0:J * E].rearrange("p (j e) -> p j e", e=E)
                    dve.wait_ge(s_lg_mm, s + 1)
                    nc.vector.tensor_reduce(lmax[:, :], lg, axis=AX.X, op=ALU.max).then_inc(s_l_max, 1)
                    dve.wait_ge(s_l_max, s + 1)
                    nc.vector.tensor_tensor(lex[:, :, :], lg, wide(lmax[:, :], E), ALU.subtract).then_inc(s_l_sub, 1)
                    nc.vector.tensor_tensor(eqm[:, :, :], lg, wide(lmax[:, :], E), ALU.is_equal).then_inc(s_l_eq, 1)
                    dve.wait_ge(s_l_eq, s + 1)
                    nc.vector.tensor_tensor(eqm[:, :, :], eqm[:, :, :], desc[:, :, :], ALU.mult).then_inc(s_w_done, 1)
                    dve.wait_ge(s_w_done, s + 1)
                    nc.vector.tensor_reduce(wmax[:, :], eqm[:, :, :], axis=AX.X, op=ALU.max).then_inc(s_w_max, 1)
                    dve.wait_ge(s_w_max, s + 1)
                    nc.vector.tensor_tensor(oh[:, :, :], eqm[:, :, :], wide(wmax[:, :], E), ALU.is_equal)\
                      .then_inc(s_oh_done, 1)
                    for j in range(J):
                        dve.wait_ge(s_oh_done, s + 1)
                        dve.wait_ge(s_cum_done, J * s + j)
                        nc.vector.tensor_tensor(cum[:, j + 1, :], cum[:, j, :], oh[:, j, :], ALU.add)\
                          .then_inc(s_cum_done, 1)
                    dve.wait_ge(s_l_exp, s + 1)
                    nc.vector.tensor_reduce(lsum[:, :], lex[:, :, :], axis=AX.X, op=ALU.add).then_inc(s_l_sum, 1)
                    if more:
                        scale_of(s + 1)
                    dve.wait_ge(s_l_sum, s + 1)
                    nc.vector.reciprocal(xd[:, par, :, D], lsum[:, :]).then_inc(s_prb_done, 1)
                    dve.wait_ge(s_pos_mm, s + 1)
                    nc.vector.tensor_tensor(seen[:, :], seen[:, :], cum[:, J, :], ALU.add).then_inc(s_seen_done, 1)
                    nc.vector.tensor_tensor(pos[:, :, :], cum[:, 0:J, :],
                                            psC[0:T, 0:E].rearrange("p (a e) -> p a e", a=1).broadcast_to([T, J, E]),
                                            ALU.add).then_inc(s_pos_done, 1)
                    dve.wait_ge(s_pos_done, s + 1)
                    nc.vector.tensor_tensor(over[:, :, :], pos[:, :, :], limit[:, :, :], ALU.is_ge).then_inc(s_over_done, 1)
                    dve.wait_ge(s_over_done, s + 1)
                    nc.vector.scalar_tensor_tensor(pos[:, :, :], over[:, :, :], BIG, pos[:, :, :], ALU.mult, ALU.add)\
                      .then_inc(s_pos2_done, 1)
                    dve.wait_ge(s_pos2_done, s + 1)
                    nc.vector.tensor_tensor(over[:, :, :], pos[:, :, :], oh[:, :, :], ALU.mult).then_inc(s_pick_done, 1)
                    dve.wait_ge(s_pick_done, s + 1)
                    nc.vector.tensor_reduce(slotf[:, :], over[:, :, :], axis=AX.X, op=ALU.add).then_inc(s_slot_sum, 1)
                    dve.wait_ge(s_slot_sum, s + 1)
                    dve.wait_ge(s_prb_done, s + 1)
                    dve.wait_ge(scat[par], 16 * J * h)
                    nc.vector.tensor_copy(slots[:, par, :], slotf[:, :]).then_inc(s_slots_ready, 1)

                pair = all_steps(a_half, b_half)
                a_half(0, 0, 0, False)
                scale_of(0)
                pair(0)
                with dve.Fori(1, NS // 2) as i:
                    pair(i)
                b_half(NS - 1, 0, NS // 2, more=False)

            @block.tensor
            def _(pe):
                for c in range(KC):
                    for fc in range(KC):
                        ins = nc.tensor.transpose(psB[c][:, fc * P:(fc + 1) * P], g_sb[:, fc, c * P:(c + 1) * P],
                                                  ident[:, :])
                    ins.then_inc(s_gt_mm, 1)
                pe.wait_ge(s_gt_sb_done, KC)
                for ec in range(KC):
                    for cc in range(KC):
                        ins = nc.tensor.matmul(psM[ec][:, 0:P], wv_t[:, cc, ec * P:(ec + 1) * P],
                                               gt_sb[:, cc, ec * P:(ec + 1) * P], start=cc == 0, stop=cc == KC - 1)
                    ins.then_inc(s_ctx_mm, 1)
                pe.wait_ge(s_ctx_done, KC)
                for fc in range(KC):
                    nc.tensor.matmul(psX[fc][:, 0:D], ctx_t[:, fc, :], wp_t[:, fc, :], start=True, stop=True)\
                      .then_inc(s_mixw_mm, 1)
                pe.wait_ge(s_mixw_done, KC)
                pe.wait_ge(s_heads_set, 2)
                pe.wait_ge(s_c_in, 48)
                pe.wait_ge(s_c_set, 2)

                def a_half(s, par, h, last):
                    pe.wait_ge(s_q_ready, s + 1)
                    pe.wait_ge(s_qp_done, KC * s)
                    for j in range(J):
                        for c in range(KC):
                            ins = nc.tensor.matmul(psB[0][0:T, j * QH:(j + 1) * QH], q_cur[:, c, j * T:(j + 1) * T],
                                                   ksum[:, c, :], start=c == 0, stop=c == KC - 1)
                    ins.then_inc(s_d_mm, 1)
                    pe.wait_ge(s_den_done, s + 1)
                    nc.tensor.transpose(psB[1][0:J * QH, 0:T], den[:, :], ident[0:T, 0:T]).then_inc(s_dt_mm, 1)
                    pe.wait_ge(s_den_t, s + 1)
                    for c in range(KC):
                        for j in range(J):
                            ins = nc.tensor.matmul(psB[c][:, j * T:(j + 1) * T], spread[:, j, c, :], den_t[:, :],
                                                   start=True, stop=True)
                        ins.then_inc(s_b_mm, 1)
                    pe.wait_ge(s_qp_done, KC * (s + 1))
                    pe.wait_ge(s_x2_ready, 2 * s)
                    for j in range(J):
                        o = psM[j // 2][0:T, (j % 2) * D:(j % 2 + 1) * D]
                        nc.tensor.matmul(o, first[:, :], bias_p[:, :], start=True, stop=False)
                        for kc in range(KC):
                            ins = nc.tensor.matmul(o, qp[:, kc, j * T:(j + 1) * T], mix_w[:, kc, :],
                                                   start=False, stop=kc == KC - 1)
                        if j % 2:
                            ins.then_inc(s_mix_mm, 1)

                def b_half(s, par, h):
                    pe.wait_ge(s_xn2_ready, s + 1)
                    pe.wait_ge(s_x2t_ready, KC * s)
                    for c in range(KC):
                        for j in range(J):
                            ins = nc.tensor.transpose(psX[c][:, j * T:(j + 1) * T], xn2[:, j, c * P:(c + 1) * P],
                                                      ident[0:T, 0:T])
                    ins.then_inc(s_t2_done, 1)
                    pe.wait_ge(s_x2t_ready, KC * (s + 1))
                    pe.wait_ge(s_l_sub, s)
                    pe.wait_ge(s_l_eq, s)
                    for j in range(J):
                        o = psL[0:T, j * E:(j + 1) * E]
                        nc.tensor.matmul(o, first[:, :], bias_g[:, :], start=True, stop=False)
                        for kc in range(KC):
                            ins = nc.tensor.matmul(o, x2t[:, kc, j * T:(j + 1) * T], gw_sb[:, kc, :],
                                                   start=False, stop=kc == KC - 1)
                    ins.then_inc(s_lg_mm, 1)
                    pe.wait_ge(s_cum_done, J * (s + 1))
                    pe.wait_ge(s_seen_done, s)
                    pe.wait_ge(s_pos_done, s)
                    nc.tensor.matmul(psC[0:T, 0:E], before[0:T, :], cum[:, J, :], start=True, stop=False)
                    nc.tensor.matmul(psC[0:T, 0:E], ones[0:T, :], seen[:, :], start=False, stop=True)\
                      .then_inc(s_pos_mm, 1)

                pair = all_steps(a_half, b_half)
                a_half(0, 0, 0, False)
                pair(0)
                with pe.Fori(1, NS // 2) as i:
                    pair(i)
                b_half(NS - 1, 0, NS // 2)

        late.close()
        with ExitStack() as ph, nc.Block() as block:
            def sb3(name, shape, dt=F32):
                return sb_in(ph, name, shape, dt)

            NG = E * ST
            wraw = sb3("wraw", [P, KC * F + NF * D])
            w1_raw = wraw[:, 0:KC * F].rearrange("p (c f) -> p c f", c=KC)
            w2_raw = wraw[:, KC * F:].rearrange("p (c d) -> p c d", c=NF)
            w1_hi = sb3("w1_hi", [P, KC, F], F32R)
            w1_lo = sb3("w1_lo", [P, KC, F], F32R)
            w2_hi = sb3("w2_hi", [P, NF, D], F32R)
            w2_lo = sb3("w2_lo", [P, NF, D], F32R)
            b1_rows = sb3("b1_rows", [E * NF, P])
            b1_sb = sb3("b1_sb", [P, E * NF])
            b2_bc = sb3("b2_bc", [T3, E, D])
            xr = sb3("xr", [T3, ST, J, RW])
            st6 = sb3("st6c", [T3, J, 6])
            mv = sb3("mvc", [T3, J, 2])
            std = sb3("std", [T3, J])
            rstd = sb3("rstdc", [T3, J])
            nmr = sb3("nmrc", [T3, J])
            eps_c = sb3("eps_c", [P, 1])
            xn3 = sb3("xn3", [T3, J, D])
            xt_hi = sb3("xt3_hi", [P, 2, KC, TS3], F32R)
            xt_lo = sb3("xt3_lo", [P, 2, KC, TS3], F32R)
            hf = sb3("hf", [P, 4, TS3])
            h_hi = sb3("h_hi", [P, 4, TS3], F32R)
            h_lo = sb3("h_lo", [P, 4, TS3], F32R)
            yb = sb3("yb", [T3, J, D])
            ys = sb3("ys", [T3, J, D])
            top = sb3("top", [T3, J, D])
            bottom = sb3("bottom", [T3, J, D])
            yc = sb3("yc", [T3, J, D])
            fin = sb3("fin", [T3, J, D], I32)
            o_sb = sb3("o_sb", [T3, 2, J, D])
            tok_i = sb3("tok_i", [T3, 2, J], I32)

            psX = [ps_in(ph, f"psX3{c}", [P, 512]) for c in range(KC)]
            psH = [ps_in(ph, f"psH{c}", [P, 512]) for c in range(2)]
            psY = [ps_in(ph, f"psY{c}", [P, 512]) for c in range(J)]

            s_b_in = sem_in(ph, "s_b_in")
            s_w_in = sem_in(ph, "s_w_in")
            s_w1hi = sem_in(ph, "s_w1hi")
            s_w1lo = sem_in(ph, "s_w1lo")
            s_w2hi = sem_in(ph, "s_w2hi")
            s_w2lo = sem_in(ph, "s_w2lo")
            s_xr_in0 = sem_in(ph, "s_xr_in0")
            s_xr_in1 = sem_in(ph, "s_xr_in1")
            s_xr_in2 = sem_in(ph, "s_xr_in2")
            s_xr_in3 = sem_in(ph, "s_xr_in3")
            s_stats = sem_in(ph, "s_stats")
            s_aggr = sem_in(ph, "s_aggr")
            s_std_ready = sem_in(ph, "s_std_ready")
            s_rstd_ready = sem_in(ph, "s_rstd_ready")
            s_nmr_ready = sem_in(ph, "s_nmr_ready")
            s_xn_ready = sem_in(ph, "s_xn_ready")
            s_t_done = sem_in(ph, "s_t_done")
            s_hit = sem_in(ph, "s_hit")
            s_lot = sem_in(ph, "s_lot")
            s_h_mm = sem_in(ph, "s_h_mm")
            s_hf_ready = sem_in(ph, "s_hf_ready")
            s_hhi_ready = sem_in(ph, "s_hhi_ready")
            s_hlo_ready = sem_in(ph, "s_hlo_ready")
            s_w2_mm = sem_in(ph, "s_w2_mm")
            s_yb_done = sem_in(ph, "s_yb_done")
            s_ys_done = sem_in(ph, "s_ys_done")
            s_top_done = sem_in(ph, "s_top_done")
            s_fin_done = sem_in(ph, "s_fin_done")
            s_bottom_done = sem_in(ph, "s_bottom_done")
            s_yz_done = sem_in(ph, "s_yz_done")
            s_yp_done = sem_in(ph, "s_yp_done")
            s_o_ready = sem_in(ph, "s_o_ready")
            s_tok_ready = sem_in(ph, "s_tok_ready")
            s_sc0 = sem_in(ph, "s_sc0")
            s_sc1 = sem_in(ph, "s_sc1")
            s_eps_set = sem_in(ph, "s_eps_set")
            s_b1_t = sem_in(ph, "s_b1_t")
            s_b1_set = sem_in(ph, "s_b1_set")
            s_pool_passed = sem_in(ph, "s_pool_passed")
            s_dve_passed = sem_in(ph, "s_dve_passed")
            s_act_passed = sem_in(ph, "s_act_passed")
            xr_in, sc = [s_xr_in0, s_xr_in1, s_xr_in2, s_xr_in3], [s_sc0, s_sc1]

            LAG = 3

            def over_experts(eng, body):
                body(0, False)
                with eng.Fori(1, E - 1) as e:
                    body(e, False)
                body(E - 1, True)

            def is_first(e, st):
                return isinstance(e, int) and e == 0 and st == 0

            @block.sync
            def _(sp):
                def load_w(e):
                    w1e = w1[bass.ds(e, 1), :, :].rearrange("a (c p) f -> p (a c) f", p=P)
                    w2e = w2[bass.ds(e, 1), :, :].rearrange("a (c p) d -> p (a c) d", p=P)
                    sp.dma_start(w1_raw, w1e).then_inc(s_w_in, 16)
                    sp.dma_start(w2_raw, w2e).then_inc(s_w_in, 16)

                def load_x(g, slot):
                    sp.dma_start(xr[:, slot, :, :],
                                 rows[bass.ds(g * TS3, TS3), :].rearrange("(p j) w -> p j w", j=J)).then_inc(xr_in[slot], 16)

                load_x(0, 0)
                load_w(0)
                sp.dma_start(b1_rows[:, :], b1.rearrange("e (c p) -> (e c) p", p=P)).then_inc(s_b_in, 16)
                sp.dma_start(b2_bc[:, :, :], b2.rearrange("(a e) d -> a (e d)", a=1).partition_broadcast(T3)
                             ).then_inc(s_b_in, 16)
                for g in range(1, ST):
                    load_x(g, g)

                def body(e, last):
                    for st in range(ST):
                        g = ST * e + st
                        if st == 1 and not last:
                            for sem in (s_w1hi, s_w1lo, s_w2hi, s_w2lo):
                                sp.wait_ge(sem, NF * (e + 1))
                            load_w(e + 1)
                        if not is_first(e, st) and not (last and st > 0):
                            sp.wait_ge(s_o_ready, g)
                            sp.wait_ge(s_tok_ready, g)
                            load_x(g + ST - 1, (st - 1) % ST)

                over_experts(sp, body)
                sp.wait_ge(sc[0], 16 * J * (NG // 2))
                sp.wait_ge(sc[1], 16 * J * (NG // 2))

            @block.gpsimd
            def _(pool):
                def scatter(n, par):
                    pool.wait_ge(s_o_ready, n)
                    pool.wait_ge(s_tok_ready, n)
                    passed(pool, s_pool_passed)
                    for j in range(J):
                        pool.indirect_dma_start(out=out, in_=o_sb[:, par, j, :], in_offset=None,
                                                out_offset=bass.IndirectOffsetOnAxis(ap=tok_i[:, par, j:j + 1], axis=0),
                                                bounds_check=N - 1, oob_is_err=False).then_inc(sc[par], 16)

                def body(e, last):
                    for st in range(ST):
                        if not is_first(e, st):
                            scatter(ST * e + st, 1 - st % 2)

                over_experts(pool, body)
                scatter(NG, 1)

            @block.scalar
            def _(act):
                def split_w1(f, n):
                    act.wait_ge(s_w_in, 32 * n)
                    act.activation(w1_hi[:, :, f * P:(f + 1) * P], w1_raw[:, :, f * P:(f + 1) * P], ACT.Copy)\
                       .then_inc(s_w1hi, 1)

                def split_w2(f, n):
                    act.wait_ge(s_w_in, 32 * n)
                    act.activation(w2_hi[:, f, :], w2_raw[:, f, :], ACT.Copy).then_inc(s_w2hi, 1)

                def normal(g, slot):
                    act.wait_ge(s_aggr, J * (g + 1))
                    act.wait_ge(s_rstd_ready, g)
                    act.activation(std[:, :], mv[:, :, 1], ACT.Sqrt, bias=eps_c[0:T3, :]).then_inc(s_std_ready, 1)
                    act.wait_ge(s_nmr_ready, g + 1)
                    act.wait_ge(s_t_done, g)
                    for j in range(J):
                        ins = act.activation(xn3[:, j, :], xr[:, slot, j, 0:D], ACT.Identity, bias=nmr[:, j:j + 1],
                                             scale=rstd[:, j:j + 1])
                    ins.then_inc(s_xn_ready, 1)

                def high_t(g, par):
                    act.wait_ge(s_t_done, g + 1)
                    for c in range(KC):
                        act.activation(xt_hi[:, par, c, :], psX[c][:, 0:TS3], ACT.Copy).then_inc(s_hit, 1)

                act.wait_ge(s_eps_set, 1)
                normal(0, 0)
                high_t(0, 0)
                for f in range(NF):
                    split_w1(f, 1)
                    split_w2(f, 1)
                act.wait_ge(s_b1_t, 1)
                act.activation(b1_sb[:, :], psY[0][:, 0:E * NF], ACT.Copy).then_inc(s_b1_set, 1)
                act.wait_ge(s_b1_set, 1)

                def times_prob(n, slot):
                    act.wait_ge(s_yp_done, n - 1)
                    act.wait_ge(s_top_done, n - 1)
                    act.wait_ge(s_bottom_done, n - 1)
                    act.wait_ge(s_fin_done, n - 1)
                    act.wait_ge(s_yb_done, J * n)
                    for j in range(J):
                        ins = act.activation(ys[:, j, :], yb[:, j, :], ACT.Copy, scale=xr[:, slot, j, D:D + 1])
                    ins.then_inc(s_ys_done, 1)

                def body(e, last):
                    for st in range(ST):
                        g, par = ST * e + st, st % 2
                        end = last and st == ST - 1
                        for f in range(NF):
                            act.wait_ge(s_h_mm, NF * g + f + 1)
                            act.wait_ge(s_hlo_ready, NF * g + f - 3 if f >= 4 else NF * g)
                            act.wait_ge(s_w2_mm, NF * g + f - 3 if f >= 4 else NF * g)
                            passed(act, s_act_passed)
                            act.activation(h_hi[:, f % 4, :], psH[f % 2][:, 0:TS3], ACT.Relu,
                                           bias=b1_sb[:, bass.ds(e * NF + f, 1)]).then_inc(s_hhi_ready, 1)
                            act.activation(hf[:, f % 4, :], psH[f % 2][:, 0:TS3], ACT.Relu,
                                           bias=b1_sb[:, bass.ds(e * NF + f, 1)]).then_inc(s_hf_ready, 1)
                            if f == 0 and not is_first(e, st):
                                times_prob(g, (st - 1) % ST)
                            if f == 2 and not end:
                                normal(g + 1, (st + 1) % ST)
                            if f == 6 and not end:
                                high_t(g + 1, 1 - par)
                            if st == ST - 1 and not last:
                                split_w1(f, e + 2)
                                if f >= LAG:
                                    act.wait_ge(s_w2_mm, NF * g + f - LAG + 1)
                                    split_w2(f - LAG, e + 2)
                            if st == 0 and f < LAG and not is_first(e, 0):
                                act.wait_ge(s_w2_mm, NF * g - LAG + f + 1)
                                split_w2(NF - LAG + f, e + 1)

                over_experts(act, body)
                times_prob(NG, ST - 1)

            @block.vector
            def _(dve):
                nc.vector.memset(eps_c[:, :], EPS).then_inc(s_eps_set, 1)

                def split_w1(f, n):
                    dve.wait_ge(s_w1hi, NF * (n - 1) + f + 1)
                    nc.vector.tensor_tensor(w1_lo[:, :, f * P:(f + 1) * P], w1_raw[:, :, f * P:(f + 1) * P],
                                            w1_hi[:, :, f * P:(f + 1) * P].bitcast(F32), ALU.subtract).then_inc(s_w1lo, 1)

                def split_w2(f, n):
                    dve.wait_ge(s_w2hi, NF * (n - 1) + f + 1)
                    nc.vector.tensor_tensor(w2_lo[:, f, :], w2_raw[:, f, :], w2_hi[:, f, :].bitcast(F32),
                                            ALU.subtract).then_inc(s_w2lo, 1)

                def stats(g, slot, n):
                    dve.wait_ge(xr_in[slot], 16 * n)
                    for j in range(J):
                        nc.vector.bn_stats(st6[:, j, :], xr[:, slot, j, 0:D]).then_inc(s_stats, 1)
                    dve.wait_ge(s_xn_ready, g)
                    dve.wait_ge(s_stats, J * (g + 1))
                    passed(dve, s_dve_passed)
                    for j in range(J):
                        nc.vector.bn_aggr(mv[:, j, :], st6[:, j, :]).then_inc(s_aggr, 1)

                def scales(g):
                    dve.wait_ge(s_std_ready, g + 1)
                    nc.vector.reciprocal(rstd[:, :], std[:, :]).then_inc(s_rstd_ready, 1)
                    dve.wait_ge(s_rstd_ready, g + 1)
                    nc.vector.scalar_tensor_tensor(nmr[:, :], mv[:, :, 0], -1.0, rstd[:, :], ALU.mult, ALU.mult)\
                      .then_inc(s_nmr_ready, 1)

                def low_t(g, par):
                    for c in range(KC):
                        dve.wait_ge(s_hit, KC * g + c + 1)
                        nc.vector.tensor_tensor(xt_lo[:, par, c, :], psX[c][:, 0:TS3], xt_hi[:, par, c, :].bitcast(F32),
                                                ALU.subtract).then_inc(s_lot, 1)

                stats(0, 0, 1)
                scales(0)
                low_t(0, 0)
                for f in range(NF):
                    split_w1(f, 1)
                    split_w2(f, 1)
                dve.wait_ge(s_b_in, 32)
                dve.wait_ge(s_b1_set, 1)

                def limits(n):
                    dve.wait_ge(s_ys_done, n)
                    nc.vector.tensor_scalar(top[:, :, :], ys[:, :, :], 1e4, 1e4, ALU.is_ge, ALU.mult)\
                      .then_inc(s_top_done, 1)
                    nc.vector.tensor_scalar(bottom[:, :, :], ys[:, :, :], -1e4, 1e4, ALU.is_le, ALU.mult)\
                      .then_inc(s_bottom_done, 1)

                def finite(n):
                    nc.vector.tensor_scalar(fin[:, :, :], ys[:, :, :], 0.0, 0.0, ALU.mult, ALU.is_equal)\
                      .then_inc(s_fin_done, 1)
                    dve.wait_ge(s_top_done, n)
                    dve.wait_ge(s_bottom_done, n)
                    dve.wait_ge(s_o_ready, n - 1)
                    nc.vector.tensor_tensor(yc[:, :, :], top[:, :, :], bottom[:, :, :], ALU.subtract).then_inc(s_yz_done, 1)

                def keep_finite(n):
                    dve.wait_ge(s_yz_done, n)
                    dve.wait_ge(s_fin_done, n)
                    passed(dve, s_dve_passed)
                    nc.vector.copy_predicated(yc[:, :, :], fin[:, :, :], ys[:, :, :]).then_inc(s_yp_done, 1)

                def sums(n, par, slot, used):
                    dve.wait_ge(sc[par], 16 * J * used)
                    nc.vector.tensor_copy(tok_i[:, par, :], xr[:, slot, :, D + 1]).then_inc(s_tok_ready, 1)
                    dve.wait_ge(s_yp_done, n)
                    nc.vector.tensor_tensor(o_sb[:, par, :, :], yc[:, :, :], xr[:, slot, :, 0:D], ALU.add)\
                      .then_inc(s_o_ready, 1)

                def body(e, last):
                    for st in range(ST):
                        g, par = ST * e + st, st % 2
                        end = last and st == ST - 1
                        after = not is_first(e, st)
                        for f in range(NF):
                            dve.wait_ge(s_hhi_ready, NF * g + f + 1)
                            dve.wait_ge(s_hf_ready, NF * g + f + 1)
                            dve.wait_ge(s_w2_mm, NF * g + f - 3 if f >= 4 else NF * g)
                            nc.vector.tensor_tensor(h_lo[:, f % 4, :], hf[:, f % 4, :], h_hi[:, f % 4, :].bitcast(F32),
                                                    ALU.subtract).then_inc(s_hlo_ready, 1)
                            if f == 0 and not end:
                                stats(g + 1, (st + 1) % ST, e + 1 + (st + 1) // ST)
                            if f == 1 and not end:
                                scales(g + 1)
                            if f == 2 and after:
                                limits(g)
                            if f == 3 and after:
                                finite(g)
                            if f == 4 and after:
                                keep_finite(g)
                            if f == 5 and after:
                                sums(g, 1 - par, (st - 1) % ST, e * (ST // 2) + (st - 1) // 2)
                            if f == 6 and not end:
                                low_t(g + 1, 1 - par)
                            if st == ST - 1 and not last:
                                split_w1(f, e + 2)
                                if f >= LAG:
                                    split_w2(f - LAG, e + 2)
                            if st == 0 and f < LAG and not is_first(e, 0):
                                split_w2(NF - LAG + f, e + 1)
                        dve.wait_ge(s_ys_done, g)
                        dve.wait_ge(s_w2_mm, NF * (g + 1))
                        for j in range(J):
                            nc.vector.tensor_tensor(yb[:, j, :], psY[j][0:T3, 0:D],
                                                    b2_bc[:, bass.ds(e, 1), :].rearrange("p a d -> p (a d)"),
                                                    ALU.add).then_inc(s_yb_done, 1)

                over_experts(dve, body)
                limits(NG)
                finite(NG)
                keep_finite(NG)
                sums(NG, 1, ST - 1, NG // 2 - 1)

            @block.tensor
            def _(pe):
                def transposes(g):
                    pe.wait_ge(s_xn_ready, g + 1)
                    pe.wait_ge(s_hit, KC * g)
                    pe.wait_ge(s_lot, KC * g)
                    for c in range(KC):
                        for j in range(J):
                            ins = nc.tensor.transpose(psX[c][:, j * T3:(j + 1) * T3], xn3[:, j, c * P:(c + 1) * P],
                                                      ident[0:T3, 0:T3])
                    ins.then_inc(s_t_done, 1)

                pe.wait_ge(s_b_in, 32)
                nc.tensor.transpose(psY[0][:, 0:E * NF], b1_rows[:, :], ident[0:E * NF, 0:E * NF]).then_inc(s_b1_t, 1)
                transposes(0)
                pe.wait_ge(s_b1_set, 1)

                def body(e, last):
                    for st in range(ST):
                        g, par = ST * e + st, st % 2
                        for slot in range(NF + 2):
                            if slot < NF:
                                f = slot
                                if f == 0:
                                    pe.wait_ge(s_hit, KC * (g + 1))
                                    pe.wait_ge(s_lot, KC * (g + 1))
                                if st == 0:
                                    pe.wait_ge(s_w1hi, NF * e + f + 1)
                                    pe.wait_ge(s_w1lo, NF * e + f + 1)
                                pe.wait_ge(s_hf_ready, NF * g + f - 1 if f >= 2 else NF * g)
                                pe.wait_ge(s_hhi_ready, NF * g + f - 1 if f >= 2 else NF * g)
                                n = 0
                                for w, xt in ((w1_hi, xt_hi), (w1_lo, xt_hi), (w1_hi, xt_lo)):
                                    for kc in range(KC):
                                        ins = nc.tensor.matmul(psH[f % 2][:, 0:TS3], w[:, kc, f * P:(f + 1) * P],
                                                               xt[:, par, kc, :], start=n == 0, stop=n == 3 * KC - 1)
                                        n += 1
                                ins.then_inc(s_h_mm, 1)
                            if slot == 5 and not (last and st == ST - 1):
                                transposes(g + 1)
                            if slot >= 2:
                                f = slot - 2
                                if f == 0:
                                    pe.wait_ge(s_yb_done, J * g)
                                if st == 0:
                                    pe.wait_ge(s_w2hi, NF * e + f + 1)
                                    pe.wait_ge(s_w2lo, NF * e + f + 1)
                                pe.wait_ge(s_hhi_ready, NF * g + f + 1)
                                pe.wait_ge(s_hlo_ready, NF * g + f + 1)
                                for j in range(J):
                                    for n, (hh, w) in enumerate(((h_hi, w2_hi), (h_hi, w2_lo), (h_lo, w2_hi))):
                                        ins = nc.tensor.matmul(psY[j][0:T3, 0:D], hh[:, f % 4, j * T3:(j + 1) * T3],
                                                               w[:, f, :], start=f == 0 and n == 0,
                                                               stop=f == NF - 1 and n == 2)
                                ins.then_inc(s_w2_mm, 1)

                over_experts(pe, body)

_INS = ["x", "src", "dst", "L0_gnn_weight", "L0_gnn_attn_l", "L0_gnn_attn_r", "L0_mix_Wq", "L0_mix_Wkv",
        "L0_mix_Wproj", "L0_mix_bproj", "L0_ffn_gate_w", "L0_ffn_gate_b", "L0_ffn_w1", "L0_ffn_b1",
        "L0_ffn_w2", "L0_ffn_b2"]


def kernel(**inputs):
    import numpy as _np
    import concourse.bacc as _bacc
    from concourse import mybir as _mybir
    from concourse.bass_utils import run_bass_kernel_spmd as _run

    nc = _bacc.Bacc("TRN2", target_bir_lowering=False, num_devices=1)
    arrays, args = {}, []
    for name in _INS:
        a = _np.ascontiguousarray(inputs[name])
        arrays[f"in_{name}"] = a
        args.append(nc.dram_tensor(f"in_{name}", a.shape, _mybir.dt.from_np(a.dtype), kind="ExternalInput").ap())
    out = nc.dram_tensor("out_0", arrays["in_x"].shape, _mybir.dt.float32, kind="ExternalOutput").ap()
    gps_layer(nc, *args, out)
    r = _run(nc, [arrays], core_ids=[0])
    return r.results[0]["out_0"]
```

```python
from contextlib import ExitStack

import concourse.bass as bass
from concourse import mybir

ALU = mybir.AluOpType
ACT = mybir.ActivationFunctionType
F32 = mybir.dt.float32
F32R = mybir.dt.float32r
I32 = mybir.dt.int32
AX = mybir.AxisListType

P = 128
EPS = 1e-5
FAR = 60000.0
BIG = 1000000.0


def passed(eng, sem):
    eng.sem_inc(sem)


def over_tiles(eng, step, n):
    step(0, 0, 0, False)
    step(1, 1, 0, False)
    with eng.Fori(1, n // 2) as i:
        step(2 * i, 0, i, False)
        step(2 * i + 1, 1, i, False)
    step(n - 1, 0, n // 2, True)


def gps_layer(nc, x, src, dst, gnn_w, attn_l, attn_r, wq, wkv, wproj, bproj,
              gate_w, gate_b, w1, b1, w2, b2, out):
    N, D = x.shape
    H, DH = attn_l.shape
    E, _, F = w1.shape
    QH = 8
    QD = D // QH
    KC = D // P
    T, J = 125, 4
    TS = T * J
    NS = N // TS
    assert NS * TS == N and NS % 2 == 1
    CAP = -(-5 * N // (4 * E))
    T3 = 124
    TS3 = T3 * J
    ST = -(-CAP // TS3)
    ROWS = ST * TS3
    NF = F // P
    XW = D + 2 * H
    TW = D + H
    RW = D + 4
    GW = D + 2

    table = nc.dram_tensor("graph_table", [N, TW], F32, kind="Internal").ap()
    table_l = nc.dram_tensor("alpha_l_table", [N, H], F32, kind="Internal").ap()
    rows = nc.dram_tensor("expert_rows", [E * ROWS, RW], F32, kind="Internal").ap()

    base = ExitStack()

    def sb_in(stack, name, shape, dt=F32):
        return stack.enter_context(nc.sbuf_tensor(name, shape, dt))

    def ps_in(stack, name, shape):
        return stack.enter_context(nc.psum_tensor(name, shape, F32))

    def sem_in(stack, name):
        return stack.enter_context(nc.semaphore(name))

    def tok(t, s, w):
        return t[bass.ds(s * TS, TS), :].rearrange("(p j) w -> p j w", j=J)

    def wide(a, n):
        dims = list(a.shape)
        names = "pjh"[:len(dims)]
        spread = a.rearrange(f"{' '.join(names[:-1])} ({names[-1]} z) -> {' '.join(names)} z", z=1)
        return spread.broadcast_to(dims + [n])

    with base:
        def sb(name, shape, dt=F32):
            return sb_in(base, name, shape, dt)

        ident = sb("ident", [P, P])
        mhalf = sb("mhalf", [P, J])
        x_sb = sb("x_sb", [T, 2, J, D])
        wv_t = sb("wv_t", [P, KC, D])
        wp_t = sb("wp_t", [P, KC, D])
        g_sb = sb("g_sb", [P, KC, GW])

        s_pool_passed = sem_in(base, "s_pool_passed")
        s_dve_passed = sem_in(base, "s_dve_passed")
        s_act_passed = sem_in(base, "s_act_passed")
        late = ExitStack()
        q_all = sb_in(late, "q_all", [P, KC, N])

        with ExitStack() as ph, nc.Block() as block:
            def sb1(name, shape, dt=F32):
                return sb_in(ph, name, shape, dt)

            wqkvp = q_all[:, 0, N - 4 * KC * D:N].rearrange("p (n c i) -> p n c i", n=4, c=KC)
            attn_bc = q_all[:, 1, N - 2 * D:N].rearrange("p (n i) -> p n i", n=2)
            wprod = q_all[:, 1, N - 4 * D:N - 2 * D].rearrange("p (c i) -> p c i", c=KC)
            wx_f = sb1("wx_f", [P, KC, XW])
            wx_hi = sb1("wx_hi", [P, KC, XW], F32R)
            wx_lo = sb1("wx_lo", [P, KC, XW], F32R)
            wq_hi = sb1("wq_hi", [P, KC, D], F32R)
            wq_lo = sb1("wq_lo", [P, KC, D], F32R)
            wk_hi = sb1("wk_hi", [P, KC, D], F32R)
            wk_lo = sb1("wk_lo", [P, KC, D], F32R)
            empty = sb1("empty", [P, J, RW])
            st6 = sb1("st6", [T, J, 6])
            mv = sb1("mv", [T, J, 2])
            rstd = sb1("rstd", [T, J])
            xn = sb1("xn", [T, J, D])
            xn_hi = sb1("xn_hi", [T, 2, J, GW], F32R)
            xn_lo = sb1("xn_lo", [T, 2, J, GW], F32R)
            xt_hi = sb1("xt_hi", [P, KC, TS], F32R)
            xt_lo = sb1("xt_lo", [P, KC, TS], F32R)
            eq = sb1("eq", [P, KC, TS])
            ek = sb1("ek", [T, 2, 2, D])
            kf = sb1("kf", [T, 2, 2, D])
            k_hi = sb1("k_hi", [T, J, D], F32R)
            k_lo = sb1("k_lo", [T, J, D], F32R)
            tab_sb = sb1("tab_sb", [T, 2, J, XW])

            psT = [ps_in(ph, f"psT{c}", [P, 512]) for c in range(KC)]
            psG = [ps_in(ph, f"psG{c}", [P, 512]) for c in range(KC)]
            psR = [ps_in(ph, f"psR{c}", [P, 512]) for c in range(4)]

            s_w_in = sem_in(ph, "s_w_in")
            s_w_t = sem_in(ph, "s_w_t")
            s_ident0 = sem_in(ph, "s_ident0")
            s_ident1 = sem_in(ph, "s_ident1")
            s_const1 = sem_in(ph, "s_const1")
            s_wa = sem_in(ph, "s_wa")
            s_wsplit = sem_in(ph, "s_wsplit")
            s_wsplit_lo = sem_in(ph, "s_wsplit_lo")
            s_empty_set = sem_in(ph, "s_empty_set")
            s_empty_out = sem_in(ph, "s_empty_out")
            s_var_ready = sem_in(ph, "s_var_ready")
            s_mhalf_set = sem_in(ph, "s_mhalf_set")
            s_x_in0 = sem_in(ph, "s_x_in0")
            s_x_in1 = sem_in(ph, "s_x_in1")
            s_stats = sem_in(ph, "s_stats")
            s_aggr = sem_in(ph, "s_aggr")
            s_rstd_ready = sem_in(ph, "s_rstd_ready")
            s_xn_ready = sem_in(ph, "s_xn_ready")
            s_xnhi_ready = sem_in(ph, "s_xnhi_ready")
            s_xnlo_ready = sem_in(ph, "s_xnlo_ready")
            s_t_done = sem_in(ph, "s_t_done")
            s_hit_done = sem_in(ph, "s_hit_done")
            s_lot_done = sem_in(ph, "s_lot_done")
            s_q_mm = sem_in(ph, "s_q_mm")
            s_k_mm = sem_in(ph, "s_k_mm")
            s_xt_mm = sem_in(ph, "s_xt_mm")
            s_g_done = sem_in(ph, "s_g_done")
            s_eq_exp = sem_in(ph, "s_eq_exp")
            s_ek_exp = sem_in(ph, "s_ek_exp")
            s_eq_min = sem_in(ph, "s_eq_min")
            s_ek_min = sem_in(ph, "s_ek_min")
            s_q_done = sem_in(ph, "s_q_done")
            s_k_done = sem_in(ph, "s_k_done")
            s_khi_done = sem_in(ph, "s_khi_done")
            s_klo_done = sem_in(ph, "s_klo_done")
            s_tab_ready = sem_in(ph, "s_tab_ready")
            s_tab_out0 = sem_in(ph, "s_tab_out0")
            s_tab_out1 = sem_in(ph, "s_tab_out1")
            s_g_out = sem_in(ph, "s_g_out")
            x_in = [s_x_in0, s_x_in1]
            tab_out = [s_tab_out0, s_tab_out1]

            @block.sync
            def _(sp):
                def load_x(s, par):
                    sp.dma_start(x_sb[:, par, :, :], tok(x, s, D)).then_inc(x_in[par], 16)

                load_x(0, 0)
                for n, w in enumerate((wq, wkv[0:D, :], wkv[D:2 * D, :], wproj)):
                    sp.dma_start(wqkvp[:, n, :, :], w.rearrange("(c p) i -> p c i", p=P)).then_inc(s_w_in, 16)
                sp.dma_start(wx_f[:, :, 0:D], gnn_w.rearrange("(c p) o -> p c o", p=P)).then_inc(s_w_in, 16)
                for n, a in enumerate((attn_r, attn_l)):
                    sp.dma_start(attn_bc[:, n, :], a.rearrange("(a h) d -> a (h d)", a=1).partition_broadcast(P))\
                      .then_inc(s_w_in, 16)
                load_x(1, 1)

                def step(s, par, h, last, load):
                    if load:
                        sp.wait_ge(s_xn_ready, s + 1)
                        load_x(s + 2, par)
                    sp.wait_ge(s_tab_ready, J * (s + 1))
                    sp.dma_start(tok(table, s, TW), tab_sb[:, par, :, 0:TW]).then_inc(tab_out[par], 16)
                    sp.dma_start(tok(table_l, s, H), tab_sb[:, par, :, TW:XW]).then_inc(tab_out[par], 16)

                step(0, 0, 0, False, True)
                step(1, 1, 0, False, True)
                with sp.Fori(1, (NS - 3) // 2) as i:
                    step(2 * i, 0, i, False, True)
                    step(2 * i + 1, 1, i, False, True)
                step(NS - 3, 0, (NS - 3) // 2, False, True)
                step(NS - 2, 1, 0, False, False)
                step(NS - 1, 0, 0, True, False)
                sp.wait_ge(tab_out[0], 32 * (NS // 2 + 1))
                sp.wait_ge(tab_out[1], 32 * (NS // 2))
                sp.wait_ge(s_empty_out, 16 * (E * ROWS // (P * J)))

            @block.gpsimd
            def _(pool):
                nc.gpsimd.memset(ident[:, :], 0.0).then_inc(s_ident0, 1)
                pool.wait_ge(s_ident0, 1)
                nc.gpsimd.affine_select(out=ident[:, :], in_=ident[:, :], compare_op=ALU.not_equal, fill=1.0,
                                        base=0, pattern=[[-1, P]], channel_multiplier=1).then_inc(s_ident1, 1)
                nc.gpsimd.memset(empty[:, :, :], 0.0).then_inc(s_empty_set, 1)
                pool.wait_ge(s_empty_set, 1)
                nc.gpsimd.memset(empty[:, :, D + 1:D + 2], FAR).then_inc(s_empty_set, 1)
                pool.wait_ge(s_empty_set, 2)
                groups = rows.rearrange("(g p j) w -> g p (j w)", p=P, j=J)

                def clear(g):
                    pool.dma_start(groups[bass.ds(g, 1), :, :].rearrange("a p w -> (a p) w"),
                                   empty[:, :, :].rearrange("p j w -> p (j w)")).then_inc(s_empty_out, 16)

                def rstd_of(s):
                    pool.wait_ge(s_aggr, J * (s + 1))
                    pool.wait_ge(s_xn_ready, s)
                    passed(pool, s_pool_passed)
                    nc.gpsimd.tensor_scalar(rstd[:, :], mv[:, :, 1], EPS, None, ALU.add).then_inc(s_var_ready, 1)
                    pool.wait_ge(s_var_ready, s + 1)
                    nc.gpsimd.tensor_tensor(rstd[:, :], rstd[:, :], mhalf[0:T, :], ALU.pow).then_inc(s_rstd_ready, 1)

                nc.gpsimd.memset(mhalf[:, :], -0.5).then_inc(s_mhalf_set, 1)
                pool.wait_ge(s_mhalf_set, 1)
                for s in range(3):
                    rstd_of(s)
                    clear(s)
                with pool.Fori(3, NS) as s:
                    rstd_of(s)
                    clear(s)
                with pool.Fori(NS, E * ROWS // (P * J)) as s:
                    clear(s)

            @block.scalar
            def _(act):
                def xn_high(s, par):
                    act.wait_ge(s_xn_ready, s + 1)
                    act.activation(xn_hi[:, par, :, 0:D], xn[:, :, :], ACT.Copy).then_inc(s_xnhi_ready, 1)

                act.wait_ge(s_const1, 1)
                xn_high(0, 0)
                for n, o in enumerate((wq_hi, wk_hi, wv_t, wp_t)):
                    act.wait_ge(s_w_t, n + 1)
                    act.activation(o[:, :, :], psR[n][:, :].rearrange("p (c o) -> p c o", c=KC), ACT.Copy)\
                       .then_inc(s_wsplit, 1)
                act.wait_ge(s_wa, 4)
                act.activation(wx_hi[:, :, :], wx_f[:, :, :], ACT.Copy).then_inc(s_wsplit, 1)


                def step(s, par, h, last):
                    act.wait_ge(s_t_done, s + 1)
                    for c in range(KC):
                        act.activation(xt_hi[:, c, :], psT[c][:, 0:TS], ACT.Copy).then_inc(s_hit_done, 1)
                    for c in range(KC):
                        act.wait_ge(s_q_mm, KC * s + c + 1)
                        act.wait_ge(s_q_done, KC * s)
                        act.activation(eq[:, c, :], psR[c][:, 0:TS], ACT.Exp).then_inc(s_eq_exp, 1)
                    for n in range(2):
                        act.wait_ge(s_k_mm, 2 * s + n + 1)
                        act.wait_ge(s_k_done, 2 * s)
                        act.activation(ek[:, n, :, :], psR[2 + n][0:T, :].rearrange("p (j o) -> p j o", j=2),
                                       ACT.Exp).then_inc(s_ek_exp, 1)
                    for n in range(2):
                        act.wait_ge(s_k_done, 2 * s + n + 1)
                        act.wait_ge(s_g_done, s)
                        act.activation(k_hi[:, 2 * n:2 * n + 2, :], kf[:, n, :, :], ACT.Copy).then_inc(s_khi_done, 1)
                    if not last:
                        act.wait_ge(s_g_done, s)
                        xn_high(s + 1, 1 - par)
                    for j in range(J):
                        act.wait_ge(s_xt_mm, J * s + j + 1)
                        if j == 0:
                            act.wait_ge(tab_out[par], 32 * h)
                        act.activation(tab_sb[:, par, j, :], psR[j][0:T, 0:XW], ACT.Copy).then_inc(s_tab_ready, 1)

                over_tiles(act, step, NS)

            @block.vector
            def _(dve):
                for par in range(2):
                    nc.vector.memset(xn_lo[:, par, :, D:GW].bitcast(F32), 0.0)
                    nc.vector.memset(xn_hi[:, par, :, D + 1:GW].bitcast(F32), 0.0)
                    ins = nc.vector.memset(xn_hi[:, par, :, D:D + 1].bitcast(F32), 1.0)
                ins.then_inc(s_const1, 1)

                def stats(s, par, h):
                    dve.wait_ge(x_in[par], 16 * (h + 1))
                    for j in range(J):
                        nc.vector.bn_stats(st6[:, j, :], x_sb[:, par, j, :]).then_inc(s_stats, 1)
                    dve.wait_ge(s_rstd_ready, s)
                    dve.wait_ge(s_stats, J * (s + 1))
                    passed(dve, s_dve_passed)
                    for j in range(J):
                        nc.vector.bn_aggr(mv[:, j, :], st6[:, j, :]).then_inc(s_aggr, 1)

                def norm(s, par):
                    dve.wait_ge(s_rstd_ready, s + 1)
                    dve.wait_ge(s_t_done, s)
                    dve.wait_ge(s_xnhi_ready, s)
                    for j in range(J):
                        ins = nc.vector.tensor_scalar(xn[:, j, :], x_sb[:, par, j, :], mv[:, j, 0:1],
                                                      rstd[:, j:j + 1], ALU.subtract, ALU.mult)
                    ins.then_inc(s_xn_ready, 1)

                def xn_low(s, par):
                    dve.wait_ge(s_xnhi_ready, s + 1)
                    nc.vector.tensor_tensor(xn_lo[:, par, :, 0:D], xn[:, :, :],
                                            xn_hi[:, par, :, 0:D].bitcast(F32), ALU.subtract).then_inc(s_xnlo_ready, 1)

                stats(0, 0, 0)
                norm(0, 0)
                xn_low(0, 0)
                dve.wait_ge(s_w_in, 16 * 7)
                for n in range(2):
                    dve.wait_ge(s_wa, 2 * n)
                    nc.vector.tensor_tensor(wprod[:, :, :], wx_f[:, :, 0:D],
                                            attn_bc[:, n:n + 1, :].broadcast_to([P, KC, D]), ALU.mult).then_inc(s_wa, 1)
                    dve.wait_ge(s_wa, 2 * n + 1)
                    nc.vector.tensor_reduce(wx_f[:, :, D + n * H:D + (n + 1) * H],
                                            wprod[:, :, :].rearrange("p c (h d) -> p c h d", h=H),
                                            axis=AX.X, op=ALU.add).then_inc(s_wa, 1)
                for n, (hi, lo) in enumerate(((wq_hi, wq_lo), (wk_hi, wk_lo))):
                    dve.wait_ge(s_wsplit, n + 1)
                    nc.vector.tensor_tensor(lo[:, :, :], psR[n][:, :].rearrange("p (c o) -> p c o", c=KC),
                                            hi[:, :, :].bitcast(F32), ALU.subtract).then_inc(s_wsplit_lo, 1)
                dve.wait_ge(s_wsplit, 5)
                nc.vector.tensor_tensor(wx_lo[:, :, :], wx_f[:, :, :], wx_hi[:, :, :].bitcast(F32),
                                        ALU.subtract).then_inc(s_wsplit_lo, 1)

                def step(s, par, h, last):
                    for c in range(KC):
                        dve.wait_ge(s_hit_done, KC * s + c + 1)
                        nc.vector.tensor_tensor(xt_lo[:, c, :], psT[c][:, 0:TS], xt_hi[:, c, :].bitcast(F32),
                                                ALU.subtract).then_inc(s_lot_done, 1)
                    if not last:
                        stats(s + 1, 1 - par, h + par)
                    for c in range(KC):
                        dve.wait_ge(s_eq_exp, KC * s + c + 1)
                        nc.vector.tensor_scalar(eq[:, c, :], eq[:, c, :], 1.0, None, ALU.min).then_inc(s_eq_min, 1)
                        dve.wait_ge(s_eq_min, KC * s + c + 1)
                        nc.vector.scalar_tensor_tensor(q_all[:, c, bass.ds(s * TS, TS)], psR[c][:, 0:TS], 1.0,
                                                       eq[:, c, :], ALU.add, ALU.max).then_inc(s_q_done, 1)
                    for n in range(2):
                        dve.wait_ge(s_ek_exp, 2 * s + n + 1)
                        nc.vector.tensor_scalar(ek[:, n, :, :], ek[:, n, :, :], 1.0, None, ALU.min).then_inc(s_ek_min, 1)
                        dve.wait_ge(s_ek_min, 2 * s + n + 1)
                        dve.wait_ge(s_khi_done, 2 * s)
                        dve.wait_ge(s_klo_done, 2 * s)
                        nc.vector.scalar_tensor_tensor(kf[:, n, :, :],
                                                       psR[2 + n][0:T, :].rearrange("p (j o) -> p j o", j=2), 1.0,
                                                       ek[:, n, :, :], ALU.add, ALU.max).then_inc(s_k_done, 1)
                    if not last:
                        norm(s + 1, 1 - par)
                    for n in range(2):
                        dve.wait_ge(s_khi_done, 2 * s + n + 1)
                        nc.vector.tensor_tensor(k_lo[:, 2 * n:2 * n + 2, :], kf[:, n, :, :],
                                                k_hi[:, 2 * n:2 * n + 2, :].bitcast(F32),
                                                ALU.subtract).then_inc(s_klo_done, 1)
                    if not last:
                        dve.wait_ge(s_g_done, s)
                        xn_low(s + 1, 1 - par)

                over_tiles(dve, step, NS)
                dve.wait_ge(s_g_done, NS)
                for c in range(KC):
                    nc.vector.tensor_copy(g_sb[:, c, :], psG[c][:, 0:GW]).then_inc(s_g_out, 1)

            @block.tensor
            def _(pe):
                pe.wait_ge(s_ident1, 1)
                def transposes(s):
                    pe.wait_ge(s_xn_ready, s + 1)
                    pe.wait_ge(s_hit_done, KC * s)
                    pe.wait_ge(s_lot_done, KC * s)
                    for c in range(KC):
                        for j in range(J):
                            ins = nc.tensor.transpose(psT[c][:, j * T:(j + 1) * T], xn[:, j, c * P:(c + 1) * P],
                                                      ident[0:T, 0:T])
                    ins.then_inc(s_t_done, 1)

                transposes(0)
                pe.wait_ge(s_w_in, 16 * 7)
                for n in range(4):
                    for oc in range(KC):
                        for ic in range(KC):
                            ins = nc.tensor.transpose(psR[n][:, ic * D + oc * P:ic * D + oc * P + P],
                                                      wqkvp[:, n, oc, ic * P:ic * P + P], ident[:, :])
                    ins.then_inc(s_w_t, 1)

                pe.wait_ge(s_wsplit, 5)
                pe.wait_ge(s_wsplit_lo, 3)

                def step(s, par, h, last):
                    first = isinstance(s, int) and s == 0
                    pe.wait_ge(s_hit_done, KC * (s + 1))
                    pe.wait_ge(s_lot_done, KC * (s + 1))
                    pe.wait_ge(s_tab_ready, J * s)
                    for c in range(KC):
                        n = 0
                        for wgt, xt in ((wq_hi, xt_hi), (wq_lo, xt_hi), (wq_hi, xt_lo)):
                            for kc in range(KC):
                                ins = nc.tensor.matmul(psR[c][:, 0:TS], wgt[:, kc, c * P:(c + 1) * P], xt[:, kc, :],
                                                       start=n == 0, stop=n == 3 * KC - 1)
                                n += 1
                        ins.then_inc(s_q_mm, 1)
                    for j in range(J):
                        n = 0
                        for xt, wgt in ((xt_hi, wk_hi), (xt_hi, wk_lo), (xt_lo, wk_hi)):
                            for kc in range(KC):
                                ins = nc.tensor.matmul(psR[2 + j // 2][0:T, (j % 2) * D:(j % 2 + 1) * D],
                                                       xt[:, kc, j * T:(j + 1) * T], wgt[:, kc, :],
                                                       start=n == 0, stop=n == 3 * KC - 1)
                                n += 1
                        if j % 2:
                            ins.then_inc(s_k_mm, 1)
                    for j in range(J):
                        if j < KC:
                            pe.wait_ge(s_q_done, KC * s + j + 1)
                        else:
                            pe.wait_ge(s_k_done, 2 * s + j - KC + 1)
                        n = 0
                        for xt, wgt in ((xt_hi, wx_hi), (xt_hi, wx_lo), (xt_lo, wx_hi)):
                            for kc in range(KC):
                                ins = nc.tensor.matmul(psR[j][0:T, 0:XW], xt[:, kc, j * T:(j + 1) * T], wgt[:, kc, :],
                                                       start=n == 0, stop=n == 3 * KC - 1)
                                n += 1
                        ins.then_inc(s_xt_mm, 1)
                    if not last:
                        transposes(s + 1)
                    pe.wait_ge(s_khi_done, 2 * (s + 1))
                    pe.wait_ge(s_klo_done, 2 * (s + 1))
                    pe.wait_ge(s_xnhi_ready, s + 1)
                    pe.wait_ge(s_xnlo_ready, s + 1)
                    for c in range(KC):
                        for j in range(J):
                            for n, (kk, xx) in enumerate(((k_hi, xn_hi), (k_hi, xn_lo), (k_lo, xn_hi))):
                                ins = nc.tensor.matmul(psG[c][:, 0:GW], kk[:, j, c * P:(c + 1) * P], xx[:, par, j, :],
                                                       start=first and j == 0 and n == 0,
                                                       stop=last and j == J - 1 and n == 2)
                    ins.then_inc(s_g_done, 1)

                over_tiles(pe, step, NS)

        with ExitStack() as ph, nc.Block() as block:
            def sb2(name, shape, dt=F32):
                return sb_in(ph, name, shape, dt)

            heads = sb2("heads", [P, P])
            gt_sb = sb2("gt_sb", [P, KC, D])
            ctx_t = sb2("ctx_t", [P, KC, P])
            ksum = sb2("ksum", [P, KC, QH])
            of_head = sb2("of_head", [P, QH])
            spread = sb2("spread", [P, KC, P], F32R)
            q_cur = sb2("q_cur", [P, KC, TS])
            den = sb2("den", [T, J, QH])
            den_hl = sb2("den_hl", [T, J, P // J], F32R)
            den_rows = sb2("den_rows", [P, TS], F32R)
            zeros = sb2("zeros", [P, TS])
            mix_hi = sb2("mix_hi", [P, KC, D], F32R)
            mix_lo = sb2("mix_lo", [P, KC, D], F32R)
            ones_r = sb2("ones_r", [2, T], F32R)
            bias_a = sb2("bias_a", [2, D])
            bias_b = sb2("bias_b", [2, D])
            bias_ah = sb2("bias_ah", [2, D], F32R)
            bias_bh = sb2("bias_bh", [2, D], F32R)
            bias_hl = sb2("bias_hl", [2, 2, D], F32R)
            bias_g = sb2("bias_g", [E, 1])
            gw_sb = sb2("gw_sb", [P, KC, E])
            before = sb2("before", [P, T])
            ones = sb2("ones", [P, T])
            desc = sb2("desc", [T, J, E])
            limit = sb2("limit", [T, J])
            token = sb2("token", [T, J])
            seen = sb2("seen", [T, E])
            isrc = sb2("isrc", [T, 2, J], I32)
            idst = sb2("idst", [T, 2, J], I32)
            gx = sb2("gx", [T, 2, J, TW])
            gl = sb2("gl", [T, 2, J, H])
            qp = sb2("qp", [P, KC, TS])
            qp_hi = sb2("qp_hi", [P, KC, TS], F32R)
            qp_lo = sb2("qp_lo", [P, KC, TS], F32R)
            att = sb2("att", [T, J, H])
            att2 = sb2("att2", [T, J, H])
            atm = sb2("atm", [T, J])
            ati = sb2("ati", [T, J])
            pr = sb2("pr", [T, J, H, DH])
            pr2 = sb2("pr2", [T, J, 2, DH])
            pr4 = sb2("pr4", [T, J, DH])
            xg = sb2("xg", [T, J, D])
            xd = sb2("xd", [T, 2, J, RW])
            st6 = sb2("st6b", [T, J, 6])
            mv = sb2("mvb", [T, J, 2])
            rstd = sb2("rstdb", [T, J])
            nmr = sb2("nmr", [T, J])
            xn2 = sb2("xn2", [T, J, D])
            x2t = sb2("x2t", [P, KC, TS])
            lg_t = sb2("lg_t", [E, TS])
            lmax = sb2("lmax", [T, J])
            eqm = sb2("eqm", [T, J, E])
            lex = sb2("lex", [T, J, E])
            lsum = sb2("lsum", [T, J])
            wmax = sb2("wmax", [T, J])
            oh = sb2("oh", [T, J, E])
            cum = sb2("cum", [T, J + 1, E])
            pos = sb2("pos", [T, J, E])
            picked = sb2("picked", [T, J, E])
            over = sb2("over", [T, J])
            slotf = sb2("slotf", [T, J])
            slots = sb2("slots", [T, 2, J], I32)

            psB = [ps_in(ph, f"psB{c}", [P, 512]) for c in range(KC)]
            psM = [ps_in(ph, f"psM{c}", [P, 512]) for c in range(2)]
            psX = [ps_in(ph, f"psX{c}", [P, 512]) for c in range(KC)]
            psL = ps_in(ph, "psL", [P, 512])
            psC = ps_in(ph, "psC", [P, 512])

            s_x_in0 = sem_in(ph, "s_x_in0")
            s_x_in1 = sem_in(ph, "s_x_in1")
            s_idx_in0 = sem_in(ph, "s_idx_in0")
            s_idx_in1 = sem_in(ph, "s_idx_in1")
            s_gat0 = sem_in(ph, "s_gat0")
            s_gat1 = sem_in(ph, "s_gat1")
            s_x_out0 = sem_in(ph, "s_x_out0")
            s_x_out1 = sem_in(ph, "s_x_out1")
            s_scat0 = sem_in(ph, "s_scat0")
            s_scat1 = sem_in(ph, "s_scat1")
            s_c_zero = sem_in(ph, "s_c_zero")
            s_c_in = sem_in(ph, "s_c_in")
            s_x2_ready = sem_in(ph, "s_x2_ready")
            s_xg_done = sem_in(ph, "s_xg_done")
            s_c_set = sem_in(ph, "s_c_set")
            s_pr_done = sem_in(ph, "s_pr_done")
            s_slots_ready = sem_in(ph, "s_slots_ready")
            s_aggr2 = sem_in(ph, "s_aggr2")
            s_xn2_ready = sem_in(ph, "s_xn2_ready")
            s_var2 = sem_in(ph, "s_var2")
            s_rstd2 = sem_in(ph, "s_rstd2")
            s_gt_mm = sem_in(ph, "s_gt_mm")
            s_gt_sb_done = sem_in(ph, "s_gt_sb_done")
            s_mixw_mm = sem_in(ph, "s_mixw_mm")
            s_mixw_hi = sem_in(ph, "s_mixw_hi")
            s_mixw_lo = sem_in(ph, "s_mixw_lo")
            s_qp_hi = sem_in(ph, "s_qp_hi")
            s_qp_lo = sem_in(ph, "s_qp_lo")
            s_qp_done = sem_in(ph, "s_qp_done")
            s_d_mm = sem_in(ph, "s_d_mm")
            s_dve_setup = sem_in(ph, "s_dve_setup")
            s_pe_passed = sem_in(ph, "s_pe_passed")
            s_q_ready = sem_in(ph, "s_q_ready")
            s_a_sub = sem_in(ph, "s_a_sub")
            s_a_exp = sem_in(ph, "s_a_exp")
            s_t2_done = sem_in(ph, "s_t2_done")
            s_x2t_ready = sem_in(ph, "s_x2t_ready")
            s_l_sub = sem_in(ph, "s_l_sub")
            s_l_exp = sem_in(ph, "s_l_exp")
            s_nmr_done = sem_in(ph, "s_nmr_done")
            s_ctx_mm = sem_in(ph, "s_ctx_mm")
            s_ctx_done = sem_in(ph, "s_ctx_done")
            s_dt_mm = sem_in(ph, "s_dt_mm")
            s_den_max = sem_in(ph, "s_den_max")
            s_den_done = sem_in(ph, "s_den_done")
            s_a_sum = sem_in(ph, "s_a_sum")
            s_a_lin = sem_in(ph, "s_a_lin")
            s_a_max = sem_in(ph, "s_a_max")
            s_b_mm = sem_in(ph, "s_b_mm")
            s_den_t = sem_in(ph, "s_den_t")
            s_a_tot = sem_in(ph, "s_a_tot")
            s_a_inv = sem_in(ph, "s_a_inv")
            s_a_div = sem_in(ph, "s_a_div")
            s_mix_mm = sem_in(ph, "s_mix_mm")
            s_pr2_done = sem_in(ph, "s_pr2_done")
            s_pr4_done = sem_in(ph, "s_pr4_done")
            s_stats2 = sem_in(ph, "s_stats2")
            s_lgt_mm = sem_in(ph, "s_lgt_mm")
            s_lgt_ready = sem_in(ph, "s_lgt_ready")
            s_lg_mm = sem_in(ph, "s_lg_mm")
            s_den_hi = sem_in(ph, "s_den_hi")
            s_den_rcp = sem_in(ph, "s_den_rcp")
            s_l_max = sem_in(ph, "s_l_max")
            s_l_eq = sem_in(ph, "s_l_eq")
            s_w_done = sem_in(ph, "s_w_done")
            s_w_max = sem_in(ph, "s_w_max")
            s_oh_done = sem_in(ph, "s_oh_done")
            s_cum_done = sem_in(ph, "s_cum_done")
            s_l_sum = sem_in(ph, "s_l_sum")
            s_prb_done = sem_in(ph, "s_prb_done")
            s_pos_mm = sem_in(ph, "s_pos_mm")
            s_seen_done = sem_in(ph, "s_seen_done")
            s_pos_done = sem_in(ph, "s_pos_done")
            s_over_done = sem_in(ph, "s_over_done")
            s_limit_done = sem_in(ph, "s_limit_done")
            s_pick_done = sem_in(ph, "s_pick_done")
            s_slot_sum = sem_in(ph, "s_slot_sum")
            x_in, idx_in = [s_x_in0, s_x_in1], [s_idx_in0, s_idx_in1]
            gat, x_out, scat = [s_gat0, s_gat1], [s_x_out0, s_x_out1], [s_scat0, s_scat1]

            def over_steps(eng, step):
                step(0, 0, 0, 2)
                step(1, 1, 0, 2)
                with eng.Fori(1, (NS - 3) // 2) as i:
                    step(2 * i, 0, i, 2)
                    step(2 * i + 1, 1, i, 2)
                step(NS - 3, 0, (NS - 3) // 2, 2)
                step(NS - 2, 1, (NS - 3) // 2, 1)
                step(NS - 1, 0, NS // 2, 0)

            @block.sync
            def _(sp):
                sp.wait_ge(s_c_zero, 1)
                sp.dma_start(bias_a[0:1, :], bproj.rearrange("(a n) -> a n", a=1)).then_inc(s_c_in, 16)
                sp.dma_start(bias_b[1:2, :], bproj.rearrange("(a n) -> a n", a=1)).then_inc(s_c_in, 16)
                sp.dma_start(bias_g[:, :], gate_b.rearrange("(e a) -> e a", a=1)).then_inc(s_c_in, 16)
                sp.dma_start(gw_sb[:, :, :], gate_w.rearrange("(c p) e -> p c e", p=P)).then_inc(s_c_in, 16)

                def idx(t, s):
                    return t[bass.ds(s * TS, TS)].rearrange("(p j) -> p j", j=J)

                def load(s, par):
                    sp.dma_start(isrc[:, par, :], idx(src, s)).then_inc(idx_in[par], 16)
                    sp.dma_start(idst[:, par, :], idx(dst, s)).then_inc(idx_in[par], 16)
                    sp.dma_start(x_sb[:, par, :, :], tok(x, s, D)).then_inc(x_in[par], 16)

                load(0, 0)
                load(1, 1)

                def step(s, par, h, ahead):
                    sp.wait_ge(s_x2_ready, 2 * (s + 1))
                    sp.dma_start(tok(out, s, D), xd[:, par, :, 0:D]).then_inc(x_out[par], 16)
                    if ahead == 2:
                        sp.wait_ge(s_xg_done, s + 1)
                        sp.wait_ge(gat[par], 32 * J * (h + 1))
                        load(s + 2, par)

                over_steps(sp, step)
                for par in range(2):
                    n = NS // 2 + (1 - par)
                    sp.wait_ge(x_out[par], 16 * n)
                    sp.wait_ge(scat[par], 16 * J * n)

            @block.gpsimd
            def _(pool):
                nc.gpsimd.memset(bias_a[:, :], 0.0)
                nc.gpsimd.memset(bias_b[:, :], 0.0)
                nc.gpsimd.memset(before[:, :], 1.0)
                nc.gpsimd.memset(zeros[:, :], 0.0)
                nc.gpsimd.memset(ones[:, :], 1.0).then_inc(s_c_zero, 1)
                pool.wait_ge(s_c_zero, 1)
                nc.gpsimd.affine_select(out=before[:, :], in_=before[:, :], compare_op=ALU.is_gt, fill=0.0,
                                        base=0, pattern=[[1, T]], channel_multiplier=-1)
                nc.gpsimd.iota(desc[:, :, :], [[0, J], [-1, E]], base=E, channel_multiplier=0,
                               allow_small_or_imprecise_dtypes=True)
                nc.gpsimd.iota(token[:, :], [[1, J]], base=0, channel_multiplier=J,
                               allow_small_or_imprecise_dtypes=True)
                nc.gpsimd.memset(xd[:, :, :, :], 0.0)
                nc.gpsimd.memset(cum[:, 0, :], 0.0)
                nc.gpsimd.memset(seen[:, :], 0.0).then_inc(s_c_set, 1)
                pool.wait_ge(s_c_set, 1)
                nc.gpsimd.iota(seen[0:1, :], [[ROWS, E]], base=0, channel_multiplier=0,
                               allow_small_or_imprecise_dtypes=True).then_inc(s_c_set, 1)

                def gather_l(s, par, h):
                    pool.wait_ge(idx_in[par], 32 * (h + 1))
                    if not (isinstance(s, int) and s < 2):
                        pool.wait_ge(s_a_sum, s - 1)
                    passed(pool, s_pool_passed)
                    for j in range(J):
                        pool.indirect_dma_start(out=gl[:, par, j, :], out_offset=None, in_=table_l,
                                                in_offset=bass.IndirectOffsetOnAxis(ap=isrc[:, par, j:j + 1], axis=0))\
                            .then_inc(gat[par], 16)

                def gather_x(s, par, h):
                    pool.wait_ge(idx_in[par], 32 * (h + 1))
                    if not (isinstance(s, int) and s < 2):
                        pool.wait_ge(s_pr_done, s - 1)
                    passed(pool, s_pool_passed)
                    for j in range(J):
                        pool.indirect_dma_start(out=gx[:, par, j, :], out_offset=None, in_=table,
                                                in_offset=bass.IndirectOffsetOnAxis(ap=idst[:, par, j:j + 1], axis=0))\
                            .then_inc(gat[par], 16)

                def scatter(s, par):
                    pool.wait_ge(s_slots_ready, s + 1)
                    passed(pool, s_pool_passed)
                    for j in range(J):
                        pool.indirect_dma_start(out=rows, in_=xd[:, par, j, :], in_offset=None,
                                                out_offset=bass.IndirectOffsetOnAxis(ap=slots[:, par, j:j + 1], axis=0),
                                                bounds_check=E * ROWS - 1, oob_is_err=False).then_inc(scat[par], 16)

                def rstd_of(s):
                    pool.wait_ge(s_aggr2, J * (s + 1))
                    pool.wait_ge(s_xn2_ready, s)
                    passed(pool, s_pool_passed)
                    nc.gpsimd.tensor_scalar(rstd[:, :], mv[:, :, 1], EPS, None, ALU.add).then_inc(s_var2, 1)
                    pool.wait_ge(s_var2, s + 1)
                    nc.gpsimd.tensor_tensor(rstd[:, :], rstd[:, :], mhalf[0:T, :], ALU.pow).then_inc(s_rstd2, 1)

                gather_l(0, 0, 0)
                gather_x(0, 0, 0)
                gather_l(1, 1, 0)
                gather_x(1, 1, 0)

                def step(s, par, h, ahead):
                    last = ahead == 0
                    early = isinstance(s, int) and s < 2
                    fetch = not last and not (early and s == 0)
                    if not early:
                        scatter(s - 2, par)
                    if fetch:
                        gather_l(s + 1, 1 - par, h + par)
                        gather_x(s + 1, 1 - par, h + par)
                    rstd_of(s)

                over_steps(pool, step)
                scatter(NS - 2, 1)
                scatter(NS - 1, 0)


            @block.scalar
            def _(act):
                for c in range(KC):
                    act.wait_ge(s_gt_mm, KC)
                    act.activation(gt_sb[:, c, :], psB[c][:, 0:D], ACT.Copy).then_inc(s_gt_sb_done, 1)
                for c in range(KC):
                    act.wait_ge(s_mixw_mm, KC)
                    act.activation(mix_hi[:, c, :], psX[c][:, 0:D], ACT.Copy).then_inc(s_mixw_hi, 1)

                def att_exp(s):
                    act.wait_ge(s_a_sub, s + 1)
                    act.activation(att2[:, :, :], att2[:, :, :], ACT.Exp).then_inc(s_a_exp, 1)

                def q_of(s):
                    act.wait_ge(s_d_mm, s)
                    act.activation(q_cur[:, :, :], q_all[:, :, bass.ds(s * TS, TS)], ACT.Copy).then_inc(s_q_ready, 1)

                def den_across(s):
                    act.wait_ge(s_dt_mm, s + 1)
                    act.wait_ge(s_b_mm, KC * s)
                    for j in range(J):
                        mine = slice(j * (P // J), (j + 1) * (P // J))
                        ins = act.activation(den_rows[mine, j * T:(j + 1) * T], psC[mine, 256:256 + T], ACT.Copy)
                    ins.then_inc(s_den_t, 1)

                def across(s):
                    act.wait_ge(s_t2_done, s + 1)
                    act.wait_ge(s_lgt_mm, s)
                    for c in range(KC):
                        act.activation(x2t[:, c, :], psX[c][:, 0:TS], ACT.Copy).then_inc(s_x2t_ready, 1)

                def q_high(s):
                    act.wait_ge(s_mix_mm, 2 * s)
                    for c in range(KC):
                        act.wait_ge(s_qp_done, KC * s + c + 1)
                        act.activation(qp_hi[:, c, :], qp[:, c, :], ACT.Copy).then_inc(s_qp_hi, 1)

                def logits_out(s):
                    act.wait_ge(s_lgt_mm, s + 1)
                    act.wait_ge(s_lg_mm, s)
                    act.activation(lg_t[:, :], psL[0:E, 0:TS], ACT.Identity, bias=bias_g[:, :]).then_inc(s_lgt_ready, 1)

                def logit_exp(s):
                    act.wait_ge(s_l_sub, s + 1)
                    act.activation(lex[:, :, :], lex[:, :, :], ACT.Exp).then_inc(s_l_exp, 1)

                def step(s, par, h, ahead):
                    begun = not (isinstance(s, int) and s == 0)
                    if begun:
                        across(s - 1)
                    if ahead > 1:
                        q_of(s + 2)
                    if ahead > 0:
                        den_across(s + 1)
                    if begun:
                        logits_out(s - 1)
                    if ahead > 0:
                        q_high(s + 1)
                    if begun:
                        logit_exp(s - 1)
                    act.wait_ge(s_nmr_done, s + 1)
                    act.wait_ge(s_t2_done, s)
                    for j in range(J):
                        if j == J // 2 and ahead > 0:
                            att_exp(s + 1)
                        ins = act.activation(xn2[:, j, :], xd[:, par, j, 0:D], ACT.Identity, bias=nmr[:, j:j + 1],
                                             scale=rstd[:, j:j + 1])
                    ins.then_inc(s_xn2_ready, 1)

                act.wait_ge(s_dve_setup, 8)
                act.wait_ge(s_c_in, 64)
                q_of(0)
                den_across(0)
                q_of(1)
                q_high(0)
                att_exp(0)
                over_steps(act, step)
                across(NS - 1)
                logits_out(NS - 1)
                logit_exp(NS - 1)

            @block.vector
            def _(dve):
                nc.vector.memset(heads[:, :], 0.0)
                nc.vector.memset(ksum[:, :, :], 0.0).then_inc(s_dve_setup, 1)
                dve.wait_ge(s_dve_setup, 1)
                for b in range(P // QD):
                    mine = slice(b * QD, (b + 1) * QD)
                    nc.vector.memset(heads[mine, mine], 1.0)
                    for c in range(KC):
                        h = c * (QH // KC) + b
                        ins = nc.vector.tensor_copy(ksum[mine, c, h:h + 1], g_sb[mine, c, D:D + 1])
                ins.then_inc(s_dve_setup, 1)
                dve.wait_ge(s_dve_setup, 2)
                for c in range(KC):
                    dve.wait_ge(s_ctx_mm, KC)
                    nc.vector.tensor_tensor(ctx_t[:, c, :], psM[c][:, 0:P], heads[:, :], ALU.mult).then_inc(s_ctx_done, 1)
                dve.wait_ge(s_c_set, 2)
                dve.wait_ge(s_c_in, 64)
                nc.vector.tensor_copy(ones_r[:, :], ones[0:2, :])
                nc.vector.tensor_copy(bias_ah[:, :], bias_a[:, :]).then_inc(s_dve_setup, 1)
                nc.vector.tensor_copy(bias_bh[:, :], bias_b[:, :]).then_inc(s_dve_setup, 1)
                dve.wait_ge(s_dve_setup, 4)
                nc.vector.tensor_tensor(bias_b[:, :], bias_b[:, :], bias_bh[:, :].bitcast(F32), ALU.subtract)\
                  .then_inc(s_dve_setup, 1)
                dve.wait_ge(s_dve_setup, 5)
                nc.vector.tensor_tensor(bias_hl[:, 0, :], bias_b[:, :], bias_ah[:, :].bitcast(F32), ALU.add)
                nc.vector.tensor_tensor(bias_hl[:, 1, :], bias_b[:, :], bias_ah[:, :].bitcast(F32), ALU.add)\
                  .then_inc(s_dve_setup, 1)
                for c in range(KC):
                    dve.wait_ge(s_mixw_hi, c + 1)
                    nc.vector.tensor_tensor(mix_lo[:, c, :], psX[c][:, 0:D], mix_hi[:, c, :].bitcast(F32), ALU.subtract)\
                      .then_inc(s_mixw_lo, 1)

                nc.vector.tensor_reduce(of_head[:, :], ident[:, :].rearrange("p (n h) -> p h n", h=QH), axis=AX.X,
                                        op=ALU.add).then_inc(s_dve_setup, 1)
                dve.wait_ge(s_dve_setup, 7)
                for c in range(KC):
                    nc.vector.tensor_copy(spread[:, c, :].rearrange("p (h d) -> p h d", d=QD),
                                          wide(of_head[:, c * (QH // KC):(c + 1) * (QH // KC)], QD))
                nc.vector.tensor_copy(den_hl[:, :, :], zeros[0:T, 0:P].rearrange("p (j n) -> p j n", j=J))
                nc.vector.tensor_copy(den_rows[:, :], zeros[:, :]).then_inc(s_dve_setup, 1)
                dve.wait_ge(s_dve_setup, 8)

                def den_of(s):
                    dve.wait_ge(s_d_mm, s + 1)
                    dve.wait_ge(s_dt_mm, s)
                    nc.vector.tensor_scalar(den[:, :, :], psC[0:T, 128:128 + J * QH].rearrange("p (j h) -> p j h", j=J),
                                            1e-6, None, ALU.max).then_inc(s_den_max, 1)
                    dve.wait_ge(s_den_max, s + 1)
                    nc.vector.reciprocal(den[:, :, :], den[:, :, :]).then_inc(s_den_rcp, 1)
                    dve.wait_ge(s_den_rcp, s + 1)
                    nc.vector.tensor_copy(den_hl[:, :, 0:QH], den[:, :, :]).then_inc(s_den_hi, 1)

                def den_low(s):
                    dve.wait_ge(s_den_hi, s + 1)
                    nc.vector.tensor_tensor(den_hl[:, :, QH:2 * QH], den[:, :, :], den_hl[:, :, 0:QH].bitcast(F32),
                                            ALU.subtract).then_inc(s_den_done, 1)

                def q_scaled(s):
                    for c in range(KC):
                        dve.wait_ge(s_qp_hi, KC * s)
                        dve.wait_ge(s_b_mm, KC * s + c + 1)
                        nc.vector.tensor_tensor(qp[:, c, :], psB[c][:, 0:TS], q_all[:, c, bass.ds(s * TS, TS)], ALU.mult)\
                          .then_inc(s_qp_done, 1)

                def q_low(s):
                    for c in range(KC):
                        dve.wait_ge(s_mix_mm, 2 * s)
                        dve.wait_ge(s_qp_hi, KC * s + c + 1)
                        nc.vector.tensor_tensor(qp_lo[:, c, :], qp[:, c, :], qp_hi[:, c, :].bitcast(F32), ALU.subtract)\
                          .then_inc(s_qp_lo, 1)

                def att_sum(s, par, h):
                    dve.wait_ge(gat[par], 32 * J * (h + 1))
                    nc.vector.tensor_tensor(att[:, :, :], gl[:, par, :, :], gx[:, par, :, D:TW], ALU.add)\
                      .then_inc(s_a_sum, 1)

                def att_leaky(s):
                    dve.wait_ge(s_a_sum, s + 1)
                    nc.vector.scalar_tensor_tensor(att2[:, :, :], att[:, :, :], 0.01, att[:, :, :], ALU.mult, ALU.max)\
                      .then_inc(s_a_lin, 1)

                def att_max(s):
                    dve.wait_ge(s_a_lin, s + 1)
                    nc.vector.tensor_reduce(atm[:, :], att2[:, :, :], axis=AX.X, op=ALU.max).then_inc(s_a_max, 1)

                def att_sub(s):
                    dve.wait_ge(s_a_max, s + 1)
                    nc.vector.tensor_tensor(att2[:, :, :], att2[:, :, :], wide(atm[:, :], H), ALU.subtract)\
                      .then_inc(s_a_sub, 1)

                def mix_in(s, par, h, ahead):
                    dve.wait_ge(s_a_exp, s + 1)
                    nc.vector.tensor_reduce(atm[:, :], att2[:, :, :], axis=AX.X, op=ALU.add).then_inc(s_a_tot, 1)
                    dve.wait_ge(s_a_tot, s + 1)
                    nc.vector.reciprocal(ati[:, :], atm[:, :]).then_inc(s_a_inv, 1)
                    dve.wait_ge(s_a_inv, s + 1)
                    nc.vector.tensor_tensor(att2[:, :, :], att2[:, :, :], wide(ati[:, :], H), ALU.mult)\
                      .then_inc(s_a_div, 1)
                    dve.wait_ge(s_a_div, s + 1)
                    nc.vector.tensor_tensor(pr[:, :, :, :],
                                            gx[:, par, :, 0:D].rearrange("p j (h d) -> p j h d", h=H),
                                            wide(att2[:, :, :], DH), ALU.mult).then_inc(s_pr_done, 1)
                    dve.wait_ge(s_pr_done, s + 1)
                    nc.vector.tensor_tensor(pr2[:, :, :, :], pr[:, :, 0:2, :], pr[:, :, 2:4, :], ALU.add)\
                      .then_inc(s_pr2_done, 1)
                    dve.wait_ge(s_pr2_done, s + 1)
                    nc.vector.tensor_tensor(pr4[:, :, :], pr2[:, :, 0, :], pr2[:, :, 1, :], ALU.add)\
                      .then_inc(s_pr4_done, 1)
                    if ahead > 0:
                        den_of(s + 1)
                    dve.wait_ge(s_pr4_done, s + 1)
                    dve.wait_ge(x_in[par], 16 * (h + 1))
                    nc.vector.tensor_tensor(xg[:, :, :].rearrange("p j (h d) -> p j h d", h=H),
                                            x_sb[:, par, :, :].rearrange("p j (h d) -> p j h d", h=H),
                                            pr4[:, :, :].rearrange("p j (a d) -> p j a d", a=1)
                                            .broadcast_to([T, J, H, DH]), ALU.add).then_inc(s_xg_done, 1)
                    if ahead > 0:
                        den_low(s + 1)
                    dve.wait_ge(s_xg_done, s + 1)
                    dve.wait_ge(x_out[par], 16 * h)
                    dve.wait_ge(scat[par], 16 * J * h)
                    for n in range(2):
                        dve.wait_ge(s_mix_mm, 2 * s + n + 1)
                        nc.vector.tensor_tensor(xd[:, par, 2 * n:2 * n + 2, 0:D],
                                                psM[n][0:T, :].rearrange("p (j o) -> p j o", j=2),
                                                xg[:, 2 * n:2 * n + 2, :], ALU.add).then_inc(s_x2_ready, 1)
                    nc.vector.tensor_scalar(xd[:, par, :, D + 1], token[:, :], 0.0, None, ALU.add)
                    for j in range(J):
                        dve.wait_ge(s_x2_ready, 2 * s + j // 2 + 1)
                        nc.vector.bn_stats(st6[:, j, :], xd[:, par, j, 0:D]).then_inc(s_stats2, 1)
                    nc.vector.tensor_scalar(token[:, :], token[:, :], float(TS), None, ALU.add)
                    dve.wait_ge(s_stats2, J * (s + 1))
                    passed(dve, s_dve_passed)
                    for j in range(J):
                        nc.vector.bn_aggr(mv[:, j, :], st6[:, j, :]).then_inc(s_aggr2, 1)

                def route(s, par, h, following, ahead):
                    lg = psL[0:T, 0:J * E].rearrange("p (j e) -> p j e", e=E)
                    dve.wait_ge(s_lg_mm, s + 1)
                    nc.vector.tensor_reduce(lmax[:, :], lg, axis=AX.X, op=ALU.max).then_inc(s_l_max, 1)
                    dve.wait_ge(s_l_max, s + 1)
                    nc.vector.tensor_tensor(eqm[:, :, :], lg, wide(lmax[:, :], E), ALU.is_equal).then_inc(s_l_eq, 1)
                    nc.vector.tensor_tensor(lex[:, :, :], lg, wide(lmax[:, :], E), ALU.subtract).then_inc(s_l_sub, 1)
                    dve.wait_ge(s_l_eq, s + 1)
                    nc.vector.tensor_tensor(eqm[:, :, :], eqm[:, :, :], desc[:, :, :], ALU.mult).then_inc(s_w_done, 1)
                    dve.wait_ge(s_w_done, s + 1)
                    nc.vector.tensor_reduce(wmax[:, :], eqm[:, :, :], axis=AX.X, op=ALU.max).then_inc(s_w_max, 1)
                    dve.wait_ge(s_w_max, s + 1)
                    nc.vector.tensor_tensor(oh[:, :, :], eqm[:, :, :], wide(wmax[:, :], E), ALU.is_equal)\
                      .then_inc(s_oh_done, 1)
                    nc.vector.tensor_scalar(limit[:, :], wmax[:, :], -float(ROWS), float(E * ROWS + CAP), ALU.mult, ALU.add)\
                      .then_inc(s_limit_done, 1)
                    for j in range(J):
                        dve.wait_ge(s_oh_done, s + 1)
                        dve.wait_ge(s_cum_done, J * s + j)
                        nc.vector.tensor_tensor(cum[:, j + 1, :], cum[:, j, :], oh[:, j, :], ALU.add)\
                          .then_inc(s_cum_done, 1)
                    dve.wait_ge(s_l_exp, s + 1)
                    nc.vector.tensor_reduce(lsum[:, :], lex[:, :, :], axis=AX.X, op=ALU.add).then_inc(s_l_sum, 1)
                    if following:
                        scale_of(s + 1)
                    dve.wait_ge(s_l_sum, s + 1)
                    nc.vector.reciprocal(xd[:, par, :, D], lsum[:, :]).then_inc(s_prb_done, 1)
                    dve.wait_ge(s_pos_mm, s + 1)
                    nc.vector.tensor_tensor(pos[:, :, :], cum[:, 0:J, :],
                                            psC[0:T, 0:E].rearrange("p (a e) -> p a e", a=1).broadcast_to([T, J, E]),
                                            ALU.add).then_inc(s_pos_done, 1)
                    nc.vector.tensor_tensor(seen[:, :], seen[:, :], cum[:, J, :], ALU.add).then_inc(s_seen_done, 1)
                    if ahead:
                        att_sum(s + 2, par, h)
                    dve.wait_ge(s_pos_done, s + 1)
                    nc.vector.tensor_tensor(picked[:, :, :], pos[:, :, :], oh[:, :, :], ALU.mult).then_inc(s_pick_done, 1)
                    if ahead:
                        att_leaky(s + 2)
                    dve.wait_ge(s_pick_done, s + 1)
                    nc.vector.tensor_reduce(slotf[:, :], picked[:, :, :], axis=AX.X, op=ALU.add).then_inc(s_slot_sum, 1)
                    if ahead:
                        att_max(s + 2)
                    dve.wait_ge(s_slot_sum, s + 1)
                    dve.wait_ge(s_limit_done, s + 1)
                    nc.vector.tensor_tensor(over[:, :], slotf[:, :], limit[:, :], ALU.is_ge).then_inc(s_over_done, 1)
                    if ahead:
                        att_sub(s + 2)
                    dve.wait_ge(s_over_done, s + 1)
                    dve.wait_ge(s_prb_done, s + 1)
                    nc.vector.scalar_tensor_tensor(slots[:, par, :], over[:, :], BIG, slotf[:, :], ALU.mult, ALU.add)\
                      .then_inc(s_slots_ready, 1)

                def scale_of(s):
                    dve.wait_ge(s_rstd2, s + 1)
                    nc.vector.scalar_tensor_tensor(nmr[:, :], mv[:, :, 0], -1.0, rstd[:, :], ALU.mult, ALU.mult)\
                      .then_inc(s_nmr_done, 1)

                def step(s, par, h, ahead):
                    mix_in(s, par, h, ahead)
                    if ahead > 0:
                        q_scaled(s + 1)
                    if isinstance(s, int) and s == 0:
                        scale_of(0)
                        q_low(1)
                        att_sum(1, 1, 0)
                        att_leaky(1)
                        att_max(1)
                        att_sub(1)
                    else:
                        route(s - 1, 1 - par, h + par, True, ahead > 0)
                        if ahead > 0:
                            q_low(s + 1)

                den_of(0)
                den_low(0)
                q_scaled(0)
                q_low(0)
                att_sum(0, 0, 0)
                att_leaky(0)
                att_max(0)
                att_sub(0)
                over_steps(dve, step)
                route(NS - 1, 0, 0, False, False)

            @block.tensor
            def _(pe):
                for c in range(KC):
                    for fc in range(KC):
                        ins = nc.tensor.transpose(psB[c][:, fc * P:(fc + 1) * P], g_sb[:, fc, c * P:(c + 1) * P],
                                                  ident[:, :])
                    ins.then_inc(s_gt_mm, 1)
                pe.wait_ge(s_gt_sb_done, KC)
                for ec in range(KC):
                    for cc in range(KC):
                        ins = nc.tensor.matmul(psM[ec][:, 0:P], wv_t[:, cc, ec * P:(ec + 1) * P],
                                               gt_sb[:, cc, ec * P:(ec + 1) * P], start=cc == 0, stop=cc == KC - 1)
                    ins.then_inc(s_ctx_mm, 1)
                pe.wait_ge(s_ctx_done, KC)
                for fc in range(KC):
                    nc.tensor.matmul(psX[fc][:, 0:D], ctx_t[:, fc, :], wp_t[:, fc, :], start=True, stop=True)\
                      .then_inc(s_mixw_mm, 1)

                def q_ksum(s, routed):
                    pe.wait_ge(s_q_ready, s + 1)
                    pe.wait_ge(s_den_t, s)
                    if not (isinstance(routed, int) and routed <= 0):
                        pe.wait_ge(s_pos_done, routed)
                    for j in range(J):
                        for c in range(KC):
                            ins = nc.tensor.matmul(psC[0:T, 128 + j * QH:128 + (j + 1) * QH],
                                                   q_cur[:, c, j * T:(j + 1) * T],
                                                   ksum[:, c, :], start=c == 0, stop=c == KC - 1)
                    ins.then_inc(s_d_mm, 1)

                def den_transpose(s):
                    pe.wait_ge(s_den_done, s + 1)
                    nc.tensor.transpose(psC[:, 256:256 + T], den_hl[:, :, :].bitcast(F32).rearrange("p j n -> p (j n)"),
                                        ident[0:T, 0:T]).then_inc(s_dt_mm, 1)

                def den_spread(s):
                    pe.wait_ge(s_den_t, s + 1)
                    pe.wait_ge(s_qp_done, KC * s)
                    for c in range(KC):
                        nc.tensor.matmul(psB[c][:, 0:TS], spread[:, c, :], den_rows[:, :], start=True, stop=True)\
                          .then_inc(s_b_mm, 1)

                def mix(s):
                    pe.wait_ge(s_qp_hi, KC * (s + 1))
                    pe.wait_ge(s_x2_ready, 2 * s)
                    for j in range(J):
                        o = psM[j // 2][0:T, (j % 2) * D:(j % 2 + 1) * D]
                        if j % 2 == 0:
                            nc.tensor.matmul(psM[j // 2][0:T, :], ones_r[:, :], bias_hl[:, :, :].rearrange("p n o -> p (n o)"),
                                             start=True, stop=False)
                        for w in (mix_hi, mix_lo):
                            for kc in range(KC):
                                nc.tensor.matmul(o, qp_hi[:, kc, j * T:(j + 1) * T], w[:, kc, :], start=False, stop=False)
                    pe.wait_ge(s_qp_lo, KC * (s + 1))
                    for j in range(J):
                        o = psM[j // 2][0:T, (j % 2) * D:(j % 2 + 1) * D]
                        for kc in range(KC):
                            ins = nc.tensor.matmul(o, qp_lo[:, kc, j * T:(j + 1) * T], mix_hi[:, kc, :],
                                                   start=False, stop=j % 2 == 1 and kc == KC - 1)
                        if j % 2:
                            ins.then_inc(s_mix_mm, 1)

                def transposes(s):
                    pe.wait_ge(s_xn2_ready, s + 1)
                    pe.wait_ge(s_x2t_ready, KC * s)
                    for c in range(KC):
                        for j in range(J):
                            ins = nc.tensor.transpose(psX[c][:, j * T:(j + 1) * T], xn2[:, j, c * P:(c + 1) * P],
                                                      ident[0:T, 0:T])
                    ins.then_inc(s_t2_done, 1)

                def logits_by_expert(s):
                    pe.wait_ge(s_x2t_ready, KC * (s + 1))
                    pe.wait_ge(s_l_sub, s)
                    pe.wait_ge(s_l_eq, s)
                    for kc in range(KC):
                        ins = nc.tensor.matmul(psL[0:E, 0:TS], gw_sb[:, kc, :], x2t[:, kc, :],
                                               start=kc == 0, stop=kc == KC - 1)
                    ins.then_inc(s_lgt_mm, 1)

                def logits_by_token(s):
                    pe.wait_ge(s_lgt_ready, s + 1)
                    passed(pe, s_pe_passed)
                    for j in range(J):
                        ins = nc.tensor.transpose(psL[0:T, j * E:(j + 1) * E], lg_t[:, j * T:(j + 1) * T],
                                                  ident[0:E, 0:E])
                    ins.then_inc(s_lg_mm, 1)

                def positions(s):
                    pe.wait_ge(s_cum_done, J * (s + 1))
                    pe.wait_ge(s_seen_done, s)
                    nc.tensor.matmul(psC[0:T, 0:E], before[0:T, :], cum[:, J, :], start=True, stop=False)
                    nc.tensor.matmul(psC[0:T, 0:E], ones[0:T, :], seen[:, :], start=False, stop=True)\
                      .then_inc(s_pos_mm, 1)

                def step(s, par, h, ahead):
                    begun = not (isinstance(s, int) and s == 0)
                    if begun:
                        transposes(s - 1)
                    if ahead > 0:
                        den_transpose(s + 1)
                    if begun:
                        logits_by_expert(s - 1)
                    if ahead > 0:
                        den_spread(s + 1)
                    if begun:
                        logits_by_token(s - 1)
                    if ahead > 1:
                        q_ksum(s + 2, s - 1)
                    if begun:
                        positions(s - 1)
                    if ahead > 0:
                        mix(s + 1)

                pe.wait_ge(s_mixw_lo, KC)
                pe.wait_ge(s_c_in, 64)
                pe.wait_ge(s_c_set, 2)
                pe.wait_ge(s_dve_setup, 8)
                q_ksum(0, 0)
                den_transpose(0)
                den_spread(0)
                q_ksum(1, 0)
                mix(0)
                over_steps(pe, step)
                transposes(NS - 1)
                logits_by_expert(NS - 1)
                logits_by_token(NS - 1)
                positions(NS - 1)

        late.close()
        with ExitStack() as ph, nc.Block() as block:
            def sb3(name, shape, dt=F32):
                return sb_in(ph, name, shape, dt)

            NG = E * ST
            wraw = sb3("wraw", [P, KC * F + NF * D])
            w1_raw = wraw[:, 0:KC * F].rearrange("p (c f) -> p c f", c=KC)
            w2_raw = wraw[:, KC * F:].rearrange("p (c d) -> p c d", c=NF)
            w1_hi = sb3("w1_hi", [P, KC, F], F32R)
            w1_lo = sb3("w1_lo", [P, KC, F], F32R)
            w2_hi = sb3("w2_hi", [P, NF, D], F32R)
            w2_lo = sb3("w2_lo", [P, NF, D], F32R)
            b1_rows = sb3("b1_rows", [E * NF, P])
            b1_sb = sb3("b1_sb", [P, E * NF])
            b2_bc = sb3("b2_bc", [T3, E, D])
            xr = sb3("xr", [T3, ST, J, RW])
            st6 = sb3("st6c", [T3, J, 6])
            mv = sb3("mvc", [T3, J, 2])
            std = sb3("std", [T3, J])
            rstd = sb3("rstdc", [T3, J])
            nmr = sb3("nmrc", [T3, J])
            eps_c = sb3("eps_c", [P, 1])
            xn3 = sb3("xn3", [T3, J, D])
            xt_hi = sb3("xt3_hi", [P, 2, KC, TS3], F32R)
            xt_lo = sb3("xt3_lo", [P, 2, KC, TS3], F32R)
            hf = sb3("hf", [P, 4, TS3])
            h_hi = sb3("h_hi", [P, 4, TS3], F32R)
            h_lo = sb3("h_lo", [P, 4, TS3], F32R)
            yb = sb3("yb", [T3, J, D])
            ys = sb3("ys", [T3, J, D])
            top = sb3("top", [T3, J, D])
            bottom = sb3("bottom", [T3, J, D])
            yc = sb3("yc", [T3, J, D])
            fin = sb3("fin", [T3, J, D], I32)
            o_sb = sb3("o_sb", [T3, 2, J, D])
            tok_i = sb3("tok_i", [T3, 2, J], I32)

            psX = [ps_in(ph, f"psX3{c}", [P, 512]) for c in range(KC)]
            psH = [ps_in(ph, f"psH{c}", [P, 512]) for c in range(2)]
            psY = [ps_in(ph, f"psY{c}", [P, 512]) for c in range(J)]

            s_b_in = sem_in(ph, "s_b_in")
            s_b2_in = sem_in(ph, "s_b2_in")
            s_w_in = sem_in(ph, "s_w_in")
            s_w1hi = sem_in(ph, "s_w1hi")
            s_w1lo = sem_in(ph, "s_w1lo")
            s_w2hi = sem_in(ph, "s_w2hi")
            s_w2lo = sem_in(ph, "s_w2lo")
            s_xr_in0 = sem_in(ph, "s_xr_in0")
            s_xr_in1 = sem_in(ph, "s_xr_in1")
            s_xr_in2 = sem_in(ph, "s_xr_in2")
            s_xr_in3 = sem_in(ph, "s_xr_in3")
            s_stats = sem_in(ph, "s_stats")
            s_aggr = sem_in(ph, "s_aggr")
            s_std_ready = sem_in(ph, "s_std_ready")
            s_rstd_ready = sem_in(ph, "s_rstd_ready")
            s_nmr_ready = sem_in(ph, "s_nmr_ready")
            s_xn_ready = sem_in(ph, "s_xn_ready")
            s_t_done = sem_in(ph, "s_t_done")
            s_hit = sem_in(ph, "s_hit")
            s_lot = sem_in(ph, "s_lot")
            s_h_mm = sem_in(ph, "s_h_mm")
            s_hf_ready = sem_in(ph, "s_hf_ready")
            s_hhi_ready = sem_in(ph, "s_hhi_ready")
            s_hlo_ready = sem_in(ph, "s_hlo_ready")
            s_w2_mm = sem_in(ph, "s_w2_mm")
            s_yb_done = sem_in(ph, "s_yb_done")
            s_ys_done = sem_in(ph, "s_ys_done")
            s_limits_done = sem_in(ph, "s_limits_done")
            s_fin_done = sem_in(ph, "s_fin_done")
            s_yz_done = sem_in(ph, "s_yz_done")
            s_yp_done = sem_in(ph, "s_yp_done")
            s_o_ready = sem_in(ph, "s_o_ready")
            s_tok_ready = sem_in(ph, "s_tok_ready")
            s_sc0 = sem_in(ph, "s_sc0")
            s_sc1 = sem_in(ph, "s_sc1")
            s_eps_set = sem_in(ph, "s_eps_set")
            s_b1_t = sem_in(ph, "s_b1_t")
            s_b1_set = sem_in(ph, "s_b1_set")
            xr_in, sc = [s_xr_in0, s_xr_in1, s_xr_in2, s_xr_in3], [s_sc0, s_sc1]

            LAG = 3

            def over_experts(eng, body):
                body(0, False)
                with eng.Fori(1, E - 1) as e:
                    body(e, False)
                body(E - 1, True)

            def is_first(e, st):
                return isinstance(e, int) and e == 0 and st == 0

            @block.sync
            def _(sp):
                def load_w(e):
                    w1e = w1[bass.ds(e, 1), :, :].rearrange("a (c p) f -> p (a c) f", p=P)
                    w2e = w2[bass.ds(e, 1), :, :].rearrange("a (c p) d -> p (a c) d", p=P)
                    sp.dma_start(w1_raw, w1e).then_inc(s_w_in, 16)
                    sp.dma_start(w2_raw, w2e).then_inc(s_w_in, 16)

                def load_x(g, slot):
                    sp.dma_start(xr[:, slot, :, :],
                                 rows[bass.ds(g * TS3, TS3), :].rearrange("(p j) w -> p j w", j=J)).then_inc(xr_in[slot], 16)

                load_x(0, 0)
                sp.dma_start(b1_rows[:, :], b1.rearrange("e (c p) -> (e c) p", p=P)).then_inc(s_b_in, 16)
                load_w(0)
                sp.dma_start(b2_bc[:, :, :], b2.rearrange("(a e) d -> a (e d)", a=1).partition_broadcast(T3)
                             ).then_inc(s_b2_in, 16)
                for g in range(1, ST):
                    load_x(g, g)

                def body(e, last):
                    for st in range(ST):
                        g = ST * e + st
                        if st == 1 and not last:
                            for sem in (s_w1hi, s_w1lo, s_w2hi, s_w2lo):
                                sp.wait_ge(sem, NF * (e + 1))
                            load_w(e + 1)
                        if not is_first(e, st) and not (last and st > 0):
                            sp.wait_ge(s_o_ready, g)
                            sp.wait_ge(s_tok_ready, g)
                            load_x(g + ST - 1, (st - 1) % ST)

                over_experts(sp, body)
                sp.wait_ge(sc[0], 16 * J * (NG // 2))
                sp.wait_ge(sc[1], 16 * J * (NG // 2))

            @block.gpsimd
            def _(pool):
                def scatter(n, par):
                    pool.wait_ge(s_o_ready, n)
                    pool.wait_ge(s_tok_ready, n)
                    passed(pool, s_pool_passed)
                    for j in range(J):
                        pool.indirect_dma_start(out=out, in_=o_sb[:, par, j, :], in_offset=None,
                                                out_offset=bass.IndirectOffsetOnAxis(ap=tok_i[:, par, j:j + 1], axis=0),
                                                bounds_check=N - 1, oob_is_err=False).then_inc(sc[par], 16)

                def body(e, last):
                    for st in range(ST):
                        if not is_first(e, st):
                            scatter(ST * e + st, 1 - st % 2)

                over_experts(pool, body)
                scatter(NG, 1)

            @block.scalar
            def _(act):
                def split_w1(f, n):
                    act.wait_ge(s_w_in, 32 * n)
                    act.activation(w1_hi[:, :, f * P:(f + 1) * P], w1_raw[:, :, f * P:(f + 1) * P], ACT.Copy)\
                       .then_inc(s_w1hi, 1)

                def split_w2(f, n):
                    act.wait_ge(s_w_in, 32 * n)
                    act.activation(w2_hi[:, f, :], w2_raw[:, f, :], ACT.Copy).then_inc(s_w2hi, 1)

                def normal(g, slot):
                    act.wait_ge(s_aggr, J * (g + 1))
                    act.wait_ge(s_rstd_ready, g)
                    act.activation(std[:, :], mv[:, :, 1], ACT.Sqrt, bias=eps_c[0:T3, :]).then_inc(s_std_ready, 1)
                    act.wait_ge(s_nmr_ready, g + 1)
                    act.wait_ge(s_t_done, g)
                    for j in range(J):
                        ins = act.activation(xn3[:, j, :], xr[:, slot, j, 0:D], ACT.Identity, bias=nmr[:, j:j + 1],
                                             scale=rstd[:, j:j + 1])
                    ins.then_inc(s_xn_ready, 1)

                def high_t(g, par):
                    act.wait_ge(s_t_done, g + 1)
                    for c in range(KC):
                        act.activation(xt_hi[:, par, c, :], psX[c][:, 0:TS3], ACT.Copy).then_inc(s_hit, 1)

                act.wait_ge(s_eps_set, 1)
                normal(0, 0)
                high_t(0, 0)
                act.wait_ge(s_b1_t, 1)
                act.activation(b1_sb[:, :], psY[0][:, 0:E * NF], ACT.Copy).then_inc(s_b1_set, 1)
                act.wait_ge(s_b1_set, 1)
                for f in range(NF):
                    split_w1(f, 1)

                def times_prob(n, slot):
                    act.wait_ge(s_yp_done, n - 1)
                    act.wait_ge(s_limits_done, 2 * (n - 1))
                    act.wait_ge(s_fin_done, n - 1)
                    act.wait_ge(s_yb_done, J * n)
                    for j in range(J):
                        ins = act.activation(ys[:, j, :], yb[:, j, :], ACT.Copy, scale=xr[:, slot, j, D:D + 1])
                    ins.then_inc(s_ys_done, 1)

                def body(e, last):
                    for st in range(ST):
                        g, par = ST * e + st, st % 2
                        end = last and st == ST - 1
                        for f in range(NF):
                            act.wait_ge(s_h_mm, NF * g + f + 1)
                            act.wait_ge(s_hlo_ready, NF * g + f - 3 if f >= 4 else NF * g)
                            act.wait_ge(s_w2_mm, NF * g + f - 3 if f >= 4 else NF * g)
                            passed(act, s_act_passed)
                            act.activation(h_hi[:, f % 4, :], psH[f % 2][:, 0:TS3], ACT.Relu,
                                           bias=b1_sb[:, bass.ds(e * NF + f, 1)]).then_inc(s_hhi_ready, 1)
                            act.activation(hf[:, f % 4, :], psH[f % 2][:, 0:TS3], ACT.Relu,
                                           bias=b1_sb[:, bass.ds(e * NF + f, 1)]).then_inc(s_hf_ready, 1)
                            if is_first(e, st):
                                split_w2(f, 1)
                            if f == 0 and not is_first(e, st):
                                times_prob(g, (st - 1) % ST)
                            if f == 2 and not end:
                                normal(g + 1, (st + 1) % ST)
                            if f == 6 and not end:
                                high_t(g + 1, 1 - par)
                            if st == ST - 1 and not last:
                                split_w1(f, e + 2)
                                if f >= LAG:
                                    act.wait_ge(s_w2_mm, NF * g + f - LAG + 1)
                                    split_w2(f - LAG, e + 2)
                            if st == 0 and f < LAG and not is_first(e, 0):
                                act.wait_ge(s_w2_mm, NF * g - LAG + f + 1)
                                split_w2(NF - LAG + f, e + 1)

                over_experts(act, body)
                times_prob(NG, ST - 1)

            @block.vector
            def _(dve):
                nc.vector.memset(eps_c[:, :], EPS).then_inc(s_eps_set, 1)

                def split_w1(f, n):
                    dve.wait_ge(s_w1hi, NF * (n - 1) + f + 1)
                    nc.vector.tensor_tensor(w1_lo[:, :, f * P:(f + 1) * P], w1_raw[:, :, f * P:(f + 1) * P],
                                            w1_hi[:, :, f * P:(f + 1) * P].bitcast(F32), ALU.subtract).then_inc(s_w1lo, 1)

                def split_w2(f, n):
                    dve.wait_ge(s_w2hi, NF * (n - 1) + f + 1)
                    nc.vector.tensor_tensor(w2_lo[:, f, :], w2_raw[:, f, :], w2_hi[:, f, :].bitcast(F32),
                                            ALU.subtract).then_inc(s_w2lo, 1)

                def stats(g, slot, n):
                    dve.wait_ge(xr_in[slot], 16 * n)
                    for j in range(J):
                        nc.vector.bn_stats(st6[:, j, :], xr[:, slot, j, 0:D]).then_inc(s_stats, 1)
                    dve.wait_ge(s_xn_ready, g)
                    dve.wait_ge(s_stats, J * (g + 1))
                    passed(dve, s_dve_passed)
                    for j in range(J):
                        nc.vector.bn_aggr(mv[:, j, :], st6[:, j, :]).then_inc(s_aggr, 1)

                def scales(g):
                    dve.wait_ge(s_std_ready, g + 1)
                    nc.vector.reciprocal(rstd[:, :], std[:, :]).then_inc(s_rstd_ready, 1)
                    dve.wait_ge(s_rstd_ready, g + 1)
                    nc.vector.scalar_tensor_tensor(nmr[:, :], mv[:, :, 0], -1.0, rstd[:, :], ALU.mult, ALU.mult)\
                      .then_inc(s_nmr_ready, 1)

                def low_t(g, par):
                    for c in range(KC):
                        dve.wait_ge(s_hit, KC * g + c + 1)
                        nc.vector.tensor_tensor(xt_lo[:, par, c, :], psX[c][:, 0:TS3], xt_hi[:, par, c, :].bitcast(F32),
                                                ALU.subtract).then_inc(s_lot, 1)

                stats(0, 0, 1)
                scales(0)
                low_t(0, 0)
                for f in range(NF):
                    split_w1(f, 1)
                dve.wait_ge(s_b2_in, 16)
                dve.wait_ge(s_b1_set, 1)

                def limits(n):
                    dve.wait_ge(s_ys_done, n)
                    nc.vector.tensor_scalar(top[:, :, :], ys[:, :, :], 1e4, 1e4, ALU.is_ge, ALU.mult)\
                      .then_inc(s_limits_done, 1)
                    nc.vector.tensor_scalar(bottom[:, :, :], ys[:, :, :], -1e4, 1e4, ALU.is_le, ALU.mult)\
                      .then_inc(s_limits_done, 1)

                def finite(n):
                    nc.vector.tensor_scalar(fin[:, :, :], ys[:, :, :], 0.0, 0.0, ALU.mult, ALU.is_equal)\
                      .then_inc(s_fin_done, 1)
                    dve.wait_ge(s_limits_done, 2 * n)
                    dve.wait_ge(s_o_ready, n - 1)
                    nc.vector.tensor_tensor(yc[:, :, :], top[:, :, :], bottom[:, :, :], ALU.subtract).then_inc(s_yz_done, 1)

                def keep_finite(n):
                    dve.wait_ge(s_yz_done, n)
                    dve.wait_ge(s_fin_done, n)
                    passed(dve, s_dve_passed)
                    nc.vector.copy_predicated(yc[:, :, :], fin[:, :, :], ys[:, :, :]).then_inc(s_yp_done, 1)

                def sums(n, par, slot, used):
                    dve.wait_ge(sc[par], 16 * J * used)
                    nc.vector.tensor_copy(tok_i[:, par, :], xr[:, slot, :, D + 1]).then_inc(s_tok_ready, 1)
                    dve.wait_ge(s_yp_done, n)
                    nc.vector.tensor_tensor(o_sb[:, par, :, :], yc[:, :, :], xr[:, slot, :, 0:D], ALU.add)\
                      .then_inc(s_o_ready, 1)

                def body(e, last):
                    for st in range(ST):
                        g, par = ST * e + st, st % 2
                        end = last and st == ST - 1
                        after = not is_first(e, st)
                        for f in range(NF):
                            dve.wait_ge(s_hhi_ready, NF * g + f + 1)
                            dve.wait_ge(s_hf_ready, NF * g + f + 1)
                            dve.wait_ge(s_w2_mm, NF * g + f - 3 if f >= 4 else NF * g)
                            nc.vector.tensor_tensor(h_lo[:, f % 4, :], hf[:, f % 4, :], h_hi[:, f % 4, :].bitcast(F32),
                                                    ALU.subtract).then_inc(s_hlo_ready, 1)
                            if is_first(e, st):
                                split_w2(f, 1)
                            if f == 0 and not end:
                                stats(g + 1, (st + 1) % ST, e + 1 + (st + 1) // ST)
                            if f == 1 and not end:
                                scales(g + 1)
                            if f == 2 and after:
                                limits(g)
                            if f == 3 and after:
                                finite(g)
                            if f == 4 and after:
                                keep_finite(g)
                            if f == 5 and after:
                                sums(g, 1 - par, (st - 1) % ST, e * (ST // 2) + (st - 1) // 2)
                            if f == 6 and not end:
                                low_t(g + 1, 1 - par)
                            if st == ST - 1 and not last:
                                split_w1(f, e + 2)
                                if f >= LAG:
                                    split_w2(f - LAG, e + 2)
                            if st == 0 and f < LAG and not is_first(e, 0):
                                split_w2(NF - LAG + f, e + 1)
                        dve.wait_ge(s_ys_done, g)
                        dve.wait_ge(s_w2_mm, NF * (g + 1))
                        for j in range(J):
                            nc.vector.tensor_tensor(yb[:, j, :], psY[j][0:T3, 0:D],
                                                    b2_bc[:, bass.ds(e, 1), :].rearrange("p a d -> p (a d)"),
                                                    ALU.add).then_inc(s_yb_done, 1)

                over_experts(dve, body)
                limits(NG)
                finite(NG)
                keep_finite(NG)
                sums(NG, 1, ST - 1, NG // 2 - 1)

            @block.tensor
            def _(pe):
                def transposes(g):
                    pe.wait_ge(s_xn_ready, g + 1)
                    pe.wait_ge(s_hit, KC * g)
                    pe.wait_ge(s_lot, KC * g)
                    for c in range(KC):
                        for j in range(J):
                            ins = nc.tensor.transpose(psX[c][:, j * T3:(j + 1) * T3], xn3[:, j, c * P:(c + 1) * P],
                                                      ident[0:T3, 0:T3])
                    ins.then_inc(s_t_done, 1)

                pe.wait_ge(s_b_in, 16)
                nc.tensor.transpose(psY[0][:, 0:E * NF], b1_rows[:, :], ident[0:E * NF, 0:E * NF]).then_inc(s_b1_t, 1)
                transposes(0)
                pe.wait_ge(s_b1_set, 1)

                def body(e, last):
                    for st in range(ST):
                        g, par = ST * e + st, st % 2
                        for slot in range(NF + 2):
                            if slot < NF:
                                f = slot
                                if f == 0:
                                    pe.wait_ge(s_hit, KC * (g + 1))
                                    pe.wait_ge(s_lot, KC * (g + 1))
                                if st == 0:
                                    pe.wait_ge(s_w1hi, NF * e + f + 1)
                                    pe.wait_ge(s_w1lo, NF * e + f + 1)
                                pe.wait_ge(s_hf_ready, NF * g + f - 1 if f >= 2 else NF * g)
                                pe.wait_ge(s_hhi_ready, NF * g + f - 1 if f >= 2 else NF * g)
                                n = 0
                                for w, xt in ((w1_hi, xt_hi), (w1_lo, xt_hi), (w1_hi, xt_lo)):
                                    for kc in range(KC):
                                        ins = nc.tensor.matmul(psH[f % 2][:, 0:TS3], w[:, kc, f * P:(f + 1) * P],
                                                               xt[:, par, kc, :], start=n == 0, stop=n == 3 * KC - 1)
                                        n += 1
                                ins.then_inc(s_h_mm, 1)
                            if slot == 5 and not (last and st == ST - 1):
                                transposes(g + 1)
                            if slot >= 2:
                                f = slot - 2
                                if f == 0:
                                    pe.wait_ge(s_yb_done, J * g)
                                if st == 0:
                                    pe.wait_ge(s_w2hi, NF * e + f + 1)
                                    pe.wait_ge(s_w2lo, NF * e + f + 1)
                                pe.wait_ge(s_hhi_ready, NF * g + f + 1)
                                pe.wait_ge(s_hlo_ready, NF * g + f + 1)
                                for j in range(J):
                                    for n, (hh, w) in enumerate(((h_hi, w2_hi), (h_hi, w2_lo), (h_lo, w2_hi))):
                                        ins = nc.tensor.matmul(psY[j][0:T3, 0:D], hh[:, f % 4, j * T3:(j + 1) * T3],
                                                               w[:, f, :], start=f == 0 and n == 0,
                                                               stop=f == NF - 1 and n == 2)
                                ins.then_inc(s_w2_mm, 1)

                over_experts(pe, body)

_INS = ["x", "src", "dst", "L0_gnn_weight", "L0_gnn_attn_l", "L0_gnn_attn_r", "L0_mix_Wq", "L0_mix_Wkv",
        "L0_mix_Wproj", "L0_mix_bproj", "L0_ffn_gate_w", "L0_ffn_gate_b", "L0_ffn_w1", "L0_ffn_b1",
        "L0_ffn_w2", "L0_ffn_b2"]


def kernel(**inputs):
    import numpy as _np
    import concourse.bacc as _bacc
    from concourse import mybir as _mybir
    from concourse.bass_utils import run_bass_kernel_spmd as _run

    nc = _bacc.Bacc("TRN2", target_bir_lowering=False, num_devices=1)
    arrays, args = {}, []
    for name in _INS:
        a = _np.ascontiguousarray(inputs[name])
        arrays[f"in_{name}"] = a
        args.append(nc.dram_tensor(f"in_{name}", a.shape, _mybir.dt.from_np(a.dtype), kind="ExternalInput").ap())
    out = nc.dram_tensor("out_0", arrays["in_x"].shape, _mybir.dt.float32, kind="ExternalOutput").ap()
    gps_layer(nc, *args, out)
    r = _run(nc, [arrays], core_ids=[0])
    return r.results[0]["out_0"]
```
